# Optimizing a Trainium2 kernel written in Bass

```python
import numpy as np
import jax
import jax.numpy as jnp

def _softmax(x, axis=-1):
    return jax.nn.softmax(x, axis=axis)

def _gelu(x):
    return jax.nn.gelu(x, approximate=True)

def _silu(x):
    return jax.nn.silu(x)

def _sigmoid(x):
    return jax.nn.sigmoid(x)

def _layernorm(x, axis=-1, eps=1e-05):
    m = jnp.mean(x, axis=axis, keepdims=True)
    v = jnp.var(x, axis=axis, keepdims=True)
    return (x - m) / jnp.sqrt(v + eps)

def _scatter_add(tgt, idx, src, axis=0):
    return tgt.at[idx].add(src)

def _segment_sum(src, seg, n):
    return jax.ops.segment_sum(src, seg, n)
kernel_name = 'mk_xattn_ffn_d4_seqx_r8_069edf'

def setup_inputs(seed: int=0):
    np.random.seed(seed)
    _w = jnp.asarray

    def _rec_inputs():
        import jax
        import jax.numpy as jnp
        _rk = jax.random.key(seed)
        x = -0.0003929 + 0.9999 * jax.random.normal(jax.random.fold_in(_rk, 1), (16, 256, 128), jnp.float32)
        _lenS = 256 - jax.random.randint(jax.random.fold_in(_rk, 7), (16,), 0, max(1, 256 // 4) + 1, jnp.int32)
        _lenS2 = 64 - jax.random.randint(jax.random.fold_in(_rk, 8), (16,), 0, max(1, 64 // 4) + 1, jnp.int32)
        _ctx_512P = jax.random.normal(jax.random.fold_in(_rk, 11), (16, 16, 64), jnp.float32)
        _ctx_512c = jax.random.dirichlet(jax.random.fold_in(_rk, 511), 0.3 * jnp.ones((16,), jnp.float32), (16, 64))
        _ctx_512t = jnp.einsum('bsk,bkd->bsd', _ctx_512c, _ctx_512P)
        _ctx_512t = _ctx_512t * jax.lax.rsqrt(jnp.mean(jnp.square(_ctx_512t)) + 1e-12) * 0.953939
        ctx_512 = -1.39393e-06 + 0.999914 * (_ctx_512t + 0.3 * jax.random.normal(jax.random.fold_in(_rk, 611), (16, 64, 64), jnp.float32))
        return (x, ctx_512)
    x, ctx_512 = _rec_inputs()

    def _L0_xattn_setup():
        import jax, jax.numpy as jnp
        import numpy as np
        HEADS = 16
        D_MODEL = 128
        IMG_MODEL = 64
        D_K = D_MODEL // HEADS
        key = jax.random.key(seed)
        ks = jax.random.split(key, 12)
        B, LQ, LKV = (8, 256, 128)
        s_dm = 1.0 / np.sqrt(D_MODEL)
        s_im = 1.0 / np.sqrt(IMG_MODEL)
        return {'q': jax.random.normal(ks[0], (B, LQ, D_MODEL), jnp.float32), 'k': jax.random.normal(ks[1], (B, LKV, IMG_MODEL), jnp.float32), 'v': jax.random.normal(ks[2], (B, LKV, IMG_MODEL), jnp.float32), 'Wq': jax.random.normal(ks[3], (D_MODEL, D_MODEL), jnp.float32) * s_dm, 'bq': jnp.zeros((D_MODEL,), jnp.float32), 'Wk': jax.random.normal(ks[4], (IMG_MODEL, D_MODEL), jnp.float32) * s_im, 'bk': jnp.zeros((D_MODEL,), jnp.float32), 'Wv': jax.random.normal(ks[5], (IMG_MODEL, D_MODEL), jnp.float32) * s_im, 'bv': jnp.zeros((D_MODEL,), jnp.float32), 'Wo': jax.random.normal(ks[6], (D_MODEL, D_MODEL), jnp.float32) * s_dm, 'bo': jnp.zeros((D_MODEL,), jnp.float32)}
    _L0_xattn_all = _L0_xattn_setup()
    _L0_xattn_in = {k: v for k, v in _L0_xattn_all.items() if k in ('Wq', 'bq', 'Wk', 'bk', 'Wv', 'bv', 'Wo', 'bo')}
    del _L0_xattn_all

    def _L0_ffn_setup():
        import jax, jax.numpy as jnp
        import numpy as np
        B, S, H = (2, 128, 128)
        DFF = 256
        E = 8
        TOPK = 2

        def _expert_ffn(x, w1, b1, w2, b2, wg, bg, w3, b3):
            x1 = jnp.einsum('bsh,hf->bsf', x, w1) + b1
            x2 = jnp.einsum('bsh,hf->bsf', x, w2) + b2
            z = x1 * x2
            s = jax.nn.silu(jnp.einsum('bsf,fg->bsg', z, wg) + bg)
            return jnp.einsum('bsg,gh->bsh', s, w3) + b3
        key = jax.random.key(seed)
        ks = jax.random.split(key, 12)
        sc = 0.02
        return {'x': jax.random.normal(ks[0], (B, S, H), jnp.float32), 'gate_w': jax.random.normal(ks[1], (H, E), jnp.float32) * sc, 'gate_b': jnp.zeros((E,), jnp.float32), 'w1': jax.random.normal(ks[2], (E, H, DFF), jnp.float32) * sc, 'b1': jnp.zeros((E, DFF), jnp.float32), 'w2': jax.random.normal(ks[3], (E, H, DFF), jnp.float32) * sc, 'b2': jnp.zeros((E, DFF), jnp.float32), 'wg': jax.random.normal(ks[4], (E, DFF, DFF), jnp.float32) * sc, 'bg': jnp.zeros((E, DFF), jnp.float32), 'w3': jax.random.normal(ks[5], (E, DFF, H), jnp.float32) * sc, 'b3': jnp.zeros((E, H), jnp.float32)}
    _L0_ffn_all = _L0_ffn_setup()
    _L0_ffn_in = {k: v for k, v in _L0_ffn_all.items() if k in ('gate_w', 'gate_b', 'w1', 'b1', 'w2', 'b2', 'wg', 'bg', 'w3', 'b3')}
    del _L0_ffn_all

    def _L1_xattn_setup():
        import jax, jax.numpy as jnp
        import numpy as np
        B, T, TC, C, CC, H = (2, 256, 64, 128, 64, 16)
        D = C // H

        def _heads(t):
            b, l, _ = t.shape
            return t.reshape(b, l, H, D).transpose(0, 2, 1, 3)
        key = jax.random.key(seed)
        ks = jax.random.split(key, 18)
        w = lambda k, i, o: jax.random.normal(k, (i, o), jnp.float32) / np.sqrt(i).astype(np.float32)
        return {'x': jax.random.normal(ks[0], (B, T, C), jnp.float32), 'cross_input': jax.random.normal(ks[1], (B, TC, CC), jnp.float32), 'Wk': w(ks[2], C, C), 'bk': jnp.zeros((C,), jnp.float32), 'Wq': w(ks[3], C, C), 'bq': jnp.zeros((C,), jnp.float32), 'Wv': w(ks[4], C, C), 'bv': jnp.zeros((C,), jnp.float32), 'Wck': w(ks[5], CC, C), 'bck': jnp.zeros((C,), jnp.float32), 'Wcq': w(ks[6], C, C), 'bcq': jnp.zeros((C,), jnp.float32), 'Wcv': w(ks[7], CC, C), 'bcv': jnp.zeros((C,), jnp.float32), 'Wp': w(ks[8], C, C), 'bp': jnp.zeros((C,), jnp.float32)}
    _L1_xattn_all = _L1_xattn_setup()
    _L1_xattn_in = {k: v for k, v in _L1_xattn_all.items() if k in ('Wk', 'bk', 'Wq', 'bq', 'Wv', 'bv', 'Wck', 'bck', 'Wcq', 'bcq', 'Wcv', 'bcv', 'Wp', 'bp')}
    del _L1_xattn_all

    def _L1_ffn_setup():
        import jax, jax.numpy as jnp
        import numpy as np
        E, K, D = (8, 2, 128)
        B, S = (2, 512)

        def _layernorm(x, g, b, eps=1e-06):
            m = jnp.mean(x, axis=-1, keepdims=True)
            v = jnp.var(x, axis=-1, keepdims=True)
            return (x - m) * jax.lax.rsqrt(v + eps) * g + b
        key = jax.random.key(seed)
        ks = jax.random.split(key, 6)
        n = lambda k, shape, scale: jax.random.normal(k, shape, jnp.float32) * scale
        return {'x': n(ks[0], (B, S, D), 1.0), 'gate_w': n(ks[1], (D, E), 0.02), 'w1': n(ks[2], (E, D, 2 * D), 0.02), 'b1': jnp.zeros((E, 2 * D), jnp.float32), 'w2': n(ks[3], (E, 2 * D, D), 0.02), 'b2': jnp.zeros((E, D), jnp.float32), 'ln_g': jnp.ones((E, D), jnp.float32), 'ln_b': jnp.zeros((E, D), jnp.float32)}
    _L1_ffn_all = _L1_ffn_setup()
    _L1_ffn_in = {k: v for k, v in _L1_ffn_all.items() if k in ('gate_w', 'w1', 'b1', 'w2', 'b2', 'ln_g', 'ln_b')}
    del _L1_ffn_all

    def _L2_xattn_setup():
        import jax, jax.numpy as jnp
        import numpy as np
        H, D, C1, C2, S, M, B, W = (16, 32, 128, 64, 256, 64, 2, 4)

        def _ln(x, g, b):
            m = jnp.mean(x, -1, keepdims=True)
            v = jnp.var(x, -1, keepdims=True)
            return (x - m) * jax.lax.rsqrt(v + 1e-05) * g + b

        def _mha(x, y, wq, wk, wv, li1_w, li1_b, lnx_g, lnx_b, lny_g, lny_b, ln3_g, ln3_b, li2_w, li2_b, li3_w, li3_b, causal):
            xn = _ln(x, lnx_g, lnx_b)
            yn = _ln(y, lny_g, lny_b)
            q = jnp.einsum('bsc,hcd->bhsd', xn, wq)
            k = jnp.einsum('btc,hcd->bhtd', yn, wk)
            v = jnp.einsum('btc,hcd->bhtd', yn, wv)
            a = jax.nn.softmax(jnp.einsum('bhsd,bhtd->bhst', q, k) * D ** (-0.5), axis=-1)
            if causal:
                s, t = (a.shape[-2], a.shape[-1])
                mask = (jnp.arange(t)[None, :] > jnp.arange(s)[:, None]).astype(a.dtype)
                a = a * mask
            o = jnp.einsum('bhst,bhtd->bhsd', a, v)
            o = o.transpose(0, 2, 1, 3).reshape(x.shape[0], x.shape[1], H * D)
            x_out = x + o @ li1_w + li1_b
            h = jax.nn.gelu(_ln(x_out, ln3_g, ln3_b) @ li2_w + li2_b, approximate=False)
            return x_out + h @ li3_w + li3_b
        key = jax.random.key(seed)
        ks = iter(jax.random.split(key, 64))

        def w(shape, scale=0.02):
            return jax.random.normal(next(ks), shape, jnp.float32) * scale
        inp = {'xx': jax.random.normal(next(ks), (B, S, C1), jnp.float32), 'ee': jax.random.normal(next(ks), (B, M, C2), jnp.float32), 'ln1_g': jnp.ones(C1, jnp.float32), 'ln1_b': jnp.zeros(C1, jnp.float32), 'ln2_g': jnp.ones(C1, jnp.float32), 'ln2_b': jnp.zeros(C1, jnp.float32)}
        for pfx, cy in (('a1', C1), ('a2', C2)):
            inp[pfx + '_wq'] = w((H, C1, D))
            inp[pfx + '_wk'] = w((H, cy, D))
            inp[pfx + '_wv'] = w((H, cy, D))
            inp[pfx + '_li1_w'] = w((H * D, C1))
            inp[pfx + '_li1_b'] = jnp.zeros(C1, jnp.float32)
            inp[pfx + '_lnx_g'] = jnp.ones(C1, jnp.float32)
            inp[pfx + '_lnx_b'] = jnp.zeros(C1, jnp.float32)
            inp[pfx + '_lny_g'] = jnp.ones(cy, jnp.float32)
            inp[pfx + '_lny_b'] = jnp.zeros(cy, jnp.float32)
            inp[pfx + '_ln3_g'] = jnp.ones(C1, jnp.float32)
            inp[pfx + '_ln3_b'] = jnp.zeros(C1, jnp.float32)
            inp[pfx + '_li2_w'] = w((C1, C1 * W))
            inp[pfx + '_li2_b'] = jnp.zeros(C1 * W, jnp.float32)
            inp[pfx + '_li3_w'] = w((C1 * W, C1))
            inp[pfx + '_li3_b'] = jnp.zeros(C1, jnp.float32)
        inp['training'] = 0
        return inp
    _L2_xattn_all = _L2_xattn_setup()
    _L2_xattn_in = {k: v for k, v in _L2_xattn_all.items() if k in ('ln1_g', 'ln1_b', 'ln2_g', 'ln2_b', 'a1_wq', 'a1_wk', 'a1_wv', 'a1_li1_w', 'a1_li1_b', 'a1_lnx_g', 'a1_lnx_b', 'a1_lny_g', 'a1_lny_b', 'a1_ln3_g', 'a1_ln3_b', 'a1_li2_w', 'a1_li2_b', 'a1_li3_w', 'a1_li3_b', 'a2_wq', 'a2_wk', 'a2_wv', 'a2_li1_w', 'a2_li1_b', 'a2_lnx_g', 'a2_lnx_b', 'a2_lny_g', 'a2_lny_b', 'a2_ln3_g', 'a2_ln3_b', 'a2_li2_w', 'a2_li2_b', 'a2_li3_w', 'a2_li3_b')}
    del _L2_xattn_all

    def _L2_ffn_setup():
        import jax, jax.numpy as jnp
        import numpy as np
        from jax import lax
        D = 128
        H = 512
        E = 8
        TOPK = 2
        key = jax.random.key(seed)
        ks = jax.random.split(key, 7)
        s = 0.02
        return {'x': jax.random.normal(ks[0], (2, 256, D), dtype=jnp.float32), 'W1': jax.random.normal(ks[1], (E, D, H), dtype=jnp.float32) * s, 'b1': jnp.zeros((E, H), dtype=jnp.float32), 'W2': jax.random.normal(ks[2], (E, H, D), dtype=jnp.float32) * s, 'b2': jnp.zeros((E, D), dtype=jnp.float32), 'Wr': jax.random.normal(ks[3], (D, E), dtype=jnp.float32) * s, 'br': jnp.zeros((E,), dtype=jnp.float32)}
    _L2_ffn_all = _L2_ffn_setup()
    _L2_ffn_in = {k: v for k, v in _L2_ffn_all.items() if k in ('W1', 'b1', 'W2', 'b2', 'Wr', 'br')}
    del _L2_ffn_all

    def _L3_xattn_setup():
        import jax, jax.numpy as jnp
        import numpy as np
        DIM = 128
        LATENT_DIM = 64
        NUM_HEADS = 16
        HEAD_DIM = DIM // NUM_HEADS
        SCALE = HEAD_DIM ** (-0.5)
        key = jax.random.key(seed)
        k1, k2, k3, k4, k5 = jax.random.split(key, 5)
        B, xN, zN = (2, 256, 256)
        x = jax.random.normal(k1, (B, xN, DIM), dtype=jnp.float32)
        z = jax.random.normal(k2, (B, zN, LATENT_DIM), dtype=jnp.float32)
        Wq = jax.random.normal(k3, (DIM, DIM), dtype=jnp.float32) * DIM ** (-0.5)
        Wkv = jax.random.normal(k4, (2 * DIM, LATENT_DIM), dtype=jnp.float32) * LATENT_DIM ** (-0.5)
        Wo = jax.random.normal(k5, (DIM, DIM), dtype=jnp.float32) * DIM ** (-0.5)
        return {'x': x, 'z': z, 'Wq': Wq, 'Wkv': Wkv, 'Wo': Wo}
    _L3_xattn_all = _L3_xattn_setup()
    _L3_xattn_in = {k: v for k, v in _L3_xattn_all.items() if k in ('Wq', 'Wkv', 'Wo')}
    del _L3_xattn_all

    def _L3_ffn_setup():
        import jax, jax.numpy as jnp
        import numpy as np
        QB = 127.0
        EPS = 1e-05

        def _ste(x, q):
            return x + jax.lax.stop_gradient(q - x)

        def bitlinear(x, W, b):
            w_scale = jnp.clip(jnp.mean(jnp.abs(W)), EPS, None)
            Wq = _ste(W, jnp.clip(jnp.round(W / w_scale), -1.0, 1.0) * w_scale)
            x_scale = jnp.clip(jnp.max(jnp.abs(x), axis=-1, keepdims=True), EPS, None)
            xq = _ste(x, jnp.clip(jnp.round(x * (QB / x_scale)), -QB - 1.0, QB) * (x_scale / QB))
            return jnp.einsum('bnd,hd->bnh', xq, Wq) + b
        key = jax.random.key(seed)
        k0, k1, k2 = jax.random.split(key, 3)
        B, N, D = (8, 512, 128)
        H = int(D * 4.0)
        x = jax.random.normal(k0, (B, N, D), dtype=jnp.float32)
        W1 = jax.random.normal(k1, (H, D), dtype=jnp.float32) * 0.02
        b1 = jnp.zeros((H,), dtype=jnp.float32)
        W2 = jax.random.normal(k2, (D, H), dtype=jnp.float32) * 0.02
        b2 = jnp.zeros((D,), dtype=jnp.float32)
        return {'x': x, 'W1': W1, 'b1': b1, 'W2': W2, 'b2': b2}
    _L3_ffn_all = _L3_ffn_setup()
    _L3_ffn_in = {k: v for k, v in _L3_ffn_all.items() if k in ('W1', 'b1', 'W2', 'b2')}
    del _L3_ffn_all
    return {'x': x, 'ctx_512': ctx_512, 'L0_xattn_Wq': _L0_xattn_in['Wq'], 'L0_xattn_bq': _L0_xattn_in['bq'], 'L0_xattn_Wk': _L0_xattn_in['Wk'], 'L0_xattn_bk': _L0_xattn_in['bk'], 'L0_xattn_Wv': _L0_xattn_in['Wv'], 'L0_xattn_bv': _L0_xattn_in['bv'], 'L0_xattn_Wo': _L0_xattn_in['Wo'], 'L0_xattn_bo': _L0_xattn_in['bo'], 'L0_ffn_gate_w': _L0_ffn_in['gate_w'], 'L0_ffn_gate_b': _L0_ffn_in['gate_b'], 'L0_ffn_w1': _L0_ffn_in['w1'], 'L0_ffn_b1': _L0_ffn_in['b1'], 'L0_ffn_w2': _L0_ffn_in['w2'], 'L0_ffn_b2': _L0_ffn_in['b2'], 'L0_ffn_wg': _L0_ffn_in['wg'], 'L0_ffn_bg': _L0_ffn_in['bg'], 'L0_ffn_w3': _L0_ffn_in['w3'], 'L0_ffn_b3': _L0_ffn_in['b3'], 'L1_xattn_Wk': _L1_xattn_in['Wk'], 'L1_xattn_bk': _L1_xattn_in['bk'], 'L1_xattn_Wq': _L1_xattn_in['Wq'], 'L1_xattn_bq': _L1_xattn_in['bq'], 'L1_xattn_Wv': _L1_xattn_in['Wv'], 'L1_xattn_bv': _L1_xattn_in['bv'], 'L1_xattn_Wck': _L1_xattn_in['Wck'], 'L1_xattn_bck': _L1_xattn_in['bck'], 'L1_xattn_Wcq': _L1_xattn_in['Wcq'], 'L1_xattn_bcq': _L1_xattn_in['bcq'], 'L1_xattn_Wcv': _L1_xattn_in['Wcv'], 'L1_xattn_bcv': _L1_xattn_in['bcv'], 'L1_xattn_Wp': _L1_xattn_in['Wp'], 'L1_xattn_bp': _L1_xattn_in['bp'], 'L1_ffn_gate_w': _L1_ffn_in['gate_w'], 'L1_ffn_w1': _L1_ffn_in['w1'], 'L1_ffn_b1': _L1_ffn_in['b1'], 'L1_ffn_w2': _L1_ffn_in['w2'], 'L1_ffn_b2': _L1_ffn_in['b2'], 'L1_ffn_ln_g': _L1_ffn_in['ln_g'], 'L1_ffn_ln_b': _L1_ffn_in['ln_b'], 'L2_xattn_ln1_g': _L2_xattn_in['ln1_g'], 'L2_xattn_ln1_b': _L2_xattn_in['ln1_b'], 'L2_xattn_ln2_g': _L2_xattn_in['ln2_g'], 'L2_xattn_ln2_b': _L2_xattn_in['ln2_b'], 'L2_xattn_a1_wq': _L2_xattn_in['a1_wq'], 'L2_xattn_a1_wk': _L2_xattn_in['a1_wk'], 'L2_xattn_a1_wv': _L2_xattn_in['a1_wv'], 'L2_xattn_a1_li1_w': _L2_xattn_in['a1_li1_w'], 'L2_xattn_a1_li1_b': _L2_xattn_in['a1_li1_b'], 'L2_xattn_a1_lnx_g': _L2_xattn_in['a1_lnx_g'], 'L2_xattn_a1_lnx_b': _L2_xattn_in['a1_lnx_b'], 'L2_xattn_a1_lny_g': _L2_xattn_in['a1_lny_g'], 'L2_xattn_a1_lny_b': _L2_xattn_in['a1_lny_b'], 'L2_xattn_a1_ln3_g': _L2_xattn_in['a1_ln3_g'], 'L2_xattn_a1_ln3_b': _L2_xattn_in['a1_ln3_b'], 'L2_xattn_a1_li2_w': _L2_xattn_in['a1_li2_w'], 'L2_xattn_a1_li2_b': _L2_xattn_in['a1_li2_b'], 'L2_xattn_a1_li3_w': _L2_xattn_in['a1_li3_w'], 'L2_xattn_a1_li3_b': _L2_xattn_in['a1_li3_b'], 'L2_xattn_a2_wq': _L2_xattn_in['a2_wq'], 'L2_xattn_a2_wk': _L2_xattn_in['a2_wk'], 'L2_xattn_a2_wv': _L2_xattn_in['a2_wv'], 'L2_xattn_a2_li1_w': _L2_xattn_in['a2_li1_w'], 'L2_xattn_a2_li1_b': _L2_xattn_in['a2_li1_b'], 'L2_xattn_a2_lnx_g': _L2_xattn_in['a2_lnx_g'], 'L2_xattn_a2_lnx_b': _L2_xattn_in['a2_lnx_b'], 'L2_xattn_a2_lny_g': _L2_xattn_in['a2_lny_g'], 'L2_xattn_a2_lny_b': _L2_xattn_in['a2_lny_b'], 'L2_xattn_a2_ln3_g': _L2_xattn_in['a2_ln3_g'], 'L2_xattn_a2_ln3_b': _L2_xattn_in['a2_ln3_b'], 'L2_xattn_a2_li2_w': _L2_xattn_in['a2_li2_w'], 'L2_xattn_a2_li2_b': _L2_xattn_in['a2_li2_b'], 'L2_xattn_a2_li3_w': _L2_xattn_in['a2_li3_w'], 'L2_xattn_a2_li3_b': _L2_xattn_in['a2_li3_b'], 'L2_ffn_W1': _L2_ffn_in['W1'], 'L2_ffn_b1': _L2_ffn_in['b1'], 'L2_ffn_W2': _L2_ffn_in['W2'], 'L2_ffn_b2': _L2_ffn_in['b2'], 'L2_ffn_Wr': _L2_ffn_in['Wr'], 'L2_ffn_br': _L2_ffn_in['br'], 'L3_xattn_Wq': _L3_xattn_in['Wq'], 'L3_xattn_Wkv': _L3_xattn_in['Wkv'], 'L3_xattn_Wo': _L3_xattn_in['Wo'], 'L3_ffn_W1': _L3_ffn_in['W1'], 'L3_ffn_b1': _L3_ffn_in['b1'], 'L3_ffn_W2': _L3_ffn_in['W2'], 'L3_ffn_b2': _L3_ffn_in['b2']}

def reference(x, ctx_512, L0_xattn_Wq, L0_xattn_bq, L0_xattn_Wk, L0_xattn_bk, L0_xattn_Wv, L0_xattn_bv, L0_xattn_Wo, L0_xattn_bo, L0_ffn_gate_w, L0_ffn_gate_b, L0_ffn_w1, L0_ffn_b1, L0_ffn_w2, L0_ffn_b2, L0_ffn_wg, L0_ffn_bg, L0_ffn_w3, L0_ffn_b3, L1_xattn_Wk, L1_xattn_bk, L1_xattn_Wq, L1_xattn_bq, L1_xattn_Wv, L1_xattn_bv, L1_xattn_Wck, L1_xattn_bck, L1_xattn_Wcq, L1_xattn_bcq, L1_xattn_Wcv, L1_xattn_bcv, L1_xattn_Wp, L1_xattn_bp, L1_ffn_gate_w, L1_ffn_w1, L1_ffn_b1, L1_ffn_w2, L1_ffn_b2, L1_ffn_ln_g, L1_ffn_ln_b, L2_xattn_ln1_g, L2_xattn_ln1_b, L2_xattn_ln2_g, L2_xattn_ln2_b, L2_xattn_a1_wq, L2_xattn_a1_wk, L2_xattn_a1_wv, L2_xattn_a1_li1_w, L2_xattn_a1_li1_b, L2_xattn_a1_lnx_g, L2_xattn_a1_lnx_b, L2_xattn_a1_lny_g, L2_xattn_a1_lny_b, L2_xattn_a1_ln3_g, L2_xattn_a1_ln3_b, L2_xattn_a1_li2_w, L2_xattn_a1_li2_b, L2_xattn_a1_li3_w, L2_xattn_a1_li3_b, L2_xattn_a2_wq, L2_xattn_a2_wk, L2_xattn_a2_wv, L2_xattn_a2_li1_w, L2_xattn_a2_li1_b, L2_xattn_a2_lnx_g, L2_xattn_a2_lnx_b, L2_xattn_a2_lny_g, L2_xattn_a2_lny_b, L2_xattn_a2_ln3_g, L2_xattn_a2_ln3_b, L2_xattn_a2_li2_w, L2_xattn_a2_li2_b, L2_xattn_a2_li3_w, L2_xattn_a2_li3_b, L2_ffn_W1, L2_ffn_b1, L2_ffn_W2, L2_ffn_b2, L2_ffn_Wr, L2_ffn_br, L3_xattn_Wq, L3_xattn_Wkv, L3_xattn_Wo, L3_ffn_W1, L3_ffn_b1, L3_ffn_W2, L3_ffn_b2):
    import jax
    import jax.numpy as jnp

    def _L0_xattn_ref(q, k, v, Wq, bq, Wk, bk, Wv, bv, Wo, bo):
        import jax, jax.numpy as jnp
        import numpy as np
        HEADS = 16
        D_MODEL = 128
        IMG_MODEL = 64
        D_K = D_MODEL // HEADS
        B, LQ, _ = q.shape
        LKV = k.shape[1]
        qh = (q @ Wq + bq).reshape(B, LQ, HEADS, D_K).transpose(0, 2, 1, 3)
        kh = (k @ Wk + bk).reshape(B, LKV, HEADS, D_K).transpose(0, 2, 1, 3)
        vh = (v @ Wv + bv).reshape(B, LKV, HEADS, D_K).transpose(0, 2, 1, 3)
        scale = 1.0 / np.sqrt(D_K)
        scores = jnp.einsum('bhqd,bhkd->bhqk', qh, kh) * scale
        attn = jax.nn.softmax(scores, axis=-1)
        out = jnp.einsum('bhqk,bhkd->bhqd', attn, vh)
        concat = out.transpose(0, 2, 1, 3).reshape(B, LQ, D_MODEL)
        return concat @ Wo + bo

    def _L0_ffn_ref(x, gate_w, gate_b, w1, b1, w2, b2, wg, bg, w3, b3):
        import jax, jax.numpy as jnp
        import numpy as np
        B, S, H = (2, 128, 128)
        DFF = 256
        E = 8
        TOPK = 2

        def _expert_ffn(x, w1, b1, w2, b2, wg, bg, w3, b3):
            x1 = jnp.einsum('bsh,hf->bsf', x, w1) + b1
            x2 = jnp.einsum('bsh,hf->bsf', x, w2) + b2
            z = x1 * x2
            s = jax.nn.silu(jnp.einsum('bsf,fg->bsg', z, wg) + bg)
            return jnp.einsum('bsg,gh->bsh', s, w3) + b3
        logits = jnp.einsum('bsh,he->bse', x, gate_w) + gate_b
        topv, topi = jax.lax.top_k(logits, TOPK)
        probs = jax.nn.softmax(topv, axis=-1)
        out = jnp.zeros_like(x)
        for e in range(E):
            we = jnp.sum(probs * (topi == e), axis=-1)
            y = _expert_ffn(x, w1[e], b1[e], w2[e], b2[e], wg[e], bg[e], w3[e], b3[e])
            out = out + we[..., None] * y
        return out

    def _L1_xattn_ref(x, cross_input, Wk, bk, Wq, bq, Wv, bv, Wck, bck, Wcq, bcq, Wcv, bcv, Wp, bp):
        import jax, jax.numpy as jnp
        import numpy as np
        B, T, TC, C, CC, H = (2, 256, 64, 128, 64, 16)
        D = C // H

        def _heads(t):
            b, l, _ = t.shape
            return t.reshape(b, l, H, D).transpose(0, 2, 1, 3)
        scale = np.float32(1.0 / np.sqrt(D))
        q = _heads(x @ Wq + bq)
        k = _heads(x @ Wk + bk)
        v = _heads(x @ Wv + bv)
        att = jnp.einsum('bhqd,bhkd->bhqk', q, k) * scale
        causal = jnp.tril(jnp.ones((T, T), bool))
        att = jnp.where(causal[None, None], att, -jnp.inf)
        y = jnp.einsum('bhqk,bhkd->bhqd', jax.nn.softmax(att, axis=-1), v)
        qc = _heads(x @ Wcq + bcq)
        kc = _heads(cross_input @ Wck + bck)
        vc = _heads(cross_input @ Wcv + bcv)
        attc = jnp.einsum('bhqd,bhkd->bhqk', qc, kc) * scale
        y = y + jnp.einsum('bhqk,bhkd->bhqd', jax.nn.softmax(attc, axis=-1), vc)
        y = y.transpose(0, 2, 1, 3).reshape(x.shape[0], T, C)
        return y @ Wp + bp

    def _L1_ffn_ref(x, gate_w, w1, b1, w2, b2, ln_g, ln_b):
        import jax, jax.numpy as jnp
        import numpy as np
        E, K, D = (8, 2, 128)
        B, S = (2, 512)

        def _layernorm(x, g, b, eps=1e-06):
            m = jnp.mean(x, axis=-1, keepdims=True)
            v = jnp.var(x, axis=-1, keepdims=True)
            return (x - m) * jax.lax.rsqrt(v + eps) * g + b
        orig_shape = x.shape
        xt = x.reshape(-1, orig_shape[-1])
        scores = xt @ gate_w
        ew, ei = jax.lax.top_k(scores, K)
        ew = jax.nn.softmax(ew, axis=-1)
        mask = ei[None, :, :] == jnp.arange(E)[:, None, None]
        wE = jnp.sum(ew[None, :, :] * mask, axis=-1)
        h = jax.nn.gelu(jnp.einsum('td,edf->etf', xt, w1) + b1[:, None, :], approximate=False)
        o = jnp.einsum('etf,efd->etd', h, w2) + b2[:, None, :]
        y = _layernorm(xt[None, :, :] + o, ln_g[:, None, :], ln_b[:, None, :])
        out = jnp.einsum('et,etd->td', wE, y)
        return out.reshape(orig_shape)

    def _L2_xattn_ref(xx, ee, ln1_g, ln1_b, ln2_g, ln2_b, a1_wq, a1_wk, a1_wv, a1_li1_w, a1_li1_b, a1_lnx_g, a1_lnx_b, a1_lny_g, a1_lny_b, a1_ln3_g, a1_ln3_b, a1_li2_w, a1_li2_b, a1_li3_w, a1_li3_b, a2_wq, a2_wk, a2_wv, a2_li1_w, a2_li1_b, a2_lnx_g, a2_lnx_b, a2_lny_g, a2_lny_b, a2_ln3_g, a2_ln3_b, a2_li2_w, a2_li2_b, a2_li3_w, a2_li3_b, training):
        import jax, jax.numpy as jnp
        import numpy as np
        H, D, C1, C2, S, M, B, W = (16, 32, 128, 64, 256, 64, 2, 4)

        def _ln(x, g, b):
            m = jnp.mean(x, -1, keepdims=True)
            v = jnp.var(x, -1, keepdims=True)
            return (x - m) * jax.lax.rsqrt(v + 1e-05) * g + b

        def _mha(x, y, wq, wk, wv, li1_w, li1_b, lnx_g, lnx_b, lny_g, lny_b, ln3_g, ln3_b, li2_w, li2_b, li3_w, li3_b, causal):
            xn = _ln(x, lnx_g, lnx_b)
            yn = _ln(y, lny_g, lny_b)
            q = jnp.einsum('bsc,hcd->bhsd', xn, wq)
            k = jnp.einsum('btc,hcd->bhtd', yn, wk)
            v = jnp.einsum('btc,hcd->bhtd', yn, wv)
            a = jax.nn.softmax(jnp.einsum('bhsd,bhtd->bhst', q, k) * D ** (-0.5), axis=-1)
            if causal:
                s, t = (a.shape[-2], a.shape[-1])
                mask = (jnp.arange(t)[None, :] > jnp.arange(s)[:, None]).astype(a.dtype)
                a = a * mask
            o = jnp.einsum('bhst,bhtd->bhsd', a, v)
            o = o.transpose(0, 2, 1, 3).reshape(x.shape[0], x.shape[1], H * D)
            x_out = x + o @ li1_w + li1_b
            h = jax.nn.gelu(_ln(x_out, ln3_g, ln3_b) @ li2_w + li2_b, approximate=False)
            return x_out + h @ li3_w + li3_b
        x = _ln(xx, ln1_g, ln1_b)
        x = x + _mha(x, x, a1_wq, a1_wk, a1_wv, a1_li1_w, a1_li1_b, a1_lnx_g, a1_lnx_b, a1_lny_g, a1_lny_b, a1_ln3_g, a1_ln3_b, a1_li2_w, a1_li2_b, a1_li3_w, a1_li3_b, causal=True)
        x = _ln(x, ln2_g, ln2_b)
        return x + _mha(x, ee, a2_wq, a2_wk, a2_wv, a2_li1_w, a2_li1_b, a2_lnx_g, a2_lnx_b, a2_lny_g, a2_lny_b, a2_ln3_g, a2_ln3_b, a2_li2_w, a2_li2_b, a2_li3_w, a2_li3_b, causal=False)

    def _L2_ffn_ref(x, W1, b1, W2, b2, Wr, br):
        import jax, jax.numpy as jnp
        import numpy as np
        from jax import lax
        D = 128
        H = 512
        E = 8
        TOPK = 2
        B, S, _ = x.shape
        xf = x.reshape(-1, D)
        logits = xf @ Wr + br
        topv, _ = lax.top_k(logits, TOPK)
        thresh = topv[:, TOPK - 1:TOPK]
        masked = jnp.where(logits >= thresh, logits, -jnp.inf)
        weights = jax.nn.softmax(masked, axis=-1)
        h = jax.nn.gelu(jnp.einsum('td,edh->eth', xf, W1) + b1[:, None, :], approximate=False)
        expert_out = jnp.einsum('eth,ehd->etd', h, W2) + b2[:, None, :]
        out = jnp.einsum('etd,te->td', expert_out, weights)
        return out.reshape(B, S, D)

    def _L3_xattn_ref(x, z, Wq, Wkv, Wo):
        import jax, jax.numpy as jnp
        import numpy as np
        DIM = 128
        LATENT_DIM = 64
        NUM_HEADS = 16
        HEAD_DIM = DIM // NUM_HEADS
        SCALE = HEAD_DIM ** (-0.5)
        B, xN, _ = x.shape
        _, zN, _ = z.shape
        Q = (x @ Wq.T).reshape(B, xN, NUM_HEADS, HEAD_DIM)
        KV = (z @ Wkv.T).reshape(B, zN, 2, NUM_HEADS, HEAD_DIM)
        K = KV[:, :, 0]
        V = KV[:, :, 1]
        attn = jnp.einsum('bqhd,bkhd->bhqk', Q, K) * SCALE
        attn = jax.nn.softmax(attn, axis=-1)
        O = jnp.einsum('bhqk,bkhd->bqhd', attn, V).reshape(B, xN, DIM)
        return O @ Wo.T

    def _L3_ffn_ref(x, W1, b1, W2, b2):
        import jax, jax.numpy as jnp
        import numpy as np
        QB = 127.0
        EPS = 1e-05

        def _ste(x, q):
            return x + jax.lax.stop_gradient(q - x)

        def bitlinear(x, W, b):
            w_scale = jnp.clip(jnp.mean(jnp.abs(W)), EPS, None)
            Wq = _ste(W, jnp.clip(jnp.round(W / w_scale), -1.0, 1.0) * w_scale)
            x_scale = jnp.clip(jnp.max(jnp.abs(x), axis=-1, keepdims=True), EPS, None)
            xq = _ste(x, jnp.clip(jnp.round(x * (QB / x_scale)), -QB - 1.0, QB) * (x_scale / QB))
            return jnp.einsum('bnd,hd->bnh', xq, Wq) + b
        h = bitlinear(x, W1, b1)
        h = jax.nn.gelu(h, approximate=False)
        return bitlinear(h, W2, b2)
    x = x + _L0_xattn_ref(_layernorm(x, axis=-1), ctx_512, ctx_512, L0_xattn_Wq, L0_xattn_bq, L0_xattn_Wk, L0_xattn_bk, L0_xattn_Wv, L0_xattn_bv, L0_xattn_Wo, L0_xattn_bo)
    x = x + _L0_ffn_ref(_layernorm(x, axis=-1), L0_ffn_gate_w, L0_ffn_gate_b, L0_ffn_w1, L0_ffn_b1, L0_ffn_w2, L0_ffn_b2, L0_ffn_wg, L0_ffn_bg, L0_ffn_w3, L0_ffn_b3)
    x = x + _L1_xattn_ref(_layernorm(x, axis=-1), ctx_512, L1_xattn_Wk, L1_xattn_bk, L1_xattn_Wq, L1_xattn_bq, L1_xattn_Wv, L1_xattn_bv, L1_xattn_Wck, L1_xattn_bck, L1_xattn_Wcq, L1_xattn_bcq, L1_xattn_Wcv, L1_xattn_bcv, L1_xattn_Wp, L1_xattn_bp)
    x = x + _L1_ffn_ref(_layernorm(x, axis=-1), L1_ffn_gate_w, L1_ffn_w1, L1_ffn_b1, L1_ffn_w2, L1_ffn_b2, L1_ffn_ln_g, L1_ffn_ln_b)
    x = x + _L2_xattn_ref(_layernorm(x, axis=-1), ctx_512, L2_xattn_ln1_g, L2_xattn_ln1_b, L2_xattn_ln2_g, L2_xattn_ln2_b, L2_xattn_a1_wq, L2_xattn_a1_wk, L2_xattn_a1_wv, L2_xattn_a1_li1_w, L2_xattn_a1_li1_b, L2_xattn_a1_lnx_g, L2_xattn_a1_lnx_b, L2_xattn_a1_lny_g, L2_xattn_a1_lny_b, L2_xattn_a1_ln3_g, L2_xattn_a1_ln3_b, L2_xattn_a1_li2_w, L2_xattn_a1_li2_b, L2_xattn_a1_li3_w, L2_xattn_a1_li3_b, L2_xattn_a2_wq, L2_xattn_a2_wk, L2_xattn_a2_wv, L2_xattn_a2_li1_w, L2_xattn_a2_li1_b, L2_xattn_a2_lnx_g, L2_xattn_a2_lnx_b, L2_xattn_a2_lny_g, L2_xattn_a2_lny_b, L2_xattn_a2_ln3_g, L2_xattn_a2_ln3_b, L2_xattn_a2_li2_w, L2_xattn_a2_li2_b, L2_xattn_a2_li3_w, L2_xattn_a2_li3_b, 0)
    x = x + _L2_ffn_ref(_layernorm(x, axis=-1), L2_ffn_W1, L2_ffn_b1, L2_ffn_W2, L2_ffn_b2, L2_ffn_Wr, L2_ffn_br)
    x = x + _L3_xattn_ref(_layernorm(x, axis=-1), ctx_512, L3_xattn_Wq, L3_xattn_Wkv, L3_xattn_Wo)
    x = x + _L3_ffn_ref(_layernorm(x, axis=-1), L3_ffn_W1, L3_ffn_b1, L3_ffn_W2, L3_ffn_b2)
    return x

_drawn_inputs = setup_inputs


def setup_inputs(seed=0):
    import zlib

    import numpy as np

    out = dict(_drawn_inputs(seed))
    spreads = {'L0_xattn_bq': (0.0, 0.287),
     'L0_xattn_bk': (0.0, 2.0),
     'L0_xattn_bv': (0.0, 0.1),
     'L0_xattn_bo': (0.0, 0.1),
     'L0_ffn_gate_b': (0.0, 0.1),
     'L0_ffn_b1': (0.0, 0.8),
     'L0_ffn_b2': (0.0, 0.8),
     'L0_ffn_bg': (0.0, 0.668),
     'L0_ffn_b3': (0.0, 0.314),
     'L1_xattn_bk': (0.0, 2.0),
     'L1_xattn_bq': (0.0, 0.591),
     'L1_xattn_bv': (0.0, 0.271),
     'L1_xattn_bck': (0.0, 2.0),
     'L1_xattn_bcq': (0.0, 1.102),
     'L1_xattn_bcv': (0.0, 0.1),
     'L1_xattn_bp': (0.0, 0.1),
     'L1_ffn_b1': (0.0, 0.8),
     'L1_ffn_b2': (0.0, 0.452),
     'L1_ffn_ln_g': (1.0, 0.2),
     'L1_ffn_ln_b': (0.0, 0.267),
     'L2_xattn_ln1_g': (1.0, 0.2),
     'L2_xattn_ln1_b': (0.0, 0.1),
     'L2_xattn_ln2_g': (1.0, 0.2),
     'L2_xattn_ln2_b': (0.0, 0.1),
     'L2_xattn_a1_li1_b': (0.0, 0.349),
     'L2_xattn_a1_lnx_g': (1.0, 0.6),
     'L2_xattn_a1_lnx_b': (0.0, 0.8),
     'L2_xattn_a1_lny_g': (1.0, 0.6),
     'L2_xattn_a1_lny_b': (0.0, 0.8),
     'L2_xattn_a1_ln3_g': (1.0, 0.6),
     'L2_xattn_a1_ln3_b': (0.0, 0.8),
     'L2_xattn_a1_li2_b': (0.0, 0.8),
     'L2_xattn_a1_li3_b': (0.0, 0.363),
     'L2_xattn_a2_li1_b': (0.0, 0.355),
     'L2_xattn_a2_lnx_g': (1.0, 0.6),
     'L2_xattn_a2_lnx_b': (0.0, 0.8),
     'L2_xattn_a2_lny_g': (1.0, 0.6),
     'L2_xattn_a2_lny_b': (0.0, 0.8),
     'L2_xattn_a2_ln3_g': (1.0, 0.6),
     'L2_xattn_a2_ln3_b': (0.0, 0.8),
     'L2_xattn_a2_li2_b': (0.0, 0.8),
     'L2_xattn_a2_li3_b': (0.0, 0.35),
     'L2_ffn_b1': (0.0, 0.8),
     'L2_ffn_b2': (0.0, 0.493),
     'L2_ffn_br': (0.0, 0.73),
     'L3_ffn_b1': (0.0, 0.8),
     'L3_ffn_b2': (0.0, 0.367)}
    factors = {'L0_ffn_w1': 8.0,
     'L0_ffn_w2': 8.0,
     'L0_ffn_wg': 8.0,
     'L0_ffn_w3': 4.778,
     'L1_ffn_w1': 4.91,
     'L1_ffn_w2': 4.416,
     'L2_xattn_a1_wq': 8.0,
     'L2_xattn_a1_wk': 8.0,
     'L2_xattn_a1_wv': 5.927,
     'L2_xattn_a1_li1_w': 5.945,
     'L2_xattn_a1_li2_w': 4.536,
     'L2_xattn_a1_li3_w': 3.824,
     'L2_xattn_a2_wq': 8.0,
     'L2_xattn_a2_wk': 8.0,
     'L2_xattn_a2_wv': 6.237,
     'L2_xattn_a2_li1_w': 6.183,
     'L2_xattn_a2_li2_w': 4.556,
     'L2_xattn_a2_li3_w': 4.148,
     'L2_ffn_W1': 6.773,
     'L2_ffn_W2': 6.138,
     'L2_ffn_Wr': 3.875,
     'L3_ffn_W1': 8.0,
     'L3_ffn_W2': 8.0}
    for name, (base, spread) in spreads.items():
        noise = np.random.default_rng([zlib.crc32(name.encode()), seed]).standard_normal(out[name].shape)
        drawn = base * np.exp(spread * noise) if base else spread * noise
        out[name] = jnp.asarray(drawn.astype(out[name].dtype))
    for name, factor in factors.items():
        out[name] = (out[name] * factor).astype(out[name].dtype)
    return out
```

```python
from contextlib import ExitStack

import concourse.bass as bass
from concourse import mybir

F32 = mybir.dt.float32
F32R = mybir.dt.float32r
BF16 = mybir.dt.bfloat16
U32 = mybir.dt.uint32
ACT = mybir.ActivationFunctionType
ALU = mybir.AluOpType
AX = mybir.AxisListType

P = 128
NB = 16
T = 256
TT = T // P
D = 128
CK = 64
NH = 16
NE = 8
EPS = 1e-5


def wait(eng, sem, value):
    if isinstance(value, int) and value <= 0:
        return
    eng.wait_ge(sem, value)


def phase(build):
    def built(nc, *args, **kwargs):
        with nc.cleanup_on_exit():
            build(nc, *args, **kwargs)
    return built


def bcast_row(ap, n=P):
    return ap.rearrange("(a n) -> a n", a=1).broadcast_to([n, ap.shape[0]])


def column(ap):
    return ap.rearrange("(p a) -> p a", a=1)


@phase
def make_constants(nc, K):
    with ExitStack() as ctx:
        filled = nc.alloc_semaphore("const_filled")
        step = nc.alloc_semaphore("const_step")
        block = ctx.enter_context(nc.Block())

        @block.vector
        def _(dve):
            for name in ("ident", "ident_bf", "slots1_8", "slots1_32", "slots4_8", "slots4_32", "own1_8", "own1_32",
                         "own4_8", "own4_32", "tri_post"):
                last = dve.memset(K[name][:], 0.0 if name.startswith("ident") else 1.0)
            for name in ("mask_q", "mask_k"):
                last = dve.memset(K[name][:], 0.0)
            dve.memset(K["half"][:], -0.5)
            last.then_inc(filled, 1)

        @block.gpsimd
        def _(pool):
            pool.wait_ge(filled, 1)
            n = [0]

            def select(ap, op, fill, base, cm, pattern):
                if n[0]:
                    pool.wait_ge(step, n[0])
                pool.affine_select(out=ap, in_=ap, compare_op=op, fill=fill, base=base, pattern=pattern,
                                   channel_multiplier=cm).then_inc(step, 1)
                n[0] += 1

            def window(ap, lo, width, cm, pattern):
                select(ap, ALU.is_ge, 0.0, lo, cm, pattern)
                select(ap, ALU.is_ge, 0.0, width - 1 - lo, -cm, [[-s, k] for s, k in pattern])

            for name in ("ident", "ident_bf"):
                select(K[name][:], ALU.not_equal, 1.0, 0, 1, [[-1, P]])
            window(K["slots1_8"][:].rearrange("p (a q e) -> p a q e", a=2, q=4), 0, 8, 1,
                   [[-16, 2], [-32, 4], [-8, 2]])
            window(K["slots4_8"][:].rearrange("p (u q) -> p u q", u=4), 0, 8, 1, [[-8, 4], [-32, 4]])
            for name in ("slots1_32", "slots4_32"):
                window(K[name][:].rearrange("p (a q) -> p a q", q=4), 0, 32, 1,
                       [[0, K[name].shape[1] // 4], [-32, 4]])
            v = K["own1_8"][:].rearrange("p a (l e d) -> p a l e d", l=2, e=2)
            for a in range(2):
                select(v[:, a], ALU.is_equal, 0.0, -a, 0, [[1, 2], [0, 2], [0, 8]])
                window(v[:, a], 0, 64, 1, [[0, 2], [-64, 2], [0, 8]])
            window(K["own1_32"][:].rearrange("p (e d) -> p e d", e=2), 0, 64, 1, [[-64, 2], [0, 32]])
            window(K["own4_8"][:].rearrange("p u (l d) -> p u l d", l=4), 0, 1, 0, [[-1, 4], [1, 4], [0, 8]])
            select(K["tri_post"][:], ALU.is_gt, 0.0, 0, 1, [[-1, P]])
            select(K["mask_q"][:], ALU.is_ge, -1e30, 0, 1, [[P, TT], [-1, T]])
            select(K["mask_k"][:], ALU.is_ge, -1e30, 0, -1, [[-P, TT], [1, T]])
            pool.wait_ge(step, n[0])


def constants(nc, ctx):
    def sb(name, shape, dt=F32):
        return ctx.enter_context(nc.sbuf_tensor(name, shape, dt))
    return {
        "passed": ctx.enter_context(nc.semaphore("passed")),
        "ident": sb("ident", [P, P]), "ident_bf": sb("ident_bf", [P, P], BF16),
        "slots1_8": sb("slots1_8", [P, 16]), "slots4_8": sb("slots4_8", [P, 16]),
        "slots1_32": sb("slots1_32", [P, 16]), "slots4_32": sb("slots4_32", [P, 16]),
        "own1_8": sb("own1_8", [P, 2, 32]), "own1_32": sb("own1_32", [P, 64]),
        "own4_8": sb("own4_8", [P, 4, 32]), "own4_32": sb("own4_32", [P, 32]),
        "tri_post": sb("tri_post", [P, P]),
        "mask_q": sb("mask_q", [P, TT, T], BF16), "mask_k": sb("mask_k", [P, TT, T], BF16),
        "half": sb("half", [P, 8]),
    }


@phase
def attention(nc, name, K, W, *, dh, units, x, out, norms=(), affine_q=None, affine_kv=None, biases=None,
              out_bias=None, causal=None, ctx_t=None, add_t=None, store_t=None, residual=None):
    C = dh * NH // P
    U = units
    N = NB * U
    per_unit = U == 4 and C == 4
    DP = 4 if per_unit else 2
    NLN = len(norms) + 1
    NK = CK if U == 1 else T
    split_norm = U == 1 and C == 4
    scale = float(dh) ** -0.5
    slots = K[f"slots{U}_{dh}"]
    own = K[f"own{U}_{dh}"]
    QC = 1 if per_unit else C

    with ExitStack() as ctx:
        def sb(nm, shape, dt=F32):
            return ctx.enter_context(nc.sbuf_tensor(f"{name}_{nm}", shape, dt))

        def sem(nm):
            return nc.alloc_semaphore(f"{name}_{nm}")

        wq, wk, wv, wo = (sb(n, [P, C, P] if n == "wo" else [P, C * P]) for n in ("wq", "wk", "wv", "wo"))
        bq = bk = bvb = bob = None
        if biases:
            bq, bk, bvb = sb("bq", [P, 1]), sb("bk", [P, 1]), sb("bvb", [P, P])
        if out_bias is not None:
            bob = sb("bob", [P, P])
        gb = [pair and (sb(f"g{i}", [P, P]), sb(f"b{i}", [P, P])) for i, pair in enumerate(norms)]
        aq = (sb("aqg", [P, 1]), sb("aqb", [P, 1])) if affine_q else None
        akv = (sb("akg", [P, 1]), sb("akb", [P, 1])) if affine_kv else None

        xn = sb("xn", [P, TT, P])
        mv = sb("mv", [P, NLN, TT, 2])
        st6 = sb("st6", [P, NLN, TT, 6])
        rstd = sb("rstd", [P, NLN, TT])
        veps = sb("veps", [P, NLN, TT])
        xq_t = sb("xq_t", [P, T])
        xkv_t = sb("xkv_t", [P, T]) if affine_kv else xq_t
        cdup = sb("cdup", [P, 2, 2, CK]) if U == 1 else None
        q_f = sb("q_f", [P, QC, T])
        k_f = sb("k_f", [P, QC, NK])
        q_hi, q_lo = sb("q_hi", [P, 2, QC, T], F32R), sb("q_lo", [P, 2, QC, T], F32R)
        k_hi, k_lo = sb("k_hi", [P, 2, QC, NK], F32R), sb("k_lo", [P, 2, QC, NK], F32R)
        kb_hi, kb_lo = sb("kb_hi", [P, 2, 1024], F32R), sb("kb_lo", [P, 2, 1024], F32R)
        negm = sb("negm", [P, 2, TT, 16 // U], BF16)
        if per_unit:
            v_f = sb("v_f", [P, DP, TT, P])
            vb = v_f
        else:
            v_f = sb("v_f", [P, TT if U == 4 else 1, C * P])
            vb = sb("vb", [P, 2, {(1, 8): 256, (1, 32): 512, (4, 8): 1024}[U, dh]])
        pt = sb("pt", [P, 2, 4, T])
        pm = sb("pm", [P, 2, 4, P]) if causal == "after" else None
        rden = sb("rden", [P, 2, 512 if split_norm else T])
        o_t = sb("o_t", [P, C, T]) if store_t is None else None
        res = sb("res", [P, TT, P]) if store_t is None else None

        psum_st = [ctx.enter_context(nc.psum_tensor(f"{name}_st{g}", [P, 4, T], F32)) for g in range(2)]
        WN = 512 if split_norm else T
        psum_nd = ctx.enter_context(nc.psum_tensor(f"{name}_nd", [P, 2, WN], F32))
        psum_num, psum_den = psum_nd[:, 0, :], psum_nd[:, 1, :]
        psum_act = ctx.enter_context(nc.psum_tensor(f"{name}_pa", [P, 512], F32))
        BANKS = 1 if split_norm else 2
        psum_s = [ctx.enter_context(nc.psum_tensor(f"{name}_s{i}", [P, 512], F32)) for i in range(BANKS)]
        psum_w = psum_s[-1]

        loaded = sem("loaded")
        zeroed = sem("zeroed")
        stats = sem("stats")
        rstd_ready = sem("rstd_ready")
        vstep = sem("vstep")
        pstep = sem("pstep")
        xn_ready = sem("xn_ready")
        xn_turned = sem("xn_turned")
        x_t_ready = sem("x_t_ready")
        cdup_ready = sem("cdup_ready")
        proj_done = sem("proj_done")
        proj_out = sem("proj_out")
        k_split = sem("k_split")
        q_split = sem("q_split")
        kb_hi_ready = sem("kb_hi_ready")
        kb_lo_ready = sem("kb_lo_ready")
        v_step = sem("v_step")
        vb_ready = sem("vb_ready")
        s_ready = sem("s_ready")
        max_done = sem("max_done")
        st_ready = sem("st_ready")
        exp_done = sem("exp_done")
        pm_ready = sem("pm_ready")
        pv_done = sem("pv_done")
        rden_ready = sem("rden_ready")
        norm_done = sem("norm_done")
        w_done = sem("w_done")
        wres = sem("wres")
        res_done = sem("res_done")

        if U == 4:
            uses = [["q0", "k0"], ["v"]]
        elif C == 1:
            uses = [["q0", "k0", "v"]]
        else:
            uses = [["q0", "q1"], ["q2", "q3"], ["k0", "k1", "k2", "k3"], ["v"]]
        NU = len(uses)
        PM_ = N if per_unit else NB

        def pset(n, b):
            return n if per_unit else b

        def arrived(m, what):
            return m * NU + max(i for i, use in enumerate(uses) if any(w[0] == what for w in use)) + 1

        def steps(emit):
            def pos(i, j):
                def at(k):
                    jj = j + k
                    return 2 * U * i + jj, 2 * i + jj // U, jj % U, jj % (2 * U)
                return at
            return pos

        def run(eng, emit):
            pos = steps(emit)
            for j in range(-3, 2 * U):
                emit(pos(0, j))
            looped = NB // 2 - (2 if U == 1 else 1)
            with eng.Fori(1, looped) as i:
                for j in range(2 * U):
                    emit(pos(i, j))
            for j in range(2 * U * (NB // 2 - looped) + 1):
                emit(pos(looped, j))

        def inside(n, limit=N):
            return not isinstance(n, int) or 0 <= n < limit

        def spread_keys(eng, dst, src, n, b, u, pos):
            par, par_m = pos % 2, (pos % 2) if (per_unit or U == 1) else (pos // U) % 2
            if U == 1 and C == 1:
                o, a = [P, 16, CK], src[:, par_m, 0, :].bitcast(F32).unsqueeze(1).broadcast_to([P, 16, CK])
                s = slots[:].unsqueeze(2).broadcast_to(o)
                d = dst[:, par, :].rearrange("p (s k) -> p s k", s=16)
            elif U == 1:
                o = [P, C, 4, CK]
                a = src[:, par_m].bitcast(F32).unsqueeze(2).broadcast_to(o)
                s = slots[:].rearrange("p (c q) -> p c q", q=4).unsqueeze(3).broadcast_to(o)
                d = dst[:, par, :].rearrange("p (c q k) -> p c q k", c=C, q=4)
            else:
                o = [P, 4, T]
                a = src[:, par_m, 0, :].bitcast(F32).unsqueeze(1).broadcast_to(o)
                s = slots[:, 4 * u:4 * u + 4].unsqueeze(2).broadcast_to(o)
                d = dst[:, par, :].rearrange("p (q k) -> p q k", q=4)
            return eng.tensor_tensor(d, a, s, ALU.mult)

        vb_sum = sem("vb_sum")
        res_out = sem("res_out")
        block = ctx.enter_context(nc.Block())

        @block.sync
        def _(sp):
            n = 0
            rows = W["k_rows"]
            for dst, src in ([(wq[:], W["wq"]), (wk[0:rows, :], W["wk"]), (wv[0:rows, :], W["wv"]), (wo[:], W["wo"])]
                             + ([(bq[:], column(biases[0])), (bk[:], column(biases[1])),
                                 (bvb[:], bcast_row(biases[2]))] if biases else [])
                             + ([(bob[:], bcast_row(out_bias))] if bob is not None else [])
                             + [(t[:], bcast_row(a)) for pair, own_ in zip(norms, gb) if pair for a, t in zip(pair, own_)]
                             + ([(t[:], column(a)) for a, t in zip(affine_q, aq)] if aq else [])
                             + ([(t[:], column(a)) for a, t in zip(affine_kv, akv)] if akv else [])):
                sp.dma_start(dst, src).then_inc(loaded, 16)
                n += 1
            sp.wait_ge(loaded, 16 * n)

        n_loads = 4 + (3 if biases else 0) + (bob is not None) + 2 * sum(pair is not None for pair in norms) + (2 if aq else 0) + (2 if akv else 0)

        @block.tensor
        def _(pe):
            pe.wait_ge(loaded, 16 * n_loads)
            if U == 1:
                pe.wait_ge(zeroed, 1)

            def turn(b):
                sets = b * (U if per_unit else 1)
                wait(pe, proj_out, sets * NU)
                pe.wait_ge(xn_ready, b + 1)
                for t in range(TT):
                    last = pe.transpose(psum_act[:, t * P:(t + 1) * P], xn[:, t, :], K["ident"][:])
                last.then_inc(xn_turned, 1)

            def project(n, b, u, pos, i):
                m = pset(n, b)
                if i == 0:
                    pe.wait_ge(x_t_ready, b + 1)
                    wait(pe, proj_out, m * NU)
                else:
                    pe.wait_ge(proj_out, m * NU + i)
                if U == 1 and "v" in uses[i]:
                    pe.wait_ge(cdup_ready, b + 1)
                col = 0
                for what in uses[i]:
                    if what[0] == "q":
                        c = u if per_unit else int(what[1])
                        last = pe.matmul(psum_act[:, col:col + T], wq[:, c * P:(c + 1) * P], xq_t[:],
                                         start=True, stop=True)
                        col += T
                    elif what[0] == "k":
                        c = u if per_unit else int(what[1])
                        src = xkv_t[:] if U == 4 else ctx_t[:, bass.ds(b * CK, CK)]
                        last = pe.matmul(psum_act[:, col:col + NK], wk[:, c * P:(c + 1) * P], src,
                                         start=True, stop=True)
                        col += NK
                    elif U == 4:
                        c = u if per_unit else 0
                        for t in range(TT):
                            last = pe.matmul(psum_act[:, t * P:(t + 1) * P], xkv_t[:, t * P:(t + 1) * P],
                                             wv[:, c * P:(c + 1) * P], start=True, stop=True)
                    else:
                        last = pe.matmul(psum_act[:, col:col + C * P],
                                         cdup[:, (pos // U) % 2].rearrange("p a k -> p (a k)"), wv[:],
                                         start=True, stop=True)
                last.then_inc(proj_done, 1)

            def scores(n, b, u, pos, i, projected=None):
                qt, half = divmod(i, 2)
                if i == 0:
                    pe.wait_ge(proj_out, arrived(pset(n, b), "q"))
                    pe.wait_ge(kb_hi_ready, n + 1)
                wait(pe, max_done, 4 * n + i + 1 - BANKS)
                if i == 3 and projected is not None:
                    pe.wait_ge(res_done, projected + 1)
                dst = psum_s[i % BANKS]
                par_q = (pos % 2) if (per_unit or U == 1) else (pos // U) % 2
                n_mm = 2 if split_norm else 1
                for s in range(n_mm):
                    c = 2 * half + s if split_norm else 0
                    w = 512 // n_mm
                    last = pe.matmul(dst[:, s * w:(s + 1) * w], q_hi[:, par_q, c, qt * P:(qt + 1) * P],
                                     kb_hi[:, pos % 2, half * 512 + s * w:half * 512 + (s + 1) * w],
                                     start=True, stop=causal != "before")
                if causal == "before":
                    last = pe.matmul(dst[:].rearrange("p (h k) -> p h k", h=2), K["ident_bf"][:],
                                     K["mask_q"][:, qt:qt + 1, :].broadcast_to([P, 2, T]), start=False, stop=True)
                last.then_inc(s_ready, 1)

            def scores_t(n, b, u, pos, g):
                if g == 0:
                    pe.wait_ge(q_split, pset(n, b) + 1)
                    pe.wait_ge(kb_lo_ready, n + 1)
                    pe.wait_ge(max_done, 4 * n + 4)
                wait(pe, exp_done, 2 * n - 1 + g)
                par, par_q = pos % 2, (pos % 2) if (per_unit or U == 1) else (pos // U) % 2
                for i in range(4):
                    t = 4 * g + i
                    c = t // 2 if split_norm else 0
                    col = t * P if U == 1 else (t % 4) * T + (t // 4) * P
                    dst = psum_st[g][:, i, :]
                    for j, (a, q) in enumerate(((kb_hi, q_hi), (kb_lo, q_hi), (kb_hi, q_lo))):
                        pe.matmul(dst, a[:, par, col:col + P], q[:, par_q, c, :], start=j == 0, stop=False)
                    if causal == "before":
                        pe.matmul(dst, K["ident_bf"][:], K["mask_k"][:, t // 4, :], start=False, stop=False)
                    for qt in range(TT):
                        if U == 4:
                            last = pe.matmul(dst[:, qt * P:(qt + 1) * P],
                                             negm[:, par, qt, t % 4:t % 4 + 1].broadcast_to([P, P]),
                                             K["ident_bf"][:], start=False, stop=qt == 1)
                        else:
                            for e in range(2):
                                last = pe.matmul(psum_st[g][64 * e:64 * e + 64, i, qt * P:(qt + 1) * P],
                                                 negm[:, par, qt, 2 * t + e:2 * t + e + 1].broadcast_to([P, 64]),
                                                 K["ident_bf"][:], start=False, stop=qt == 1)
                last.then_inc(st_ready, 1)

            def values(n, b, u, pos, g):
                pe.wait_ge(exp_done, 2 * n + 1 + g)
                if g == 0:
                    pe.wait_ge(vb_ready if not per_unit else proj_out,
                               (pset(n, b) + 1) * (NU if per_unit else 1))
                if split_norm:
                    wait(pe, norm_done, 2 * n + g)
                elif U == 4 and not per_unit:
                    if u == 0 and g == 0:
                        wait(pe, norm_done, b)
                elif g == 0:
                    wait(pe, norm_done, n)
                if pm is not None:
                    pe.wait_ge(pm_ready, 2 * n + 1 + g)
                par = pos % 2
                for kind in ("num", "den"):
                    bank = psum_num if kind == "num" else psum_den
                    for i in range(4):
                        t = 4 * g + i
                        if split_norm:
                            lhs = vb[:, par, t * 64:(t + 1) * 64] if kind == "num" else own[:]
                            dst = bank[64 * (t % 2):64 * (t % 2) + 64, (i // 2) * T:(i // 2 + 1) * T]
                            last = pe.matmul(dst, lhs, pt[:, g, i, :], start=True, stop=True)
                            continue
                        dst = bank[32 * i:32 * i + 32, 0:T]
                        if U == 1:
                            lhs = vb[:, par, g * P + i * 32:g * P + (i + 1) * 32] if kind == "num" else own[:, g, :]
                            start, stop = g == 0, g == 1
                        elif C == 1:
                            vpar = (pos // U) % 2
                            o = g * 512 + u * P + i * 32
                            lhs = vb[:, vpar, o:o + 32] if kind == "num" else own[:, u, :]
                            start, stop = u == 0 and g == 0, u == 3 and g == 1
                        else:
                            lhs = vb[:, pos % DP, g, 32 * i:32 * i + 32] if kind == "num" else own[:]
                            start, stop = g == 0, g == 1
                        start, stop = start and kind == "num", stop and kind == "den"
                        if pm is not None and kind == "num":
                            if g == 0:
                                last = pe.matmul(dst[:, 0:P], lhs, pm[:, 0, i, :], start=True, stop=False)
                            else:
                                pe.matmul(dst[:, 0:P], lhs, pt[:, 1, i, 0:P], start=False, stop=False)
                                last = pe.matmul(dst[:, P:T], lhs, pm[:, 1, i, :], start=False, stop=False)
                        else:
                            last = pe.matmul(dst, lhs, pt[:, g, i, :], start=start, stop=stop)
                last.then_inc(pv_done, 1)

            def project_out(n, b):
                pe.wait_ge(norm_done, (b + 1) * (2 if split_norm else U if per_unit else 1))
                for t in range(TT):
                    for c in range(C):
                        last = pe.matmul(psum_w[:, t * P:(t + 1) * P], o_t[:, c, t * P:(t + 1) * P], wo[:, c, :],
                                         start=c == 0, stop=c == C - 1)
                last.then_inc(w_done, 1)

            def emit(at):
                n, b, u, pos = at(0)
                n1, b1, u1, pos1 = at(-1)
                nn, bn, un, posn = at(1)
                n2, b2, u2, pos2 = at(2)
                out_now = inside(n1) and u1 == U - 1 and store_t is None
                do_p = inside(n2) and (per_unit or u2 == 0)
                if inside(n):
                    scores_t(n, b, u, pos, 0)
                if inside(n1):
                    values(n1, b1, u1, pos1, 1)
                if inside(nn):
                    scores(nn, bn, un, posn, 0)
                if inside(n2) and u2 == 0:
                    turn(b2)
                if inside(nn):
                    scores(nn, bn, un, posn, 1)
                if inside(n):
                    scores_t(n, b, u, pos, 1)
                if do_p:
                    project(n2, b2, u2, pos2, 0)
                if inside(nn):
                    scores(nn, bn, un, posn, 2)
                if out_now:
                    pe.wait_ge(max_done, 4 * nn + 4 - BANKS if inside(nn) else 4 * N)
                    if not inside(nn):
                        wait(pe, res_done, b1)
                    project_out(n1, b1)
                if do_p and NU == 4:
                    project(n2, b2, u2, pos2, 1)
                if inside(n):
                    values(n, b, u, pos, 0)
                if do_p and NU == 4:
                    project(n2, b2, u2, pos2, 2)
                if inside(nn):
                    scores(nn, bn, un, posn, 3, b1 if out_now else None)
                if do_p and NU > 1:
                    project(n2, b2, u2, pos2, NU - 1)

            run(pe, emit)

        @block.scalar
        def _(act):
            act.wait_ge(loaded, 16 * n_loads)

            def exps(n, g):
                act.wait_ge(st_ready, 2 * n + 1 + g)
                wait(act, pv_done, 2 * n - 1 + g)
                if pm is not None:
                    wait(act, pm_ready, 2 * n - 1 + g)
                act.activation(pt[:, g], psum_st[g][:], ACT.Exp, scale=scale).then_inc(exp_done, 1)

            def turned(b):
                act.wait_ge(xn_turned, b + 1)
                if akv:
                    act.activation(xkv_t[:], psum_act[:, 0:T], ACT.Identity, scale=akv[0][:], bias=akv[1][:])
                act.activation(xq_t[:], psum_act[:, 0:T], ACT.Identity, scale=aq[0][:] if aq else 1.0,
                               bias=aq[1][:] if aq else 0.0).then_inc(x_t_ready, 1)

            def hi_free(m):
                wait(act, st_ready, 2 * (m - 1) if (per_unit or U == 1) else 2 * U * (m - 1))

            def copy_out(n, b, u, pos, i):
                m = pset(n, b)
                par = (pos % 2) if (per_unit or U == 1) else (pos // U) % 2
                act.wait_ge(proj_done, m * NU + i + 1)
                col, k, nq = 0, 0, 0
                last = None
                for what in uses[i]:
                    if what[0] == "q":
                        c = int(what[1])
                        if c == 0:
                            wait(act, q_split, m)
                            hi_free(m)
                        for dst in (q_f[:, c, :], q_hi[:, par, c, :]):
                            last = act.activation(dst, psum_act[:, col:col + T], ACT.Identity,
                                                  bias=bq[:] if bq is not None else 0.0)
                        col += T
                    elif what[0] == "k":
                        c = int(what[1])
                        if c == 0:
                            wait(act, k_split, m)
                        for dst in (k_f[:, c, :], k_hi[:, par, c, :]):
                            last = act.activation(dst, psum_act[:, col:col + NK], ACT.Identity,
                                                  bias=bk[:] if bk is not None else 0.0)
                        col += NK
                    elif per_unit:
                        wait(act, pv_done, 2 * (n - 3))
                        last = act.activation(v_f[:, pos % DP].rearrange("p t d -> p (t d)"), psum_act[:, 0:T],
                                              ACT.Identity)
                    elif U == 4:
                        wait(act, vb_ready, m)
                        last = act.activation(v_f[:].rearrange("p t d -> p (t d)"), psum_act[:, 0:T], ACT.Identity)
                    else:
                        wait(act, vb_ready, m)
                        last = act.activation(v_f[:, 0, :], psum_act[:, col:col + C * P], ACT.Identity)
                last.then_inc(proj_out, 1)

            def emit(at):
                n, b, u, pos = at(0)
                if inside(n):
                    exps(n, 0)
                n2, b2, u2, pos2 = at(2)
                if inside(n2) and u2 == 0:
                    turned(b2)
                do_p = inside(n2) and (per_unit or u2 == 0)
                if inside(n):
                    exps(n, 1)
                if do_p:
                    for i in range(NU):
                        copy_out(n2, b2, u2, pos2, i)

            run(act, emit)

        @block.vector
        def _(dve):
            dve.wait_ge(loaded, 16 * n_loads)
            if U == 1:
                dve.memset(wk[64:P, :], 0.0)
                dve.memset(wv[64:P, :], 0.0).then_inc(zeroed, 1)
            before = [sum(1 if pair is None else 3 for pair in norms[:i]) for i in range(NLN)]
            SB = before[-1] + 1

            def ln_stats(b, i):
                src = x[:, bass.ds(b * TT, TT), :] if i == 0 else (
                    residual[:, bass.ds(b * TT, TT), :] if residual is not None else None)
                dve.sem_inc(K["passed"], 1)
                for t in range(TT):
                    last = dve.bn_stats(st6[:, i, t, :], src[:, t, :])
                last.then_inc(vstep, 1)
                dve.wait_ge(vstep, b * SB + before[i] + 1)
                dve.sem_inc(K["passed"], 1)
                for t in range(TT):
                    last = dve.bn_aggr(mv[:, i, t, :], st6[:, i, t, :])
                last.then_inc(stats, 1)

            def ln_apply(b, i):
                dve.wait_ge(rstd_ready, b * NLN + i + 1)
                src = (x if i == 0 else residual)[:, bass.ds(b * TT, TT), :]
                if i == 0 or norms[0] is None:
                    wait(dve, xn_turned, b)
                plain = i < NLN - 1 and norms[i] is None
                dst = residual[:, bass.ds(b * TT, TT), :] if plain else xn
                for t in range(TT):
                    last = dve.tensor_scalar(dst[:, t, :], src[:, t, :], mv[:, i, t, 0:1], rstd[:, i, t:t + 1],
                                             ALU.subtract, ALU.mult)
                if i == NLN - 1:
                    last.then_inc(xn_ready, 1)
                    return
                if plain:
                    last.then_inc(wres, 1)
                else:
                    last.then_inc(vstep, 1)
                    dve.wait_ge(vstep, b * SB + before[i] + 2)
                    g, bb = gb[i]
                    dve.tensor_tensor(xn[:], xn[:], g[:].unsqueeze(1).broadcast_to([P, TT, P]), ALU.mult)\
                       .then_inc(vstep, 1)
                    dve.wait_ge(vstep, b * SB + before[i] + 3)
                    dve.tensor_tensor(residual[:, bass.ds(b * TT, TT), :], xn[:],
                                      bb[:].unsqueeze(1).broadcast_to([P, TT, P]), ALU.add).then_inc(wres, 1)
                dve.wait_ge(wres, b * len(norms) + i + 1)

            def keys_hi(n, b, u, pos):
                dve.wait_ge(proj_out, arrived(pset(n, b), "k"))
                wait(dve, st_ready, 2 * (n - 1))
                spread_keys(dve, kb_hi, k_hi, n, b, u, pos).then_inc(kb_hi_ready, 1)

            def maxima(n, pos, i):
                qt, half = divmod(i, 2)
                dve.wait_ge(s_ready, 4 * n + i + 1)
                h = 8 // U
                if i == 0:
                    wait(dve, st_ready, 2 * (n - 1))
                dve.tensor_reduce(negm[:, pos % 2, qt, half * h:(half + 1) * h],
                                  psum_s[i % BANKS][:].rearrange("p (h k) -> p h k", h=h), AX.X, ALU.max, negate=True)\
                   .then_inc(max_done, 1)

            norm_count = 2 if split_norm else 1

            def normalise(idx, n, b, u, g):
                w = 512 if split_norm else T
                dve.wait_ge(pv_done, 2 * n + 1 + g)
                dve.reciprocal(rden[:, 0, 0:w], psum_den[:, 0:w]).then_inc(rden_ready, 1)
                dve.wait_ge(rden_ready, idx + 1)
                if store_t is not None:
                    dve.tensor_tensor(store_t[:, bass.ds(b * T, T)], psum_num[:, 0:T], rden[:, 0, 0:T], ALU.mult)\
                       .then_inc(norm_done, 1)
                    return
                dst = o_t[:, 2 * g:2 * g + 2, :].rearrange("p c t -> p (c t)") if split_norm else \
                    o_t[:, u if per_unit else 0, :]
                if add_t is None:
                    dve.tensor_tensor(dst, psum_num[:, 0:w], rden[:, 0, 0:w], ALU.mult).then_inc(norm_done, 1)
                else:
                    dve.tensor_tensor(rden[:, 1, :], psum_num[:, 0:w], rden[:, 0, 0:w], ALU.mult)\
                       .then_inc(vb_sum, 1)
                    dve.wait_ge(vb_sum, idx + 1)
                    dve.tensor_tensor(dst, rden[:, 1, :], add_t[:, bass.ds(b * T, T)], ALU.add)\
                       .then_inc(norm_done, 1)

            def residuals(b):
                dve.wait_ge(w_done, b + 1)
                view = psum_w[:, 0:T].rearrange("p (t d) -> p t d", t=TT)
                base = (residual if residual is not None else x)[:, bass.ds(b * TT, TT), :]
                if bob is None:
                    dve.tensor_tensor(out[:, bass.ds(b * TT, TT), :], view, base, ALU.add).then_inc(res_done, 1)
                else:
                    dve.tensor_tensor(res[:], view, bob[:].unsqueeze(1).broadcast_to([P, TT, P]), ALU.add)\
                       .then_inc(res_done, 1)
                    dve.wait_ge(res_done, b + 1)
                    dve.tensor_tensor(out[:, bass.ds(b * TT, TT), :], res[:], base, ALU.add).then_inc(res_out, 1)

            def emit(at):
                n, b, u, pos = at(0)
                n1, b1, u1, _ = at(-1)
                nn, bn, un, posn = at(1)
                n3, b3, u3, _ = at(3)
                ln = inside(n3) and u3 == 0
                if inside(nn):
                    keys_hi(nn, bn, un, posn)
                    maxima(nn, posn, 0)
                if inside(n1):
                    if split_norm:
                        normalise(2 * n1 + 1, n1, b1, u1, 1)
                    elif per_unit or U == 1:
                        normalise(n1, n1, b1, u1, 1)
                    elif u1 == U - 1:
                        normalise(b1, n1, b1, u1, 1)
                if inside(nn):
                    maxima(nn, posn, 1)
                if ln:
                    ln_stats(b3, 0)
                if inside(nn):
                    maxima(nn, posn, 2)
                if inside(n1) and u1 == U - 1 and store_t is None:
                    residuals(b1)
                for i in range(NLN if ln else 0):
                    ln_apply(b3, i)
                    if i + 1 < NLN:
                        ln_stats(b3, i + 1)
                if inside(nn):
                    maxima(nn, posn, 3)
                if inside(n) and split_norm:
                    normalise(2 * n, n, b, u, 0)

            run(dve, emit)
            if bob is not None and store_t is None:
                dve.wait_ge(res_out, NB)

        @block.gpsimd
        def _(pool):
            pool.wait_ge(loaded, 16 * n_loads)

            def rstds(b, i):
                pool.wait_ge(stats, b * NLN + i + 1)
                pool.sem_inc(K["passed"], 1)
                pool.tensor_scalar(veps[:, i, :], mv[:, i, :, 1], EPS, None, ALU.add).then_inc(pstep, 1)
                pool.wait_ge(pstep, b * NLN + i + 1)
                pool.tensor_tensor(rstd[:, i, :], veps[:, i, :], K["half"][:, 0:TT], ALU.pow).then_inc(rstd_ready, 1)

            def context(b, pos):
                pool.sem_inc(K["passed"], 1)
                pool.tensor_copy(cdup[:, pos % 2],
                                 ctx_t[:, bass.ds(b * CK, CK)].unsqueeze(1).broadcast_to([P, 2, CK]))\
                    .then_inc(cdup_ready, 1)

            def split(m, par, src, hi, lo, what, ready):
                pool.wait_ge(proj_out, arrived(m, what))
                pool.tensor_tensor(lo[:, par], src[:], hi[:, par].bitcast(F32), ALU.subtract).then_inc(ready, 1)

            def lay_values(m, par):
                pool.wait_ge(proj_out, m * NU + NU)
                if bvb is not None:
                    o = [P, v_f.shape[1], P]
                    pool.tensor_tensor(v_f[:], v_f[:], bvb[:].unsqueeze(1).broadcast_to(o), ALU.add)\
                        .then_inc(v_step, 1)
                    pool.wait_ge(v_step, m + 1)
                wait(pool, pv_done, 2 * (m - 1) if U == 1 else 2 * U * (m - 1))
                if U == 1 and C == 1:
                    o = [P, 2, 4, 32]
                    pool.tensor_tensor(vb[:, par].rearrange("p (a q d) -> p a q d", a=2, q=4),
                                       v_f[:, 0].rearrange("p (q d) -> p q d", q=4).unsqueeze(1).broadcast_to(o),
                                       own[:].unsqueeze(2).broadcast_to(o), ALU.mult).then_inc(vb_ready, 1)
                elif U == 1:
                    o = [P, 8, 64]
                    pool.tensor_tensor(vb[:, par].rearrange("p (j d) -> p j d", j=8),
                                       v_f[:, 0].rearrange("p (j d) -> p j d", j=8),
                                       own[:].unsqueeze(1).broadcast_to(o), ALU.mult).then_inc(vb_ready, 1)
                else:
                    o = [P, 4, 4, 32]
                    for t in range(TT):
                        last = pool.tensor_tensor(
                            vb[:, par, t * 512:(t + 1) * 512].rearrange("p (u q d) -> p u q d", u=4, q=4),
                            v_f[:, t].rearrange("p (q d) -> p q d", q=4).unsqueeze(1).broadcast_to(o),
                            own[:].unsqueeze(2).broadcast_to(o), ALU.mult)
                    last.then_inc(vb_ready, 1)

            def mask(n, g):
                pool.wait_ge(exp_done, 2 * n + 1 + g)
                wait(pool, pv_done, 2 * n - 1 + g)
                pool.tensor_tensor(pm[:, g], pt[:, g, :, g * P:(g + 1) * P],
                                   K["tri_post"][:].unsqueeze(1).broadcast_to([P, 4, P]), ALU.mult)\
                    .then_inc(pm_ready, 1)

            def emit(at):
                n, b, u, pos = at(0)
                nn, bn, un, posn = at(1)
                n2, b2, u2, pos2 = at(2)
                n3, b3, u3, pos3 = at(3)
                ln = inside(n3) and u3 == 0
                first = inside(nn) and (per_unit or un == 0)
                m = pset(nn, bn)
                par_m = (posn % 2) if (per_unit or U == 1) else (posn // U) % 2
                if first:
                    wait(pool, st_ready, 2 * (m - 1) if (per_unit or U == 1) else 2 * U * (m - 1))
                    split(m, par_m, k_f, k_hi, k_lo, "k", k_split)
                    split(m, par_m, q_f, q_hi, q_lo, "q", q_split)
                if U == 1 and inside(n2):
                    wait(pool, proj_done, NU * (b2 - 1))
                    context(b2, pos2)
                if pm is not None and inside(n):
                    mask(n, 0)
                if inside(nn):
                    pool.wait_ge(k_split, m + 1)
                    wait(pool, st_ready, 2 * (nn - 1))
                    spread_keys(pool, kb_lo, k_lo, nn, bn, un, posn).then_inc(kb_lo_ready, 1)
                if first and not per_unit:
                    lay_values(m, par_m)
                for i in range(NLN if ln else 0):
                    rstds(b3, i)
                if pm is not None and inside(n):
                    mask(n, 1)

            run(pool, emit)
NT = NB * TT
NTOK = NB * T
CH = 512
NCH = NTOK // CH
CT = CH // P


@phase
def prepare(nc, name, K, x, x_hi, x_lo, *, affine=None, gate=None, tokens=None):
    with ExitStack() as ctx:
        def sb(nm, shape, dt=F32):
            return ctx.enter_context(nc.sbuf_tensor(f"{name}_{nm}", shape, dt))

        def sem(nm):
            return nc.alloc_semaphore(f"{name}_{nm}")

        st6, mv = sb("st6", [P, CT, 6]), sb("mv", [P, CT, 2])
        veps, rstd = sb("veps", [P, CT]), sb("rstd", [P, CT])
        xn = sb("xn", [P, 2, CT, P])
        x_t = sb("x_t", [P, 2, CH])
        ga = (sb("gain", [P, 1]), sb("bias", [P, 1])) if affine else None
        psum_t = [ctx.enter_context(nc.psum_tensor(f"{name}_t{i}", [P, CH], F32)) for i in range(2)]
        loaded, stats, vstep = sem("loaded"), sem("stats"), sem("vstep")
        pstep, rstd_ready, xn_ready = sem("pstep"), sem("rstd_ready"), sem("xn_ready")
        turned, x_t_ready, hi_ready, lo_ready = sem("turned"), sem("x_t_ready"), sem("hi_ready"), sem("lo_ready")
        kept = sem("kept")
        n_loads = 2 if affine else 0
        if gate:
            topk = gate["rule"] == "topk"
            by_expert = "we_t" in gate
            gw = sb("gw", [P, NE])
            gb = sb("gb", [P, NE]) if gate["b"] is not None else None
            lt = sb("lt", [P, CT, NE])
            m8, i8 = sb("m8", [P, CT, 8]), sb("i8", [P, CT, 8], U32)
            logits = sb("logits", [P, NT, NE])
            tops = sb("tops", [P, NT, 8])
            picks = sb("picks", [P, NT, 8])
            d1, e1, s1, p0, p1 = (sb(n, [P, NT]) for n in ("d1", "e1", "s1", "p0", "p1"))
            w0, w1 = sb("w0", [P, NT, NE]), sb("w1", [P, NT, NE])
            iota = sb("iota", [P, NE])
            psum_l = ctx.enter_context(nc.psum_tensor(f"{name}_l", [P, CT, NE], F32))
            l_ready, l_read, gstep, cstep = sem("l_ready"), sem("l_read"), sem("gstep"), sem("cstep")
            exp_ready, iota_ready, we_ready = sem("exp_ready"), sem("iota_ready"), sem("we_ready")
            n_loads += 1 + (gb is not None)
            if by_expert:
                eb = sb("eb", [NE, P])
                psum_w = [ctx.enter_context(nc.psum_tensor(f"{name}_pw{i}", [P, CH], F32)) for i in range(2)]
                psum_b = [ctx.enter_context(nc.psum_tensor(f"{name}_pb{i}", [P, CH], F32)) for i in range(2)]
                w_turned, w_copied, b_done, b_copied, stored = (
                    sem(n) for n in ("w_turned", "w_copied", "b_done", "b_copied", "stored"))
                n_loads += 1

        def run(emit):
            def body(i, last):
                emit(2 * i, 0, 2 * i + 1)
                emit(2 * i + 1, 1, None if last else 2 * i + 2)
            return body

        def loop(eng, emit):
            body = run(emit)
            body(0, False)
            with eng.Fori(1, NCH // 2 - 1) as i:
                body(i, False)
            body(NCH // 2 - 1, True)

        block = ctx.enter_context(nc.Block())

        @block.sync
        def _(sp):
            if affine:
                for a, t in zip(affine, ga):
                    sp.dma_start(t[:], column(a)).then_inc(loaded, 16)
            if gate:
                sp.dma_start(gw[:], gate["w"]).then_inc(loaded, 16)
                if gb is not None:
                    sp.dma_start(gb[:], bcast_row(gate["b"])).then_inc(loaded, 16)
                if by_expert:
                    sp.dma_start(eb[:], gate["bias"]).then_inc(loaded, 16)
                    if not gate["by_token"]:
                        sp.wait_ge(w_copied, NCH)
                        sp.dma_start(gate["dram"], gate["we_t"][:]).then_inc(stored, 16)
                        sp.wait_ge(stored, 16)

        @block.vector
        def _(dve):
            def norm(c, par):
                src = x[:, bass.ds(c * CT, CT), :]
                for t in range(CT):
                    last = dve.bn_stats(st6[:, t, :], src[:, t, :])
                last.then_inc(vstep, 1)
                dve.wait_ge(vstep, c + 1)
                dve.sem_inc(K["passed"], 1)
                for t in range(CT):
                    last = dve.bn_aggr(mv[:, t, :], st6[:, t, :])
                last.then_inc(stats, 1)
                dve.wait_ge(rstd_ready, c + 1)
                wait(dve, turned, c - 1)
                if tokens is not None:
                    wait(dve, kept, c - 1)
                for t in range(CT):
                    last = dve.tensor_scalar(xn[:, par, t, :], src[:, t, :], mv[:, t, 0:1], rstd[:, t:t + 1],
                                             ALU.subtract, ALU.mult)
                last.then_inc(xn_ready, 1)

            norm(0, 0)

            def emit(c, par, nxt):
                if nxt is not None:
                    norm(nxt, 1 - par)
                dve.wait_ge(hi_ready, c + 1)
                dve.tensor_tensor(x_lo[:, bass.ds(c * CH, CH)], x_t[:, par],
                                  x_hi[:, bass.ds(c * CH, CH)].bitcast(F32), ALU.subtract).then_inc(lo_ready, 1)
                if not gate:
                    return
                dve.wait_ge(l_ready, c + 1)
                if gb is not None:
                    dve.tensor_tensor(lt[:], psum_l[:], gb[:].unsqueeze(1).broadcast_to([P, CT, NE]), ALU.add)\
                       .then_inc(l_read, 1)
                else:
                    dve.tensor_copy(lt[:], psum_l[:]).then_inc(l_read, 1)
                dve.wait_ge(l_read, c + 1)
                dve.tensor_copy(logits[:, bass.ds(c * CT, CT), :], lt[:])
                dve.sem_inc(K["passed"], 1)
                for t in range(CT):
                    last = dve.max(m8[:, t, :], lt[:, t, :])
                last.then_inc(gstep, 1)
                dve.wait_ge(gstep, 2 * c + 1)
                dve.tensor_copy(tops[:, bass.ds(c * CT, CT), :], m8[:])
                if topk:
                    dve.sem_inc(K["passed"], 1)
                    for t in range(CT):
                        last = dve.max_index(i8[:, t, :], m8[:, t, :], lt[:, t, :])
                    last.then_inc(gstep, 1)
                    dve.wait_ge(gstep, 2 * c + 2)
                    dve.tensor_copy(picks[:, bass.ds(c * CT, CT), :], i8[:]).then_inc(cstep, 1)
                else:
                    dve.sem_inc(gstep, 1)
                    dve.tensor_copy(picks[:, bass.ds(c * CT, CT), :], m8[:]).then_inc(cstep, 1)

            loop(dve, emit)
            if gate:
                dve.wait_ge(cstep, NCH)
                n = NCH
                o = [P, NT, NE]
                weights = gate["weights"]

                def chain(ins):
                    nonlocal n
                    n += 1
                    ins.then_inc(cstep, 1)
                    dve.wait_ge(cstep, n)

                if topk:
                    dve.tensor_tensor(d1[:], tops[:, :, 1], tops[:, :, 0], ALU.subtract).then_inc(we_ready, 1)
                    dve.wait_ge(exp_ready, 1)
                    dve.wait_ge(iota_ready, NE)
                    chain(dve.tensor_scalar(s1[:], e1[:], 1.0, None, ALU.add))
                    chain(dve.reciprocal(p0[:], s1[:]))
                    chain(dve.tensor_tensor(p1[:], p0[:], e1[:], ALU.mult))
                    it = iota[:].unsqueeze(1).broadcast_to(o)
                    for k, (w, p_) in enumerate(((w0, p0), (w1, p1))):
                        chain(dve.tensor_tensor(w[:], it, picks[:, :, k:k + 1].broadcast_to(o), ALU.is_equal))
                        chain(dve.tensor_tensor(w[:], w[:], p_[:].unsqueeze(2).broadcast_to(o), ALU.mult))
                    chain(dve.tensor_tensor(weights[:], w0[:], w1[:], ALU.add))
                else:
                    dve.tensor_tensor(w0[:], logits[:], tops[:, :, 0:1].broadcast_to(o), ALU.subtract)\
                       .then_inc(we_ready, 1)
                    dve.wait_ge(exp_ready, 1)
                    chain(dve.tensor_tensor(w0[:], logits[:], tops[:, :, 1:2].broadcast_to(o), ALU.is_ge))
                    chain(dve.tensor_tensor(w0[:], w0[:], w1[:], ALU.mult))
                    chain(dve.reduce_sum(s1[:], w0[:], AX.X))
                    chain(dve.reciprocal(p0[:], s1[:]))
                    chain(dve.tensor_tensor(weights[:], w0[:], p0[:].unsqueeze(2).broadcast_to(o), ALU.mult))
                dve.sem_inc(we_ready, 1)

        @block.gpsimd
        def _(pool):
            if gate and topk:
                for e in range(NE):
                    pool.memset(iota[:, e:e + 1], float(e)).then_inc(iota_ready, 1)

            def rstds(c):
                pool.wait_ge(stats, c + 1)
                pool.sem_inc(K["passed"], 1)
                pool.tensor_scalar(veps[:], mv[:, :, 1], EPS, None, ALU.add).then_inc(pstep, 1)
                pool.wait_ge(pstep, c + 1)
                pool.tensor_tensor(rstd[:], veps[:], K["half"][:, 0:CT], ALU.pow).then_inc(rstd_ready, 1)

            rstds(0)

            def emit(c, par, nxt):
                if nxt is not None:
                    rstds(nxt)
                if tokens is not None:
                    pool.wait_ge(xn_ready, c + 1)
                    pool.sem_inc(K["passed"], 1)
                    pool.tensor_copy(tokens[:, bass.ds(c * CT, CT), :], xn[:, par]).then_inc(kept, 1)

            loop(pool, emit)

        @block.scalar
        def _(act):
            if n_loads:
                act.wait_ge(loaded, 16 * n_loads)

            def emit(c, par, nxt):
                act.wait_ge(turned, c + 1)
                wait(act, lo_ready, c - 1)
                act.activation(x_t[:, par], psum_t[par][:], ACT.Identity, scale=ga[0][:] if ga else 1.0,
                               bias=ga[1][:] if ga else 0.0).then_inc(x_t_ready, 1)
                act.wait_ge(x_t_ready, c + 1)
                act.sem_inc(K["passed"], 1)
                act.activation(x_hi[:, bass.ds(c * CH, CH)], x_t[:, par], ACT.Identity).then_inc(hi_ready, 1)

            loop(act, emit)
            if gate:
                act.wait_ge(we_ready, 1)
                if topk:
                    act.activation(e1[:], d1[:], ACT.Exp).then_inc(exp_ready, 1)
                else:
                    act.activation(w1[:], w0[:], ACT.Exp).then_inc(exp_ready, 1)
                if by_expert:
                    for c in range(NCH):
                        act.wait_ge(w_turned, c + 1)
                        act.activation(gate["we_t"][:, c * CH:(c + 1) * CH], psum_w[c % 2][0:NE, :], ACT.Identity)\
                           .then_inc(w_copied, 1)
                        act.wait_ge(b_done, c + 1)
                        act.activation(gate["acc"][:, c * CH:(c + 1) * CH], psum_b[c % 2][:], ACT.Identity)\
                           .then_inc(b_copied, 1)

        @block.tensor
        def _(pe):
            if n_loads:
                pe.wait_ge(loaded, 16 * n_loads)

            def emit(c, par, nxt):
                pe.wait_ge(xn_ready, c + 1)
                wait(pe, x_t_ready, c - 1)
                for t in range(CT):
                    last = pe.transpose(psum_t[par][:, t * P:(t + 1) * P], xn[:, par, t, :], K["ident"][:])
                last.then_inc(turned, 1)
                if gate:
                    pe.wait_ge(x_t_ready, c + 1)
                    wait(pe, l_read, c)
                    for t in range(CT):
                        last = pe.matmul(psum_l[:, t, :], x_t[:, par, t * P:(t + 1) * P], gw[:],
                                         start=True, stop=True)
                    last.then_inc(l_ready, 1)

            loop(pe, emit)
            if gate and by_expert:
                pe.wait_ge(we_ready, 2)
                for c in range(NCH):
                    if c >= 2:
                        pe.wait_ge(w_copied, c - 1)
                    for t in range(CT):
                        last = pe.transpose(psum_w[c % 2][0:NE, t * P:(t + 1) * P], gate["weights"][:, c * CT + t, :],
                                            K["ident"][:])
                    last.then_inc(w_turned, 1)
                    pe.wait_ge(w_copied, c + 1)
                    if c >= 2:
                        pe.wait_ge(b_copied, c - 1)
                    if gate["by_token"]:
                        for t in range(CT):
                            tok = c * CH + t * P
                            last = pe.matmul(psum_b[c % 2][:, t * P:(t + 1) * P], gate["we_t"][:, tok:tok + P], eb[:],
                                             start=True, stop=True)
                        last.then_inc(b_done, 1)
                    else:
                        pe.matmul(psum_b[c % 2][:], eb[:], gate["we_t"][:, c * CH:(c + 1) * CH],
                                  start=True, stop=True).then_inc(b_done, 1)


@phase
def experts(nc, name, K, x_hi, x_lo, acc, *, kind, weights, biases, last_bias=None, we_dram=None):
    glu = kind == "glu"
    E_, _, WB = weights.shape
    BLK = WB // P
    gated = we_dram is not None
    N = E_ * NCH
    PER = 2 * NCH if gated else 2
    HB = 2 if glu else 4
    with ExitStack() as ctx:
        def sb(nm, shape, dt=F32):
            return ctx.enter_context(nc.sbuf_tensor(f"{name}_{nm}", shape, dt))

        def sem(nm):
            return nc.alloc_semaphore(f"{name}_{nm}")

        WBUF = 2 if gated else 1
        raw = sb("raw", [P, WBUF, WB])
        w_hi, w_lo = sb("w_hi", [P, WBUF, WB], F32R), sb("w_lo", [P, WBUF, WB], F32R)
        bias = sb("bias", [P, biases.shape[1]])
        lb = sb("lb", [P, 1]) if last_bias is not None else None
        BC = biases.shape[1] // E_
        if glu:
            a_s, z = sb("a_s", [P, 2, CH]), sb("z", [P, 2, CH])
            z_hi, z_lo = sb("z_hi", [P, 2, 2, CH], F32R), sb("z_lo", [P, 2, 2, CH], F32R)
        h = sb("h", [P, HB, CH])
        h_hi, h_lo = sb("h_hi", [P, 2, HB, CH], F32R), sb("h_lo", [P, 2, HB, CH], F32R)
        wrow = sb("wrow", [P, 2, CH]) if gated else None
        tmp = sb("tmp", [P, 2, CH]) if gated else None
        NF = 4
        psum_f = [ctx.enter_context(nc.psum_tensor(f"{name}_f{i}", [P, CH], F32)) for i in range(NF)]
        psum_g = [ctx.enter_context(nc.psum_tensor(f"{name}_g{i}", [P, CH], F32)) for i in range(2)] if glu else None
        psum_y = [ctx.enter_context(nc.psum_tensor(f"{name}_y{i}", [P, CH], F32)) for i in range(2)]

        loaded, w_loaded = sem("loaded"), [sem(f"w_loaded{i}") for i in range(WBUF)]
        w_high, w_split = sem("w_high"), sem("w_split")
        first_done = sem("first_done")
        a_ready, z_ready, z_high, z_split = sem("a_ready"), sem("z_ready"), sem("z_high"), sem("z_split")
        g_done = sem("g_done")
        h_ready, h_high, h_split = sem("h_ready"), sem("h_high"), sem("h_split")
        y_done, y_read, added = sem("y_done"), sem("y_read"), sem("added")
        row_loaded = [sem(f"row_loaded{i}") for i in range(2)] if gated else None
        PIECES = 5 if BLK == 10 else 4
        PW = WB // PIECES

        def run(eng, emit):
            def at_of(i, j):
                def at(k):
                    jj = j + k
                    if gated:
                        return PER * i + jj, 2 * i + jj // NCH, jj % NCH, jj % PER
                    return PER * i + jj, 0, PER * i + jj, jj % PER
                return at
            reps = N // PER
            emit(at_of(0, -1))
            for j in range(PER):
                emit(at_of(0, j))
            if reps > 2:
                with eng.Fori(1, reps - 1) as i:
                    for j in range(PER):
                        emit(at_of(i, j))
            for j in range(PER + 1):
                emit(at_of(reps - 1, j))

        def inside(n):
            return not isinstance(n, int) or 0 <= n < N

        block = ctx.enter_context(nc.Block())

        @block.sync
        def _(sp):
            sp.dma_start(bias[:], biases).then_inc(loaded, 16)
            if lb is not None:
                sp.dma_start(lb[:], column(last_bias)).then_inc(loaded, 16)

            def load(e, par):
                wait(sp, w_split, (e - 1) * PIECES)
                sp.dma_start(raw[:, par, :], weights[bass.ds(e, 1), :, :].rearrange("a p n -> p (a n)"))\
                  .then_inc(w_loaded[par], 16)

            load(0, 0)
            if gated:
                load(1, 1)

            def emit(at):
                n, e, c, pos = at(1)
                if gated and inside(n):
                    wait(sp, y_read, n - 1)
                    sp.dma_start(wrow[:, pos % 2, :],
                                 we_dram[bass.ds(e, 1), c * CH:(c + 1) * CH].broadcast_to([P, CH]))\
                      .then_inc(row_loaded[pos % 2], 16)
                n, e, c, pos = at(0)
                if gated and inside(n) and c == NCH - 1 and not (isinstance(e, int) and e + 2 >= E_):
                    load(e + 2, (pos // NCH) % 2)

            run(sp, emit)

        @block.tensor
        def _(pe):
            pe.wait_ge(loaded, 16 if lb is None else 32)

            def triple(dst, wpar, blk, hi, lo, start, stop):
                cols = slice(blk * P, (blk + 1) * P)
                pe.matmul(dst, w_hi[:, wpar, cols], hi, start=start, stop=False)
                pe.matmul(dst, w_lo[:, wpar, cols], hi, start=False, stop=False)
                return pe.matmul(dst, w_hi[:, wpar, cols], lo, start=False, stop=stop)

            def first(n, e, c, pos):
                wpar = (pos // NCH) % 2 if gated else 0
                if isinstance(c, int) and c == 0:
                    pe.wait_ge(w_split, (e + 1) * PIECES)
                xs = bass.ds(c * CH, CH)
                for i in range(NF):
                    if glu:
                        wait(pe, a_ready if i % 2 == 0 else z_ready, 2 * n - 1 + i // 2)
                    else:
                        wait(pe, h_ready, 4 * (n - 1) + i + 1)
                    triple(psum_f[i][:], wpar, i, x_hi[:, xs], x_lo[:, xs], True, True).then_inc(first_done, 1)

            def middle(n, e, c, pos):
                wpar = (pos // NCH) % 2
                for g in range(2):
                    wait(pe, h_ready, 2 * n - 1 + g)
                    for j in range(2):
                        pe.wait_ge(z_split, 2 * n + 1 + j)
                        last = triple(psum_g[g][:], wpar, 4 + 2 * j + g, z_hi[:, pos % 2, j], z_lo[:, pos % 2, j], j == 0, j == 1)
                    last.then_inc(g_done, 1)

            def final(n, e, c, pos):
                wpar = (pos // NCH) % 2 if gated else 0
                wait(pe, y_read, n - 1)
                for j in range(HB):
                    pe.wait_ge(h_split, HB * n + j + 1)
                    last = triple(psum_y[pos % 2][:], wpar, BLK - HB + j, h_hi[:, pos % 2, j], h_lo[:, pos % 2, j],
                                  j == 0, j == HB - 1)
                last.then_inc(y_done, 1)

            def emit(at):
                n, e, c, pos = at(1)
                if inside(n):
                    first(n, e, c, pos)
                if glu:
                    n, e, c, pos = at(-1)
                    if inside(n):
                        final(n, e, c, pos)
                    n, e, c, pos = at(0)
                    if inside(n):
                        middle(n, e, c, pos)
                else:
                    n, e, c, pos = at(0)
                    if inside(n):
                        final(n, e, c, pos)

            run(pe, emit)

        @block.scalar
        def _(act):
            act.wait_ge(loaded, 16 if lb is None else 32)

            def col(e, k):
                if isinstance(e, int):
                    return bias[:, e * BC + k:e * BC + k + 1]
                return bias[:, bass.ds(e * BC + k, 1)]

            def emit(at):
                n, e, c, pos = at(1)
                if inside(n) and glu:
                    for j in range(2):
                        act.wait_ge(first_done, 4 * n + 2 * j + 1)
                        wait(act, z_ready, 2 * n - 1 + j)
                        act.sem_inc(K["passed"], 1)
                        act.activation(a_s[:, j], psum_f[2 * j][:], ACT.Identity, bias=col(e, j)).then_inc(a_ready, 1)
                if inside(n) and not glu:
                    for j in range(4):
                        act.wait_ge(first_done, 4 * n + j + 1)
                        wait(act, h_split, 4 * (n - 1) + j + 1)
                        act.sem_inc(K["passed"], 1)
                        act.activation(h[:, j], psum_f[j][:], ACT.Gelu, bias=col(e, j)).then_inc(h_ready, 1)
                n, e, c, pos = at(0)
                if inside(n) and glu:
                    for g in range(2):
                        act.wait_ge(g_done, 2 * n + 1 + g)
                        wait(act, h_split, 2 * n - 1 + g)
                        act.sem_inc(K["passed"], 1)
                        act.activation(h[:, g], psum_g[g][:], ACT.Silu, bias=col(e, 4 + g)).then_inc(h_ready, 1)
                        act.wait_ge(h_ready, 2 * n + 1 + g)
                        wait(act, y_done, n - 1)
                        act.activation(h_hi[:, pos % 2, g], h[:, g], ACT.Identity).then_inc(h_high, 1)

            run(act, emit)

        @block.vector
        def _(dve):
            dve.wait_ge(loaded, 16 if lb is None else 32)

            def col(e, k):
                if isinstance(e, int):
                    return bias[:, e * BC + k:e * BC + k + 1]
                return bias[:, bass.ds(e * BC + k, 1)]

            def outputs(n, e, c, pos):
                dve.wait_ge(y_done, n + 1)
                if gated:
                    dve.wait_ge(row_loaded[pos % 2], row_count(n, pos))
                    wait(dve, added, n - 1)
                    dve.tensor_tensor(tmp[:, pos % 2], psum_y[pos % 2][:], wrow[:, pos % 2, :], ALU.mult)\
                       .then_inc(y_read, 1)
                else:
                    dve.tensor_scalar(acc[:, bass.ds(c * CH, CH)], psum_y[pos % 2][:], lb[:], None, ALU.add)\
                       .then_inc(y_read, 1)

            def row_count(n, pos):
                return 8 * n + (16 if pos % 2 == 0 else 8)

            def emit(at):
                n, e, c, pos = at(-1 if glu else 0)
                if inside(n):
                    outputs(n, e, c, pos)
                n, e, c, pos = at(1)
                if inside(n) and glu:
                    for j in range(2):
                        dve.wait_ge(a_ready, 2 * n + 1 + j)
                        dve.wait_ge(first_done, 4 * n + 2 * j + 2)
                        dve.scalar_tensor_tensor(out=z[:, j], in0=psum_f[2 * j + 1][:], scalar=col(e, 2 + j),
                                                 in1=a_s[:, j], op0=ALU.add, op1=ALU.mult).then_inc(z_ready, 1)
                        dve.wait_ge(z_ready, 2 * n + 1 + j)
                        wait(dve, g_done, 2 * (n - 1))
                        dve.tensor_copy(z_hi[:, pos % 2, j], z[:, j]).then_inc(z_high, 1)
                        dve.wait_ge(z_high, 2 * n + 1 + j)
                        dve.tensor_tensor(z_lo[:, pos % 2, j], z[:, j], z_hi[:, pos % 2, j].bitcast(F32), ALU.subtract)\
                           .then_inc(z_split, 1)
                if inside(n) and not glu:
                    for j in range(4):
                        dve.wait_ge(h_ready, 4 * n + j + 1)
                        wait(dve, y_done, n - 1)
                        dve.tensor_copy(h_hi[:, pos % 2, j], h[:, j]).then_inc(h_high, 1)
                        dve.wait_ge(h_high, 4 * n + j + 1)
                        dve.tensor_tensor(h_lo[:, pos % 2, j], h[:, j], h_hi[:, pos % 2, j].bitcast(F32), ALU.subtract)\
                           .then_inc(h_split, 1)
                n, e, c, pos = at(0)
                if inside(n) and glu:
                    for g in range(2):
                        dve.wait_ge(h_high, 2 * n + 1 + g)
                        dve.tensor_tensor(h_lo[:, pos % 2, g], h[:, g], h_hi[:, pos % 2, g].bitcast(F32), ALU.subtract)\
                           .then_inc(h_split, 1)

            run(dve, emit)

        @block.gpsimd
        def _(pool):
            def split(e, par, i):
                if i == 0:
                    cnt = 8 * e + (16 if par == 0 else 8) if gated else 16
                    pool.wait_ge(w_loaded[par if gated else 0], cnt)
                    wait(pool, y_done, NCH * (e - 1))
                    pool.sem_inc(K["passed"], 1)
                cols = slice(i * PW, (i + 1) * PW)
                pool.tensor_copy(w_hi[:, par, cols], raw[:, par, cols]).then_inc(w_high, 1)
                pool.wait_ge(w_high, e * PIECES + i + 1)
                pool.tensor_tensor(w_lo[:, par, cols], raw[:, par, cols], w_hi[:, par, cols].bitcast(F32),
                                   ALU.subtract).then_inc(w_split, 1)

            for i in range(PIECES):
                split(0, 0, i)

            def emit(at):
                n, e, c, pos = at(-1 if glu else 0)
                if gated and inside(n):
                    pool.wait_ge(y_read, n + 1)
                    pool.tensor_tensor(acc[:, bass.ds(c * CH, CH)], tmp[:, pos % 2], acc[:, bass.ds(c * CH, CH)],
                                       ALU.add).then_inc(added, 1)
                n, e, c, pos = at(0)
                if gated and inside(n) and 2 <= c < 2 + PIECES and not (isinstance(e, int) and e + 1 >= E_):
                    split(e + 1, (pos // NCH + 1) % 2, c - 2)

            run(pool, emit)


@phase
def add_turned(nc, name, K, acc, base, out, more=()):
    with ExitStack() as ctx:
        def sem(nm):
            return nc.alloc_semaphore(f"{name}_{nm}")

        banks = [ctx.enter_context(nc.psum_tensor(f"{name}_p{i}", [P, CT, P], F32)) for i in range(4)]
        turned, summed, added = sem("turned"), sem("summed"), sem("added")
        block = ctx.enter_context(nc.Block())

        @block.tensor
        def _(pe):
            for c in range(NCH):
                if c >= 4:
                    pe.wait_ge(added, c - 3)
                for t in range(CT):
                    last = pe.transpose(banks[c % 4][:, t, :], acc[:, (c * CT + t) * P:(c * CT + t + 1) * P],
                                        K["ident"][:])
                last.then_inc(turned, 1)

        @block.gpsimd
        def _(pool):
            for k, other in enumerate((base, *more[1:]) if more else ()):
                for c in range(NCH):
                    tiles = slice(c * CT, (c + 1) * CT)
                    if k:
                        pool.wait_ge(summed, (k - 1) * NCH + c + 1)
                    pool.tensor_tensor(more[0][:, tiles, :], more[0][:, tiles, :], other[:, tiles, :], ALU.add)\
                        .then_inc(summed, 1)

        @block.vector
        def _(dve):
            for c in range(NCH):
                tiles = slice(c * CT, (c + 1) * CT)
                if more:
                    dve.wait_ge(summed, (len(more) - 1) * NCH + c + 1)
                dve.wait_ge(turned, c + 1)
                dve.tensor_tensor(out[:, tiles, :], banks[c % 4][:], (more[0] if more else base)[:, tiles, :],
                                  ALU.add).then_inc(added, 1)
            dve.wait_ge(added, NCH)


@phase
def experts_normed(nc, name, K, x_hi, x_lo, tokens, route, acc, x, *, weights, biases, out_biases, gains, eps):
    N = NE * NCH
    PER = 2 * NCH
    with ExitStack() as ctx:
        def sb(nm, shape, dt=F32):
            return ctx.enter_context(nc.sbuf_tensor(f"{name}_{nm}", shape, dt))

        def sem(nm):
            return nc.alloc_semaphore(f"{name}_{nm}")

        raw = sb("raw", [P, 2, 4 * P])
        w_hi, w_lo = sb("w_hi", [P, 2, 2 * P], F32R), sb("w_lo", [P, 2, 2 * P], F32R)
        bias = sb("bias", [P, 2 * NE])
        b2 = sb("b2", [P, NE, P])
        gain = sb("gain", [P, NE, P])
        h = sb("h", [P, 2, 2, CH])
        xb = sb("xb", [P, 2, CT, P])
        y = sb("y", [P, 2, CT, P])
        st6, mv = sb("st6", [P, CT, 6]), sb("mv", [P, 2, CT, 2])
        veps, rstd, rw = sb("veps", [P, CT]), sb("rstd", [P, CT]), sb("rw", [P, 2, CT])
        u, tmp = sb("u", [P, CT, P]), sb("tmp", [P, 2, CT, P])
        psum_f = [ctx.enter_context(nc.psum_tensor(f"{name}_f{i}", [P, CH], F32)) for i in range(4)]
        psum_o = [ctx.enter_context(nc.psum_tensor(f"{name}_o{i}", [P, CT, P], F32)) for i in range(2)]

        loaded, w_loaded = sem("loaded"), [sem(f"w_loaded{i}") for i in range(2)]
        w_high, w_split = sem("w_high"), sem("w_split")
        first_done, h_ready, o_done = sem("first_done"), sem("h_ready"), sem("o_done")
        xb_ready, y_ready, stepped, stats = sem("xb_ready"), sem("y_ready"), sem("stepped"), sem("stats")
        pstep, rw_ready, u_ready, tmp_ready, added = (
            sem("pstep"), sem("rw_ready"), sem("u_ready"), sem("tmp_ready"), sem("added"))
        finished = sem("finished")

        def run(eng, emit):
            def at_of(i, j):
                def at(k):
                    jj = j + k
                    return PER * i + jj, 2 * i + jj // NCH, jj % NCH, jj % PER
                return at
            for j in range(-1, PER):
                emit(at_of(0, j))
            with eng.Fori(1, N // PER - 1) as i:
                for j in range(PER):
                    emit(at_of(i, j))
            for j in range(PER + 1):
                emit(at_of(N // PER - 1, j))

        def inside(n):
            return not isinstance(n, int) or 0 <= n < N

        block = ctx.enter_context(nc.Block())

        @block.sync
        def _(sp):
            sp.dma_start(bias[:], biases).then_inc(loaded, 16)
            sp.dma_start(b2[:].rearrange("p e d -> p (e d)"), bcast_row(out_biases)).then_inc(loaded, 16)
            sp.dma_start(gain[:].rearrange("p e d -> p (e d)"), bcast_row(gains)).then_inc(loaded, 16)

            def load(e, par):
                wait(sp, o_done, NCH * (e - 1))
                wait(sp, w_split, e - 1)
                sp.dma_start(raw[:, par, :], weights[bass.ds(e, 1), :, :].rearrange("a p n -> p (a n)"))\
                  .then_inc(w_loaded[par], 16)

            load(0, 0)
            load(1, 1)

            def emit(at):
                n, e, c, pos = at(0)
                if inside(n) and c == NCH - 1 and not (isinstance(e, int) and e + 2 >= NE):
                    load(e + 2, (pos // NCH) % 2)

            run(sp, emit)

        @block.tensor
        def _(pe):
            pe.wait_ge(loaded, 48)

            def emit(at):
                n, e, c, pos = at(1)
                if inside(n):
                    par = (pos // NCH) % 2
                    if c == 0:
                        pe.wait_ge(w_split, e + 1)
                    for j in range(2):
                        dst = psum_f[2 * (pos % 2) + j][:]
                        wait(pe, h_ready, 2 * (n - 2) + j + 1)
                        cols, xs = slice(j * P, (j + 1) * P), slice(c * CH, (c + 1) * CH)
                        pe.matmul(dst, w_hi[:, par, cols], x_hi[:, xs], start=True, stop=False)
                        pe.matmul(dst, w_lo[:, par, cols], x_hi[:, xs], start=False, stop=False)
                        pe.matmul(dst, w_hi[:, par, cols], x_lo[:, xs], start=False, stop=True)\
                          .then_inc(first_done, 1)
                n, e, c, pos = at(0)
                if inside(n):
                    par = (pos // NCH) % 2
                    pe.wait_ge(h_ready, 2 * n + 2)
                    wait(pe, y_ready, n - 1)
                    for t in range(CT):
                        for j in range(2):
                            last = pe.matmul(psum_o[pos % 2][:, t, :], h[:, pos % 2, j, t * P:(t + 1) * P],
                                             raw[:, par, (2 + j) * P:(3 + j) * P], start=j == 0, stop=j == 1)
                    last.then_inc(o_done, 1)

            run(pe, emit)

        @block.scalar
        def _(act):
            act.wait_ge(loaded, 48)

            def emit(at):
                n, e, c, pos = at(1)
                if inside(n):
                    for j in range(2):
                        act.wait_ge(first_done, 2 * n + j + 1)
                        wait(act, o_done, n - 1)
                        col = bias[:, 2 * e + j:2 * e + j + 1] if isinstance(e, int) else bias[:, bass.ds(2 * e + j, 1)]
                        act.sem_inc(K["passed"], 1)
                        act.activation(h[:, pos % 2, j], psum_f[2 * (pos % 2) + j][:], ACT.Gelu, bias=col)\
                           .then_inc(h_ready, 1)

            run(act, emit)

        @block.vector
        def _(dve):
            dve.wait_ge(loaded, 48)

            def emit(at):
                n, e, c, pos = at(0)
                if inside(n):
                    par = pos % 2
                    dve.wait_ge(o_done, n + 1)
                    dve.wait_ge(xb_ready, n + 1)
                    dve.tensor_tensor(y[:, par], psum_o[par][:], xb[:, par], ALU.add).then_inc(y_ready, 1)
                    dve.wait_ge(y_ready, n + 1)
                    dve.sem_inc(K["passed"], 1)
                    for t in range(CT):
                        last = dve.bn_stats(st6[:, t, :], y[:, par, t, :])
                    last.then_inc(stepped, 1)
                    dve.wait_ge(stepped, n + 1)
                    wait(dve, rw_ready, n - 1)
                    dve.sem_inc(K["passed"], 1)
                    for t in range(CT):
                        last = dve.bn_aggr(mv[:, par, t, :], st6[:, t, :])
                    last.then_inc(stats, 1)
                n, e, c, pos = at(-1)
                if inside(n):
                    par = pos % 2
                    dve.wait_ge(rw_ready, n + 1)
                    wait(dve, tmp_ready, n)
                    for t in range(CT):
                        last = dve.tensor_scalar(u[:, t, :], y[:, par, t, :], mv[:, par, t, 0:1], rw[:, par, t:t + 1],
                                                 ALU.subtract, ALU.mult)
                    last.then_inc(u_ready, 1)
                    dve.wait_ge(u_ready, n + 1)
                    wait(dve, added, n - 1)
                    g = gain[:, e:e + 1, :] if isinstance(e, int) else gain[:, bass.ds(e, 1), :]
                    dve.tensor_tensor(tmp[:, par], u[:], g.broadcast_to([P, CT, P]), ALU.mult).then_inc(tmp_ready, 1)

            run(dve, emit)
            dve.wait_ge(added, N)
            dve.tensor_tensor(x[:], x[:], acc[:], ALU.add).then_inc(finished, 1)
            dve.wait_ge(finished, 1)

        @block.gpsimd
        def _(pool):
            pool.wait_ge(loaded, 48)

            def split(e, par):
                pool.wait_ge(w_loaded[par], 8 * e + (16 if par == 0 else 8))
                wait(pool, first_done, 2 * NCH * (e - 1))
                pool.sem_inc(K["passed"], 1)
                pool.tensor_copy(w_hi[:, par], raw[:, par, 0:2 * P]).then_inc(w_high, 1)
                pool.wait_ge(w_high, e + 1)
                pool.tensor_tensor(w_lo[:, par], raw[:, par, 0:2 * P], w_hi[:, par].bitcast(F32), ALU.subtract)\
                    .then_inc(w_split, 1)

            split(0, 0)

            def emit(at):
                n, e, c, pos = at(1)
                if inside(n):
                    wait(pool, y_ready, n - 1)
                    pool.sem_inc(K["passed"], 1)
                    b = b2[:, e:e + 1, :] if isinstance(e, int) else b2[:, bass.ds(e, 1), :]
                    pool.tensor_tensor(xb[:, pos % 2], tokens[:, c * CT:(c + 1) * CT, :],
                                       b.broadcast_to([P, CT, P]), ALU.add).then_inc(xb_ready, 1)
                n, e, c, pos = at(0)
                if inside(n):
                    par = pos % 2
                    pool.wait_ge(stats, n + 1)
                    pool.sem_inc(K["passed"], 1)
                    pool.tensor_scalar(veps[:], mv[:, par, :, 1], eps, None, ALU.add).then_inc(pstep, 1)
                    pool.wait_ge(pstep, 2 * n + 1)
                    pool.tensor_tensor(rstd[:], veps[:], K["half"][:, 0:CT], ALU.pow).then_inc(pstep, 1)
                    pool.wait_ge(pstep, 2 * n + 2)
                    wait(pool, u_ready, n - 1)
                    pool.sem_inc(K["passed"], 1)
                    w = route[:, c * CT:(c + 1) * CT, e:e + 1] if isinstance(e, int) else \
                        route[:, c * CT:(c + 1) * CT, bass.ds(e, 1)]
                    pool.tensor_tensor(rw[:, par].unsqueeze(2), rstd[:].unsqueeze(2), w, ALU.mult)\
                        .then_inc(rw_ready, 1)
                n, e, c, pos = at(-1)
                if inside(n):
                    pool.wait_ge(tmp_ready, n + 1)
                    a = acc[:, c * CT:(c + 1) * CT, :]
                    pool.tensor_tensor(a, tmp[:, pos % 2], a, ALU.add).then_inc(added, 1)
                n, e, c, pos = at(0)
                if inside(n) and c == 2 and not (isinstance(e, int) and e + 1 >= NE):
                    split(e + 1, (pos // NCH + 1) % 2)

            run(pool, emit)


@phase
def ternary_mlp(nc, name, K, x, *, w1, w2, b1, b2):
    F = 512
    FB = F // P
    QB = 127.0
    ROUND = 1.5 * 2.0 ** 23
    N = NT
    with ExitStack() as ctx:
        def sb(nm, shape, dt=F32):
            return ctx.enter_context(nc.sbuf_tensor(f"{name}_{nm}", shape, dt))

        def sem(nm):
            return nc.alloc_semaphore(f"{name}_{nm}")

        wf = [sb("w1f", [P, F]), sb("w2f", [P, F])]
        wt = [sb("w1t", [P, F], BF16), sb("w2t", [P, F], BF16)]
        wa, wsum = sb("wa", [P, 2]), sb("wsum", [P, 2])
        ws, wr, wq = sb("ws", [P, 2]), sb("wr", [P, 2]), sb("wq", [P, 2])
        ones = sb("ones", [P, P])
        b1b, b2b = sb("b1b", [P, F]), sb("b2b", [P, P])
        st6, mv = sb("st6", [P, 6]), sb("mv", [P, 2])
        veps, rstd = sb("veps", [P, 1]), sb("rstd", [P, 1])
        xn, xi, xi2 = sb("xn", [P, P]), sb("xi", [P, P]), sb("xi2", [P, P])
        xq = sb("xq", [P, 2, P], BF16)
        xq_t = sb("xq_t", [P, 2, P], BF16)
        xa, xc, xr, xs = sb("xa", [P, 1]), sb("xc", [P, 1]), sb("xr", [P, 1]), sb("xs", [P, 1])
        xd = sb("xd", [P, 3])
        hb, h = sb("hb", [P, 2, F]), sb("h", [P, 2, F])
        hi1, hi2, hq = sb("hi1", [P, F]), sb("hi2", [P, F]), sb("hq", [P, 2, F], BF16)
        ha, hc, hr, hs = sb("ha", [P, 1]), sb("hc", [P, 1]), sb("hr", [P, 1]), sb("hs", [P, 1])
        hd = sb("hd", [P, 3])
        hq_t = sb("hq_t", [P, 2, FB, P], BF16)
        o1 = sb("o1", [P, P])
        psum_w = ctx.enter_context(nc.psum_tensor(f"{name}_pw", [P, 2], F32))
        psum_x = ctx.enter_context(nc.psum_tensor(f"{name}_px", [P, P], BF16))
        psum_h = [ctx.enter_context(nc.psum_tensor(f"{name}_ph{i}", [P, F], F32)) for i in range(2)]
        psum_t = [ctx.enter_context(nc.psum_tensor(f"{name}_pt{i}", [P, FB, P], BF16)) for i in range(2)]
        psum_o = ctx.enter_context(nc.psum_tensor(f"{name}_po", [P, P], F32))

        loaded, wstep, wsummed, w_ready = sem("loaded"), sem("wstep"), sem("wsummed"), sem("w_ready")
        lstep, stats, pstep, rstd_ready = sem("lstep"), sem("stats"), sem("pstep"), sem("rstd_ready")
        xq_ready, x_turned, xq_t_ready = sem("xq_ready"), sem("x_turned"), sem("xq_t_ready")
        h_done, hb_ready, h_ready = sem("h_done"), sem("hb_ready"), sem("h_ready")
        hstep, hq_ready, h_turned, hq_t_ready = sem("hstep"), sem("hq_ready"), sem("h_turned"), sem("hq_t_ready")
        o_done, ostep = sem("o_done"), sem("ostep")
        LS, HS, OS = 8, 7, 3

        def run(eng, emit):
            def at_of(base, j):
                return lambda k: (base + j + k, (j + k) % 2)
            for j in range(-2, 2):
                emit(at_of(0, j))
            with eng.Fori(1, N // 2 - 1) as i:
                for j in range(2):
                    emit(at_of(2 * i, j))
            for j in range(2):
                emit(at_of(N - 2, j))

        def inside(n):
            return not isinstance(n, int) or 0 <= n < N

        block = ctx.enter_context(nc.Block())

        @block.sync
        def _(sp):
            for dst, src in ((wf[0], w1), (wf[1], w2), (b1b, bcast_row(b1)), (b2b, bcast_row(b2))):
                sp.dma_start(dst[:], src).then_inc(loaded, 16)

        @block.vector
        def _(dve):
            dve.memset(ones[:], 1.0).then_inc(wstep, 1)
            dve.wait_ge(loaded, 64)
            nw = [1]

            def link(ins):
                nw[0] += 1
                ins.then_inc(wstep, 1)
                dve.wait_ge(wstep, nw[0])

            for i in range(2):
                link(dve.tensor_reduce(wa[:, i:i + 1], wf[i][:], AX.X, ALU.add, apply_absolute_value=True))
            dve.wait_ge(wsummed, 1)
            link(dve.tensor_scalar(ws[:], psum_w[:], 1.0 / (F * P), EPS, ALU.mult, ALU.max))
            link(dve.reciprocal(wr[:], ws[:]))
            link(dve.tensor_scalar(wq[:], ws[:], 1.0 / QB, None, ALU.mult))
            for i in range(2):
                link(dve.tensor_scalar(wf[i][:], wf[i][:], wr[:, i:i + 1], ROUND, ALU.mult, ALU.add))
                link(dve.tensor_scalar(wf[i][:], wf[i][:], ROUND, 1.0, ALU.subtract, ALU.min))
                link(dve.tensor_scalar(wt[i][:], wf[i][:], -1.0, None, ALU.max))
            dve.sem_inc(w_ready, 1)

            def quantise(src, a, c, r, s, i1, i2, q, sem_, at0):
                k = [0]

                def step(ins):
                    k[0] += 1
                    ins.then_inc(sem_, 1)
                    dve.wait_ge(sem_, at0 + k[0])

                step(dve.tensor_reduce(a[:], src, AX.X, ALU.max, apply_absolute_value=True))
                step(dve.tensor_scalar(c[:], a[:], EPS, None, ALU.max))
                step(dve.reciprocal(r[:], c[:]))
                step(dve.tensor_scalar(s[:], r[:], QB, None, ALU.mult))
                step(dve.tensor_scalar(i1[:], src, s[:], ROUND, ALU.mult, ALU.add))
                step(dve.tensor_scalar(i2[:], i1[:], ROUND, QB, ALU.subtract, ALU.min))
                return dve.tensor_scalar(q, i2[:], -QB - 1.0, None, ALU.max)

            def scale_of(dst, slot, c, i):
                return dve.tensor_tensor(dst[:, slot:slot + 1], c[:], wq[:, i:i + 1], ALU.mult)

            def emit(at):
                n, par = at(2)
                if inside(n):
                    src = x[:, bass.ds(n, 1), :].rearrange("p a d -> p (a d)")
                    dve.bn_stats(st6[:], src).then_inc(lstep, 1)
                    dve.wait_ge(lstep, LS * n + 1)
                    dve.sem_inc(K["passed"], 1)
                    dve.bn_aggr(mv[:], st6[:]).then_inc(stats, 1)
                m, pm = at(1)
                if inside(m):
                    dve.wait_ge(h_done, m + 1)
                    wait(dve, h_ready, m - 1)
                    dve.scalar_tensor_tensor(out=hb[:, pm], in0=psum_h[pm][:], scalar=xd[:, pm:pm + 1], in1=b1b[:],
                                             op0=ALU.mult, op1=ALU.add).then_inc(hb_ready, 1)
                if inside(n):
                    dve.wait_ge(rstd_ready, n + 1)
                    dve.tensor_scalar(xn[:], src, mv[:, 0:1], rstd[:], ALU.subtract, ALU.mult).then_inc(lstep, 1)
                    dve.wait_ge(lstep, LS * n + 2)
                    wait(dve, x_turned, n - 1)
                    quantise(xn[:], xa, xc, xr, xs, xi, xi2, xq[:, par], lstep, LS * n + 2).then_inc(xq_ready, 1)
                    wait(dve, hb_ready, n - 1)
                    scale_of(xd, par, xc, 0)
                if inside(m):
                    dve.wait_ge(h_ready, m + 1)
                    wait(dve, h_turned, m - 1)
                    quantise(h[:, pm], ha, hc, hr, hs, hi1, hi2, hq[:, pm], hstep, HS * m).then_inc(hq_ready, 1)
                    wait(dve, ostep, OS * (m - 1))
                    scale_of(hd, pm, hc, 1).then_inc(hstep, 1)
                n, par = at(0)
                if inside(n):
                    dve.wait_ge(o_done, n + 1)
                    dve.wait_ge(hstep, HS * n + 7)
                    wait(dve, ostep, OS * n)
                    dst = x[:, bass.ds(n, 1), :].rearrange("p a d -> p (a d)")
                    dve.scalar_tensor_tensor(out=o1[:], in0=psum_o[:], scalar=hd[:, par:par + 1], in1=b2b[:],
                                             op0=ALU.mult, op1=ALU.add).then_inc(ostep, 1)
                    dve.wait_ge(ostep, OS * n + 1)
                    dve.tensor_tensor(dst, o1[:], dst, ALU.add).then_inc(ostep, 2)

            run(dve, emit)
            dve.wait_ge(ostep, OS * N)

        @block.gpsimd
        def _(pool):
            def emit(at):
                n, par = at(2)
                if inside(n):
                    pool.wait_ge(stats, n + 1)
                    pool.sem_inc(K["passed"], 1)
                    pool.tensor_scalar(veps[:], mv[:, 1:2], EPS, None, ALU.add).then_inc(pstep, 1)
                    pool.wait_ge(pstep, n + 1)
                    pool.tensor_tensor(rstd[:], veps[:], K["half"][:, 0:1], ALU.pow).then_inc(rstd_ready, 1)

            run(pool, emit)

        @block.tensor
        def _(pe):
            pe.wait_ge(wstep, 3)
            pe.matmul(psum_w[:], ones[:], wa[:], start=True, stop=True).then_inc(wsummed, 1)
            pe.wait_ge(w_ready, 1)

            def emit(at):
                n, par = at(1)
                if inside(n):
                    pe.wait_ge(xq_t_ready, n + 1)
                    wait(pe, hb_ready, n - 1)
                    pe.matmul(psum_h[par][:], xq_t[:, par], wt[0][:], start=True, stop=True).then_inc(h_done, 1)
                n, par = at(2)
                if inside(n):
                    pe.wait_ge(xq_ready, n + 1)
                    wait(pe, xq_t_ready, n)
                    pe.transpose(psum_x[:], xq[:, par], K["ident_bf"][:]).then_inc(x_turned, 1)
                n, par = at(1)
                if inside(n):
                    pe.wait_ge(hq_ready, n + 1)
                    wait(pe, hq_t_ready, n - 1)
                    for f in range(FB):
                        last = pe.transpose(psum_t[par][:, f, :], hq[:, par, f * P:(f + 1) * P], K["ident_bf"][:])
                    last.then_inc(h_turned, 1)
                n, par = at(0)
                if inside(n):
                    pe.wait_ge(hq_t_ready, n + 1)
                    wait(pe, ostep, OS * (n - 1) + 1)
                    for f in range(FB):
                        last = pe.matmul(psum_o[:], hq_t[:, par, f, :], wt[1][:, f * P:(f + 1) * P],
                                         start=f == 0, stop=f == FB - 1)
                    last.then_inc(o_done, 1)

            run(pe, emit)

        @block.scalar
        def _(act):
            def emit(at):
                n, par = at(1)
                if inside(n):
                    act.wait_ge(hb_ready, n + 1)
                    wait(act, hq_ready, n - 1)
                    act.activation(h[:, par], hb[:, par], ACT.Gelu).then_inc(h_ready, 1)
                n, par = at(2)
                if inside(n):
                    act.wait_ge(x_turned, n + 1)
                    wait(act, h_done, n - 1)
                    act.activation(xq_t[:, par], psum_x[:], ACT.Identity).then_inc(xq_t_ready, 1)
                n, par = at(1)
                if inside(n):
                    act.wait_ge(h_turned, n + 1)
                    wait(act, o_done, n - 1)
                    act.activation(hq_t[:, par], psum_t[par][:], ACT.Identity).then_inc(hq_t_ready, 1)

            run(act, emit)


@phase
def norm_context(nc, name, K, tokens, gain, bias, out):
    CTILES = NB * CK // P
    with ExitStack() as ctx:
        def sb(nm, shape, dt=F32):
            return ctx.enter_context(nc.sbuf_tensor(f"{name}_{nm}", shape, dt))

        def sem(nm):
            return nc.alloc_semaphore(f"{name}_{nm}")

        c = sb("c", [P, CTILES, CK])
        cn = sb("cn", [P, CTILES, CK])
        st6, mv, veps, rstd = sb("st6", [P, CTILES, 6]), sb("mv", [P, CTILES, 2]), sb("veps", [P, CTILES]), sb("rstd", [P, CTILES])
        g, b = sb("g", [CK, 1]), sb("b", [CK, 1])
        banks = [ctx.enter_context(nc.psum_tensor(f"{name}_t{i}", [CK, 4 * P], F32)) for i in range(2)]
        loaded, stepped, stats, rstd_ready = sem("loaded"), sem("stepped"), sem("stats"), sem("rstd_ready")
        pstep, cn_ready, turned, copied = sem("pstep"), sem("cn_ready"), sem("turned"), sem("copied")
        block = ctx.enter_context(nc.Block())

        @block.sync
        def _(sp):
            sp.dma_start(c[:], tokens).then_inc(loaded, 16)
            sp.dma_start(g[:], column(gain)).then_inc(loaded, 16)
            sp.dma_start(b[:], column(bias)).then_inc(loaded, 16)

        @block.vector
        def _(dve):
            dve.memset(out[CK:P, :], 0.0)
            dve.wait_ge(loaded, 48)
            for t in range(CTILES):
                last = dve.bn_stats(st6[:, t, :], c[:, t, :])
            last.then_inc(stepped, 1)
            dve.wait_ge(stepped, 1)
            for t in range(CTILES):
                last = dve.bn_aggr(mv[:, t, :], st6[:, t, :])
            last.then_inc(stats, 1)
            dve.wait_ge(rstd_ready, 1)
            for t in range(CTILES):
                last = dve.tensor_scalar(cn[:, t, :], c[:, t, :], mv[:, t, 0:1], rstd[:, t:t + 1],
                                         ALU.subtract, ALU.mult)
            last.then_inc(cn_ready, 1)

        @block.gpsimd
        def _(pool):
            pool.wait_ge(stats, 1)
            pool.tensor_scalar(veps[:], mv[:, :, 1], EPS, None, ALU.add).then_inc(pstep, 1)
            pool.wait_ge(pstep, 1)
            pool.tensor_tensor(rstd[:], veps[:], K["half"][:, 0:CTILES], ALU.pow).then_inc(rstd_ready, 1)

        @block.tensor
        def _(pe):
            pe.wait_ge(cn_ready, 1)
            for t in range(CTILES):
                pe.transpose(banks[t // 4][:, (t % 4) * P:(t % 4 + 1) * P], cn[:, t, :], K["ident"][:])\
                  .then_inc(turned, 1)

        @block.scalar
        def _(act):
            act.wait_ge(loaded, 48)
            for i in range(2):
                act.wait_ge(turned, 4 * (i + 1))
                act.activation(out[0:CK, i * 4 * P:(i + 1) * 4 * P], banks[i][:], ACT.Identity, scale=g[:], bias=b[:])\
                   .then_inc(copied, 1)


@phase
def load_tokens(nc, a, x, ctx_t):
    in_loaded, in_zeroed = nc.alloc_semaphore("in_loaded"), nc.alloc_semaphore("in_zeroed")
    with nc.Block() as block:
        @block.sync
        def _(sp):
            sp.dma_start(x[:], a["x"].rearrange("b (t p) d -> p (b t) d", p=P)).then_inc(in_loaded, 16)
            sp.dma_start(ctx_t[0:CK, :], a["ctx_t"]).then_inc(in_loaded, 16)
            sp.wait_ge(in_loaded, 32)

        @block.vector
        def _(dve):
            dve.memset(ctx_t[CK:P, :], 0.0).then_inc(in_zeroed, 1)
            dve.wait_ge(in_zeroed, 1)


@phase
def store_tokens(nc, x, out):
    out_stored = nc.alloc_semaphore("out_stored")
    with nc.Block() as block:
        @block.sync
        def _(sp):
            sp.dma_start(out.rearrange("b (t p) d -> p (b t) d", p=P), x[:]).then_inc(out_stored, 16)
            sp.wait_ge(out_stored, 16)


def heads(a, name, rows=P):
    return {"wq": a[f"{name}_wq"], "wk": a[f"{name}_wk"], "wv": a[f"{name}_wv"], "wo": a.get(f"{name}_wo"), "k_rows": rows}


def network(nc, a, out):
    with ExitStack() as stack:
        K = constants(nc, stack)
        x = stack.enter_context(nc.sbuf_tensor("tokens_x", [P, NT, D], F32))
        ctx_t = stack.enter_context(nc.sbuf_tensor("context_t", [P, NB * CK], F32))
        weights_by_expert = nc.dram_tensor("weights_by_expert", (NE, NTOK), F32, kind="Internal").ap()

        def scratch(ctx, name, shape, dt=F32):
            return ctx.enter_context(nc.sbuf_tensor(name, shape, dt))

        def parts(ctx, name):
            return (scratch(ctx, f"{name}_x_hi", [P, NTOK], F32R), scratch(ctx, f"{name}_x_lo", [P, NTOK], F32R),
                    scratch(ctx, f"{name}_acc", [P, NTOK]))

        def mixture(name, rule, kind):
            with ExitStack() as ctx:
                x_hi, x_lo, acc = parts(ctx, name)
                with ExitStack() as inner:
                    w = scratch(inner, f"{name}_route", [P, NT, NE])
                    w_t = scratch(inner, f"{name}_route_t", [NE, NTOK])
                    prepare(nc, f"{name}_prep", K, x, x_hi, x_lo,
                            gate=dict(w=a[f"{name}_gate_w"], b=a[f"{name}_gate_b"], rule=rule, weights=w, we_t=w_t,
                                      dram=weights_by_expert, bias=a[f"{name}_b_out"], acc=acc, by_token=False))
                experts(nc, f"{name}_experts", K, x_hi, x_lo, acc, kind=kind, weights=a[f"{name}_w"],
                        biases=a[f"{name}_b"], we_dram=weights_by_expert)
                add_turned(nc, f"{name}_add", K, acc, x, x)

        def mlp(name, src, base, dst, more):
            with ExitStack() as ctx:
                x_hi, x_lo, acc = parts(ctx, name)
                prepare(nc, f"{name}_prep", K, src, x_hi, x_lo, affine=(a[f"{name}_ln3_g"], a[f"{name}_ln3_b"]))
                experts(nc, f"{name}_mlp", K, x_hi, x_lo, acc, kind="gelu", weights=a[f"{name}_w"],
                        biases=a[f"{name}_b"], last_bias=a[f"{name}_b_out"])
                add_turned(nc, f"{name}_add", K, acc, base, dst, more=more)

        make_constants(nc, K)
        load_tokens(nc, a, x, ctx_t)

        attention(nc, "l0", K, heads(a, "l0", CK), dh=8, units=1, x=x, out=x, ctx_t=ctx_t,
                  biases=(a["l0_bq"], a["l0_bk"], a["l0_bv"]), out_bias=a["l0_bo"])
        mixture("l0f", "topk", "glu")

        with ExitStack() as ctx:
            y_t = scratch(ctx, "l1_y_t", [P, NTOK])
            attention(nc, "l1s", K, dict(heads(a, "l1s"), wo=a["l1c_wo"]), dh=8, units=4, x=x, out=None,
                      causal="before", store_t=y_t, biases=(a["l1s_bq"], a["l1s_bk"], a["l1s_bv"]))
            attention(nc, "l1c", K, heads(a, "l1c", CK), dh=8, units=1, x=x, out=x, ctx_t=ctx_t, add_t=y_t,
                      biases=(a["l1c_bq"], a["l1c_bk"], a["l1c_bv"]), out_bias=a["l1c_bo"])
        with ExitStack() as ctx:
            x_hi, x_lo, acc = parts(ctx, "l1f")
            kept = scratch(ctx, "l1f_tokens", [P, NT, D])
            w = scratch(ctx, "l1f_route", [P, NT, NE])
            with nc.sbuf_tensor("l1f_route_t", [NE, NTOK], F32) as w_t:
                prepare(nc, "l1f_prep", K, x, x_hi, x_lo, tokens=kept,
                        gate=dict(w=a["l1f_gate_w"], b=None, rule="topk", weights=w, we_t=w_t, dram=None,
                                  bias=a["l1f_ln_b"], acc=acc, by_token=True))
            experts_normed(nc, "l1f_experts", K, x_hi, x_lo, kept, w, acc[:].rearrange("p (t d) -> p t d", d=D), x,
                           weights=a["l1f_w"], biases=a["l1f_b"], out_biases=a["l1f_b_out"], gains=a["l1f_ln_g"],
                           eps=1e-6)

        with ExitStack() as ctx:
            base = scratch(ctx, "l2_base", [P, NT, D])
            att = scratch(ctx, "l2_att", [P, NT, D])
            attention(nc, "a1", K, heads(a, "a1"), dh=32, units=4, x=x, out=att, causal="after", residual=base,
                      norms=(None, (a["ln1_g"], a["ln1_b"])), affine_q=(a["a1_lnx_g"], a["a1_lnx_b"]),
                      affine_kv=(a["a1_lny_g"], a["a1_lny_b"]), out_bias=a["a1_bo"])
            mlp("a1", att, base, base, (att,))
            with ExitStack() as inner:
                ctx_n = scratch(inner, "context_n", [P, NB * CK])
                norm_context(nc, "ctxn", K, a["ctx"].rearrange("b (h t) d -> (b t) h d", h=1)
                             .rearrange("(n p) h d -> p n (h d)", p=P), a["a2_lny_g"], a["a2_lny_b"], ctx_n)
                attention(nc, "a2", K, heads(a, "a2", CK), dh=32, units=1, x=base, out=att, residual=base,
                          norms=((a["ln2_g"], a["ln2_b"]),), affine_q=(a["a2_lnx_g"], a["a2_lnx_b"]), ctx_t=ctx_n,
                          out_bias=a["a2_bo"])
            mlp("a2", att, base, x, (att, x))
        mixture("l2f", "threshold", "gelu")

        attention(nc, "l3", K, heads(a, "l3", CK), dh=8, units=1, x=x, out=x, ctx_t=ctx_t)
        ternary_mlp(nc, "l3f", K, x, w1=a["l3f_w1"], w2=a["l3f_w2"], b1=a["l3f_b1"], b2=a["l3f_b2"])
        store_tokens(nc, x, out)



def lay_out(v):
    import numpy as np

    def blocks(w, rows, cols):
        return [w[:, r * P:(r + 1) * P, c * P:(c + 1) * P] for r, c in zip(rows, cols)]

    def columns(*biases):
        cols = [b.reshape(b.shape[0], -1, P).transpose(2, 0, 1) for b in biases]
        return np.concatenate(cols, -1).reshape(P, -1)

    def chunks(w):
        return w.reshape(-1, P, w.shape[1]).transpose(1, 0, 2)

    def by_head(w):
        return w.transpose(1, 0, 2).reshape(w.shape[1], -1)

    a = {"x": v["x"], "ctx": v["ctx_512"], "ctx_t": v["ctx_512"].reshape(NB * CK, CK).T}
    for name, new in (("L0_xattn", "l0"), ("L1_xattn", "l1s")):
        for part in "qkv":
            a[f"{new}_w{part}"], a[f"{new}_b{part}"] = v[f"{name}_W{part}"], v[f"{name}_b{part}"]
    a["l0_wo"], a["l0_bo"] = chunks(v["L0_xattn_Wo"]), v["L0_xattn_bo"]
    for part in "qkv":
        a[f"l1c_w{part}"], a[f"l1c_b{part}"] = v[f"L1_xattn_Wc{part}"], v[f"L1_xattn_bc{part}"]
    a["l1c_wo"], a["l1c_bo"] = chunks(v["L1_xattn_Wp"]), v["L1_xattn_bp"]

    w1, w2, wg, w3 = (v[f"L0_ffn_{n}"] for n in ("w1", "w2", "wg", "w3"))
    a["l0f_w"] = np.concatenate(blocks(w1, [0], [0]) + blocks(w2, [0], [0]) + blocks(w1, [0], [1]) + blocks(w2, [0], [1])
                                + blocks(wg, [0, 0, 1, 1], [0, 1, 0, 1]) + blocks(w3, [0, 1], [0, 0]), -1)
    a["l0f_b"] = columns(v["L0_ffn_b1"], v["L0_ffn_b2"], v["L0_ffn_bg"])
    a["l0f_b_out"], a["l0f_gate_w"], a["l0f_gate_b"] = v["L0_ffn_b3"], v["L0_ffn_gate_w"], v["L0_ffn_gate_b"]

    w1, w2 = v["L1_ffn_w1"], v["L1_ffn_w2"]
    a["l1f_w"] = np.concatenate(blocks(w1, [0, 0], [0, 1]) + blocks(w2, [0, 1], [0, 0]), -1)
    a["l1f_b"] = columns(v["L1_ffn_b1"])
    a["l1f_b_out"], a["l1f_ln_g"] = v["L1_ffn_b2"].reshape(-1), v["L1_ffn_ln_g"].reshape(-1)
    a["l1f_ln_b"], a["l1f_gate_w"] = v["L1_ffn_ln_b"], v["L1_ffn_gate_w"]

    for i in (1, 2):
        n = f"L2_xattn_a{i}_"
        a[f"ln{i}_g"], a[f"ln{i}_b"] = v[f"L2_xattn_ln{i}_g"], v[f"L2_xattn_ln{i}_b"]
        for part in "qkv":
            a[f"a{i}_w{part}"] = by_head(v[f"{n}w{part}"])
        a[f"a{i}_wo"], a[f"a{i}_bo"] = chunks(v[f"{n}li1_w"]), v[f"{n}li1_b"]
        for part in ("lnx_g", "lnx_b", "lny_g", "lny_b", "ln3_g", "ln3_b"):
            a[f"a{i}_{part}"] = v[f"{n}{part}"]
        a[f"a{i}_w"] = np.concatenate(blocks(v[f"{n}li2_w"][None], [0] * 4, range(4))
                                      + blocks(v[f"{n}li3_w"][None], range(4), [0] * 4), -1)
        a[f"a{i}_b"], a[f"a{i}_b_out"] = columns(v[f"{n}li2_b"][None]), v[f"{n}li3_b"]

    a["l2f_w"] = np.concatenate(blocks(v["L2_ffn_W1"], [0] * 4, range(4))
                                + blocks(v["L2_ffn_W2"], range(4), [0] * 4), -1)
    a["l2f_b"], a["l2f_b_out"] = columns(v["L2_ffn_b1"]), v["L2_ffn_b2"]
    a["l2f_gate_w"], a["l2f_gate_b"] = v["L2_ffn_Wr"], v["L2_ffn_br"]

    a["l3_wq"], a["l3_wo"] = v["L3_xattn_Wq"].T, chunks(v["L3_xattn_Wo"].T)
    a["l3_wk"], a["l3_wv"] = v["L3_xattn_Wkv"][:D].T, v["L3_xattn_Wkv"][D:].T
    a["l3f_w1"] = v["L3_ffn_W1"].T
    a["l3f_w2"] = chunks(v["L3_ffn_W2"].T).reshape(P, -1)
    a["l3f_b1"], a["l3f_b2"] = v["L3_ffn_b1"], v["L3_ffn_b2"]
    return {f"in_{name}": np.ascontiguousarray(w) for name, w in a.items()}


def kernel(**inputs):
    import numpy as _np
    import concourse.bacc as _bacc
    from concourse import mybir as _mybir
    from concourse.bass_utils import run_bass_kernel_spmd as _run

    nc = _bacc.Bacc("TRN2", target_bir_lowering=False, num_devices=1)
    arrays = lay_out({name: _np.asarray(value) for name, value in inputs.items()})
    aps = {name[3:]: nc.dram_tensor(name, w.shape, _mybir.dt.from_np(w.dtype), kind="ExternalInput").ap()
           for name, w in arrays.items()}
    out = nc.dram_tensor("out_0_dram", (NB, T, D), _mybir.dt.float32, kind="ExternalOutput").ap()
    network(nc, aps, out)
    r = _run(nc, [arrays], core_ids=[0])
    return r.results[0]["out_0_dram"]
```

```python
from contextlib import ExitStack

import concourse.bass as bass
from concourse import mybir

F32 = mybir.dt.float32
F32R = mybir.dt.float32r
BF16 = mybir.dt.bfloat16
U32 = mybir.dt.uint32
ACT = mybir.ActivationFunctionType
ALU = mybir.AluOpType
AX = mybir.AxisListType

P = 128
NB = 16
T = 256
TT = T // P
D = 128
CK = 64
NH = 16
NE = 8
EPS = 1e-5


def wait(eng, sem, value):
    if isinstance(value, int) and value <= 0:
        return
    eng.wait_ge(sem, value)


def phase(build):
    def built(nc, *args, **kwargs):
        with nc.cleanup_on_exit():
            build(nc, *args, **kwargs)
    return built


def bcast_row(ap, n=P):
    return ap.rearrange("(a n) -> a n", a=1).broadcast_to([n, ap.shape[0]])


def column(ap):
    return ap.rearrange("(p a) -> p a", a=1)


@phase
def make_constants(nc, K):
    with ExitStack() as ctx:
        filled = nc.alloc_semaphore("const_filled")
        step = nc.alloc_semaphore("const_step")
        block = ctx.enter_context(nc.Block())

        @block.vector
        def _(dve):
            for name in ("ident", "ident_bf", "slots1_8", "slots1_32", "slots4_8", "slots4_32", "own1_8", "own1_32",
                         "own4_8", "own4_32", "tri_post"):
                last = dve.memset(K[name][:], 0.0 if name.startswith("ident") else 1.0)
            for name in ("mask_q", "mask_k"):
                last = dve.memset(K[name][:], 0.0)
            dve.memset(K["half"][:], -0.5)
            last.then_inc(filled, 1)

        @block.gpsimd
        def _(pool):
            pool.wait_ge(filled, 1)
            n = [0]

            def select(ap, op, fill, base, cm, pattern):
                if n[0]:
                    pool.wait_ge(step, n[0])
                pool.affine_select(out=ap, in_=ap, compare_op=op, fill=fill, base=base, pattern=pattern,
                                   channel_multiplier=cm).then_inc(step, 1)
                n[0] += 1

            def window(ap, lo, width, cm, pattern):
                select(ap, ALU.is_ge, 0.0, lo, cm, pattern)
                select(ap, ALU.is_ge, 0.0, width - 1 - lo, -cm, [[-s, k] for s, k in pattern])

            for name in ("ident", "ident_bf"):
                select(K[name][:], ALU.not_equal, 1.0, 0, 1, [[-1, P]])
            window(K["slots1_8"][:].rearrange("p (a q e) -> p a q e", a=2, q=4), 0, 8, 1,
                   [[-16, 2], [-32, 4], [-8, 2]])
            window(K["slots4_8"][:].rearrange("p (u q) -> p u q", u=4), 0, 8, 1, [[-8, 4], [-32, 4]])
            for name in ("slots1_32", "slots4_32"):
                window(K[name][:].rearrange("p (a q) -> p a q", q=4), 0, 32, 1,
                       [[0, K[name].shape[1] // 4], [-32, 4]])
            v = K["own1_8"][:].rearrange("p a (l e d) -> p a l e d", l=2, e=2)
            for a in range(2):
                select(v[:, a], ALU.is_equal, 0.0, -a, 0, [[1, 2], [0, 2], [0, 8]])
                window(v[:, a], 0, 64, 1, [[0, 2], [-64, 2], [0, 8]])
            window(K["own1_32"][:].rearrange("p (e d) -> p e d", e=2), 0, 64, 1, [[-64, 2], [0, 32]])
            window(K["own4_8"][:].rearrange("p u (l d) -> p u l d", l=4), 0, 1, 0, [[-1, 4], [1, 4], [0, 8]])
            select(K["tri_post"][:], ALU.is_gt, 0.0, 0, 1, [[-1, P]])
            select(K["mask_q"][:], ALU.is_ge, -1e30, 0, 1, [[P, TT], [-1, T]])
            select(K["mask_k"][:], ALU.is_ge, -1e30, 0, -1, [[-P, TT], [1, T]])
            pool.wait_ge(step, n[0])


def constants(nc, ctx):
    def sb(name, shape, dt=F32):
        return ctx.enter_context(nc.sbuf_tensor(name, shape, dt))
    return {
        "passed": ctx.enter_context(nc.semaphore("passed")),
        "ident": sb("ident", [P, P]), "ident_bf": sb("ident_bf", [P, P], BF16),
        "slots1_8": sb("slots1_8", [P, 16]), "slots4_8": sb("slots4_8", [P, 16]),
        "slots1_32": sb("slots1_32", [P, 16]), "slots4_32": sb("slots4_32", [P, 16]),
        "own1_8": sb("own1_8", [P, 2, 32]), "own1_32": sb("own1_32", [P, 64]),
        "own4_8": sb("own4_8", [P, 4, 32]), "own4_32": sb("own4_32", [P, 32]),
        "tri_post": sb("tri_post", [P, P]),
        "mask_q": sb("mask_q", [P, TT, T], BF16), "mask_k": sb("mask_k", [P, TT, T], BF16),
        "half": sb("half", [P, 8]),
    }


@phase
def attention(nc, name, K, W, *, dh, units, x, out, norms=(), affine_q=None, affine_kv=None, biases=None,
              out_bias=None, causal=None, ctx_t=None, add_t=None, store_t=None, residual=None):
    C = dh * NH // P
    U = units
    N = NB * U
    per_unit = U == 4 and C == 4
    DP = 4 if per_unit else 2
    NLN = len(norms) + 1
    NK = CK if U == 1 else T
    split_norm = U == 1 and C == 4
    scale = float(dh) ** -0.5
    slots = K[f"slots{U}_{dh}"]
    own = K[f"own{U}_{dh}"]
    QC = 1 if per_unit else C

    with ExitStack() as ctx:
        def sb(nm, shape, dt=F32):
            return ctx.enter_context(nc.sbuf_tensor(f"{name}_{nm}", shape, dt))

        def sem(nm):
            return nc.alloc_semaphore(f"{name}_{nm}")

        wq, wk, wv, wo = (sb(n, [P, C, P] if n == "wo" else [P, C * P]) for n in ("wq", "wk", "wv", "wo"))
        bq = bk = bvb = bob = None
        if biases:
            bq, bk, bvb = sb("bq", [P, 1]), sb("bk", [P, 1]), sb("bvb", [P, P])
        if out_bias is not None:
            bob = sb("bob", [P, P])
        gb = [pair and (sb(f"g{i}", [P, P]), sb(f"b{i}", [P, P])) for i, pair in enumerate(norms)]
        aq = (sb("aqg", [P, 1]), sb("aqb", [P, 1])) if affine_q else None
        akv = (sb("akg", [P, 1]), sb("akb", [P, 1])) if affine_kv else None

        xn = sb("xn", [P, TT, P])
        mv = sb("mv", [P, NLN, TT, 2])
        st6 = sb("st6", [P, NLN, TT, 6])
        rstd = sb("rstd", [P, NLN, TT])
        veps = sb("veps", [P, NLN, TT])
        xq_t = sb("xq_t", [P, T])
        xkv_t = sb("xkv_t", [P, T]) if affine_kv else xq_t
        cdup = sb("cdup", [P, 2, 2, CK]) if U == 1 else None
        q_f = sb("q_f", [P, QC, T])
        k_f = sb("k_f", [P, QC, NK])
        q_hi, q_lo = sb("q_hi", [P, 2, QC, T], F32R), sb("q_lo", [P, 2, QC, T], F32R)
        k_hi, k_lo = sb("k_hi", [P, 2, QC, NK], F32R), sb("k_lo", [P, 2, QC, NK], F32R)
        kb_hi, kb_lo = sb("kb_hi", [P, 2, 1024], F32R), sb("kb_lo", [P, 2, 1024], F32R)
        negm = sb("negm", [P, 2, TT, 16 // U], BF16)
        if per_unit:
            v_f = sb("v_f", [P, DP, TT, P])
            vb = v_f
        else:
            v_f = sb("v_f", [P, TT if U == 4 else 1, C * P])
            vb = sb("vb", [P, 2, {(1, 8): 256, (1, 32): 512, (4, 8): 1024}[U, dh]])
        pt = sb("pt", [P, 2, 4, T])
        pm = sb("pm", [P, 2, 4, P]) if causal == "after" else None
        rden = sb("rden", [P, 2, 512 if split_norm else T])
        o_t = sb("o_t", [P, C, T]) if store_t is None else None
        res = sb("res", [P, TT, P]) if store_t is None else None

        psum_st = [ctx.enter_context(nc.psum_tensor(f"{name}_st{g}", [P, 4, T], F32)) for g in range(2)]
        WN = 512 if split_norm else T
        psum_nd = ctx.enter_context(nc.psum_tensor(f"{name}_nd", [P, 2, WN], F32))
        psum_num, psum_den = psum_nd[:, 0, :], psum_nd[:, 1, :]
        psum_act = ctx.enter_context(nc.psum_tensor(f"{name}_pa", [P, 512], F32))
        BANKS = 1 if split_norm else 2
        psum_s = [ctx.enter_context(nc.psum_tensor(f"{name}_s{i}", [P, 512], F32)) for i in range(BANKS)]
        psum_w = psum_s[-1]

        loaded = sem("loaded")
        zeroed = sem("zeroed")
        stats = sem("stats")
        rstd_ready = sem("rstd_ready")
        vstep = sem("vstep")
        pstep = sem("pstep")
        xn_ready = sem("xn_ready")
        xn_turned = sem("xn_turned")
        x_t_ready = sem("x_t_ready")
        cdup_ready = sem("cdup_ready")
        proj_done = sem("proj_done")
        proj_out = sem("proj_out")
        k_split = sem("k_split")
        q_split = sem("q_split")
        kb_hi_ready = sem("kb_hi_ready")
        kb_lo_ready = sem("kb_lo_ready")
        v_step = sem("v_step")
        vb_ready = sem("vb_ready")
        s_ready = sem("s_ready")
        max_done = sem("max_done")
        st_ready = sem("st_ready")
        exp_done = sem("exp_done")
        pm_ready = sem("pm_ready")
        pv_done = sem("pv_done")
        rden_ready = sem("rden_ready")
        norm_done = sem("norm_done")
        w_done = sem("w_done")
        wres = sem("wres")
        res_done = sem("res_done")

        if U == 4:
            uses = [["q0", "k0"], ["v"]]
        elif C == 1:
            uses = [["q0", "k0", "v"]]
        else:
            uses = [["q0", "q1"], ["q2", "q3"], ["k0", "k1", "k2", "k3"], ["v"]]
        NU = len(uses)
        PM_ = N if per_unit else NB

        def pset(n, b):
            return n if per_unit else b

        def arrived(m, what):
            return m * NU + max(i for i, use in enumerate(uses) if any(w[0] == what for w in use)) + 1

        def piece_keys(qt):
            return (qt + 1) * P if causal == "before" else T

        def first_query(g):
            return g * P if causal == "before" else 0

        def steps(emit):
            def pos(i, j):
                def at(k):
                    jj = j + k
                    return 2 * U * i + jj, 2 * i + jj // U, jj % U, jj % (2 * U)
                return at
            return pos

        def run(eng, emit):
            pos = steps(emit)
            for j in range(-3, 2 * U):
                emit(pos(0, j))
            looped = NB // 2 - (2 if U == 1 else 1)
            with eng.Fori(1, looped) as i:
                for j in range(2 * U):
                    emit(pos(i, j))
            for j in range(2 * U * (NB // 2 - looped) + 1):
                emit(pos(looped, j))

        def inside(n, limit=N):
            return not isinstance(n, int) or 0 <= n < limit

        def spread_keys(eng, dst, src, n, b, u, pos):
            par, par_m = pos % 2, (pos % 2) if (per_unit or U == 1) else (pos // U) % 2
            if U == 1 and C == 1:
                o, a = [P, 16, CK], src[:, par_m, 0, :].bitcast(F32).unsqueeze(1).broadcast_to([P, 16, CK])
                s = slots[:].unsqueeze(2).broadcast_to(o)
                d = dst[:, par, :].rearrange("p (s k) -> p s k", s=16)
            elif U == 1:
                o = [P, C, 4, CK]
                a = src[:, par_m].bitcast(F32).unsqueeze(2).broadcast_to(o)
                s = slots[:].rearrange("p (c q) -> p c q", q=4).unsqueeze(3).broadcast_to(o)
                d = dst[:, par, :].rearrange("p (c q k) -> p c q k", c=C, q=4)
            else:
                o = [P, 4, T]
                a = src[:, par_m, 0, :].bitcast(F32).unsqueeze(1).broadcast_to(o)
                s = slots[:, 4 * u:4 * u + 4].unsqueeze(2).broadcast_to(o)
                d = dst[:, par, :].rearrange("p (q k) -> p q k", q=4)
            return eng.tensor_tensor(d, a, s, ALU.mult)

        vb_sum = sem("vb_sum")
        res_out = sem("res_out")
        block = ctx.enter_context(nc.Block())

        @block.sync
        def _(sp):
            n = 0
            rows = W["k_rows"]
            for dst, src in ([(wq[:], W["wq"]), (wk[0:rows, :], W["wk"]), (wv[0:rows, :], W["wv"]), (wo[:], W["wo"])]
                             + ([(bq[:], column(biases[0])), (bk[:], column(biases[1])),
                                 (bvb[:], bcast_row(biases[2]))] if biases else [])
                             + ([(bob[:], bcast_row(out_bias))] if bob is not None else [])
                             + [(t[:], bcast_row(a)) for pair, own_ in zip(norms, gb) if pair for a, t in zip(pair, own_)]
                             + ([(t[:], column(a)) for a, t in zip(affine_q, aq)] if aq else [])
                             + ([(t[:], column(a)) for a, t in zip(affine_kv, akv)] if akv else [])):
                sp.dma_start(dst, src).then_inc(loaded, 16)
                n += 1
            sp.wait_ge(loaded, 16 * n)

        n_loads = 4 + (3 if biases else 0) + (bob is not None) + 2 * sum(pair is not None for pair in norms) + (2 if aq else 0) + (2 if akv else 0)

        @block.tensor
        def _(pe):
            pe.wait_ge(loaded, 16 * n_loads)
            if U == 1:
                pe.wait_ge(zeroed, 1)

            def turn(b):
                sets = b * (U if per_unit else 1)
                wait(pe, proj_out, sets * NU)
                pe.wait_ge(xn_ready, b + 1)
                for t in range(TT):
                    last = pe.transpose(psum_act[:, t * P:(t + 1) * P], xn[:, t, :], K["ident"][:])
                last.then_inc(xn_turned, 1)

            def project(n, b, u, pos, i):
                m = pset(n, b)
                if i == 0:
                    pe.wait_ge(x_t_ready, b + 1)
                    wait(pe, proj_out, m * NU)
                else:
                    pe.wait_ge(proj_out, m * NU + i)
                if U == 1 and "v" in uses[i]:
                    pe.wait_ge(cdup_ready, b + 1)
                col = 0
                for what in uses[i]:
                    if what[0] == "q":
                        c = u if per_unit else int(what[1])
                        last = pe.matmul(psum_act[:, col:col + T], wq[:, c * P:(c + 1) * P], xq_t[:],
                                         start=True, stop=True)
                        col += T
                    elif what[0] == "k":
                        c = u if per_unit else int(what[1])
                        src = xkv_t[:] if U == 4 else ctx_t[:, bass.ds(b * CK, CK)]
                        last = pe.matmul(psum_act[:, col:col + NK], wk[:, c * P:(c + 1) * P], src,
                                         start=True, stop=True)
                        col += NK
                    elif U == 4:
                        c = u if per_unit else 0
                        for t in range(TT):
                            last = pe.matmul(psum_act[:, t * P:(t + 1) * P], xkv_t[:, t * P:(t + 1) * P],
                                             wv[:, c * P:(c + 1) * P], start=True, stop=True)
                    else:
                        last = pe.matmul(psum_act[:, col:col + C * P],
                                         cdup[:, (pos // U) % 2].rearrange("p a k -> p (a k)"), wv[:],
                                         start=True, stop=True)
                last.then_inc(proj_done, 1)

            def scores(n, b, u, pos, i, projected=None):
                qt, half = divmod(i, 2)
                if i == 0:
                    pe.wait_ge(proj_out, arrived(pset(n, b), "q"))
                    pe.wait_ge(kb_hi_ready, n + 1)
                wait(pe, max_done, 4 * n + i + 1 - BANKS)
                if i == 3 and projected is not None:
                    pe.wait_ge(res_done, projected + 1)
                dst = psum_s[i % BANKS]
                par_q = (pos % 2) if (per_unit or U == 1) else (pos // U) % 2
                keys = piece_keys(qt)
                if keys < T:
                    pe.matmul(dst[:, 0:2 * keys].rearrange("p (h k) -> p h k", h=2), q_hi[:, par_q, 0, 0:P],
                              kb_hi[:, pos % 2, half * 512:(half + 1) * 512]
                              .rearrange("p (h k) -> p h k", h=2)[:, :, 0:keys], start=True, stop=False)
                n_mm = 0 if keys < T else 2 if split_norm else 1
                for s in range(n_mm):
                    c = 2 * half + s if split_norm else 0
                    w = 512 // n_mm
                    last = pe.matmul(dst[:, s * w:(s + 1) * w], q_hi[:, par_q, c, qt * P:(qt + 1) * P],
                                     kb_hi[:, pos % 2, half * 512 + s * w:half * 512 + (s + 1) * w],
                                     start=True, stop=causal != "before")
                if causal == "before":
                    own_keys = slice(qt * P, (qt + 1) * P)
                    last = pe.matmul(dst[:, 0:2 * keys].rearrange("p (h k) -> p h k", h=2)[:, :, own_keys],
                                     K["ident_bf"][:], K["mask_q"][:, qt:qt + 1, own_keys].broadcast_to([P, 2, P]),
                                     start=False, stop=True)
                last.then_inc(s_ready, 1)

            def scores_t(n, b, u, pos, g):
                if g == 0:
                    pe.wait_ge(q_split, pset(n, b) + 1)
                    pe.wait_ge(kb_lo_ready, n + 1)
                    pe.wait_ge(max_done, 4 * n + 4)
                wait(pe, exp_done, 2 * n - 1 + g)
                par, par_q = pos % 2, (pos % 2) if (per_unit or U == 1) else (pos // U) % 2
                for i in range(4):
                    t = 4 * g + i
                    c = t // 2 if split_norm else 0
                    col = t * P if U == 1 else (t % 4) * T + (t // 4) * P
                    dst = psum_st[g][:, i, :]
                    q0 = first_query(g)
                    for j, (a, q) in enumerate(((kb_hi, q_hi), (kb_lo, q_hi), (kb_hi, q_lo))):
                        pe.matmul(dst[:, q0:T], a[:, par, col:col + P], q[:, par_q, c, q0:T],
                                  start=j == 0, stop=False)
                    if causal == "before":
                        diagonal = slice(g * P, (g + 1) * P)
                        pe.matmul(dst[:, diagonal], K["ident_bf"][:], K["mask_k"][:, g, diagonal],
                                  start=False, stop=False)
                    for qt in range(q0 // P, TT):
                        if U == 4:
                            last = pe.matmul(dst[:, qt * P:(qt + 1) * P],
                                             negm[:, par, qt, t % 4:t % 4 + 1].broadcast_to([P, P]),
                                             K["ident_bf"][:], start=False, stop=qt == 1)
                        else:
                            for e in range(2):
                                last = pe.matmul(psum_st[g][64 * e:64 * e + 64, i, qt * P:(qt + 1) * P],
                                                 negm[:, par, qt, 2 * t + e:2 * t + e + 1].broadcast_to([P, 64]),
                                                 K["ident_bf"][:], start=False, stop=qt == 1)
                last.then_inc(st_ready, 1)

            def values(n, b, u, pos, g):
                pe.wait_ge(exp_done, 2 * n + 1 + g)
                if g == 0:
                    pe.wait_ge(vb_ready if not per_unit else proj_out,
                               (pset(n, b) + 1) * (NU if per_unit else 1))
                if split_norm:
                    wait(pe, norm_done, 2 * n + g)
                elif U == 4 and not per_unit:
                    if u == 0 and g == 0:
                        wait(pe, norm_done, b)
                elif g == 0:
                    wait(pe, norm_done, n)
                if pm is not None:
                    pe.wait_ge(pm_ready, 2 * n + 1 + g)
                par = pos % 2
                for kind in ("num", "den"):
                    bank = psum_num if kind == "num" else psum_den
                    for i in range(4):
                        t = 4 * g + i
                        if split_norm:
                            lhs = vb[:, par, t * 64:(t + 1) * 64] if kind == "num" else own[:]
                            dst = bank[64 * (t % 2):64 * (t % 2) + 64, (i // 2) * T:(i // 2 + 1) * T]
                            last = pe.matmul(dst, lhs, pt[:, g, i, :], start=True, stop=True)
                            continue
                        dst = bank[32 * i:32 * i + 32, 0:T]
                        if U == 1:
                            lhs = vb[:, par, g * P + i * 32:g * P + (i + 1) * 32] if kind == "num" else own[:, g, :]
                            start, stop = g == 0, g == 1
                        elif C == 1:
                            vpar = (pos // U) % 2
                            o = g * 512 + u * P + i * 32
                            lhs = vb[:, vpar, o:o + 32] if kind == "num" else own[:, u, :]
                            start, stop = u == 0 and g == 0, u == 3 and g == 1
                        else:
                            lhs = vb[:, pos % DP, g, 32 * i:32 * i + 32] if kind == "num" else own[:]
                            start, stop = g == 0, g == 1
                        start, stop = start and kind == "num", stop and kind == "den"
                        if pm is not None and kind == "num":
                            if g == 0:
                                last = pe.matmul(dst[:, 0:P], lhs, pm[:, 0, i, :], start=True, stop=False)
                            else:
                                pe.matmul(dst[:, 0:P], lhs, pt[:, 1, i, 0:P], start=False, stop=False)
                                last = pe.matmul(dst[:, P:T], lhs, pm[:, 1, i, :], start=False, stop=False)
                        else:
                            q0 = first_query(g)
                            last = pe.matmul(dst[:, q0:T], lhs, pt[:, g, i, q0:T], start=start, stop=stop)
                last.then_inc(pv_done, 1)

            def project_out(n, b):
                pe.wait_ge(norm_done, (b + 1) * (2 if split_norm else U if per_unit else 1))
                for t in range(TT):
                    for c in range(C):
                        last = pe.matmul(psum_w[:, t * P:(t + 1) * P], o_t[:, c, t * P:(t + 1) * P], wo[:, c, :],
                                         start=c == 0, stop=c == C - 1)
                last.then_inc(w_done, 1)

            def emit(at):
                n, b, u, pos = at(0)
                n1, b1, u1, pos1 = at(-1)
                nn, bn, un, posn = at(1)
                n2, b2, u2, pos2 = at(2)
                out_now = inside(n1) and u1 == U - 1 and store_t is None
                do_p = inside(n2) and (per_unit or u2 == 0)
                if inside(n):
                    scores_t(n, b, u, pos, 0)
                if inside(n1):
                    values(n1, b1, u1, pos1, 1)
                if inside(nn):
                    scores(nn, bn, un, posn, 0)
                if inside(n2) and u2 == 0:
                    turn(b2)
                if inside(nn):
                    scores(nn, bn, un, posn, 1)
                if inside(n):
                    scores_t(n, b, u, pos, 1)
                if do_p:
                    project(n2, b2, u2, pos2, 0)
                if inside(nn):
                    scores(nn, bn, un, posn, 2)
                if out_now:
                    pe.wait_ge(max_done, 4 * nn + 4 - BANKS if inside(nn) else 4 * N)
                    if not inside(nn):
                        wait(pe, res_done, b1)
                    project_out(n1, b1)
                if do_p and NU == 4:
                    project(n2, b2, u2, pos2, 1)
                if inside(nn) and not split_norm:
                    scores(nn, bn, un, posn, 3, b1 if out_now else None)
                if inside(n):
                    values(n, b, u, pos, 0)
                if do_p and NU == 4:
                    project(n2, b2, u2, pos2, 2)
                if inside(nn) and split_norm:
                    scores(nn, bn, un, posn, 3, b1 if out_now else None)
                if do_p and NU > 1:
                    project(n2, b2, u2, pos2, NU - 1)

            run(pe, emit)

        @block.scalar
        def _(act):
            act.wait_ge(loaded, 16 * n_loads)

            def exps(n, g):
                act.wait_ge(st_ready, 2 * n + 1 + g)
                wait(act, pv_done, 2 * n - 1 + g)
                if pm is not None:
                    wait(act, pm_ready, 2 * n - 1 + g)
                q0 = first_query(g)
                act.activation(pt[:, g, :, q0:T], psum_st[g][:, :, q0:T], ACT.Exp, scale=scale).then_inc(exp_done, 1)

            def turned(b):
                act.wait_ge(xn_turned, b + 1)
                if akv:
                    act.activation(xkv_t[:], psum_act[:, 0:T], ACT.Identity, scale=akv[0][:], bias=akv[1][:])
                act.activation(xq_t[:], psum_act[:, 0:T], ACT.Identity, scale=aq[0][:] if aq else 1.0,
                               bias=aq[1][:] if aq else 0.0).then_inc(x_t_ready, 1)

            def hi_free(m):
                wait(act, st_ready, 2 * (m - 1) if (per_unit or U == 1) else 2 * U * (m - 1))

            def copy_out(n, b, u, pos, i):
                m = pset(n, b)
                par = (pos % 2) if (per_unit or U == 1) else (pos // U) % 2
                act.wait_ge(proj_done, m * NU + i + 1)
                col, k, nq = 0, 0, 0
                last = None
                for what in uses[i]:
                    if what[0] == "q":
                        c = int(what[1])
                        if c == 0:
                            wait(act, q_split, m)
                            hi_free(m)
                        for dst in (q_f[:, c, :], q_hi[:, par, c, :]):
                            last = act.activation(dst, psum_act[:, col:col + T], ACT.Identity,
                                                  bias=bq[:] if bq is not None else 0.0)
                        col += T
                    elif what[0] == "k":
                        c = int(what[1])
                        if c == 0:
                            wait(act, k_split, m)
                        for dst in (k_f[:, c, :], k_hi[:, par, c, :]):
                            last = act.activation(dst, psum_act[:, col:col + NK], ACT.Identity,
                                                  bias=bk[:] if bk is not None else 0.0)
                        col += NK
                    elif per_unit:
                        wait(act, pv_done, 2 * (n - 3))
                        last = act.activation(v_f[:, pos % DP].rearrange("p t d -> p (t d)"), psum_act[:, 0:T],
                                              ACT.Identity)
                    elif U == 4:
                        wait(act, vb_ready, m)
                        last = act.activation(v_f[:].rearrange("p t d -> p (t d)"), psum_act[:, 0:T], ACT.Identity)
                    else:
                        wait(act, vb_ready, m)
                        last = act.activation(v_f[:, 0, :], psum_act[:, col:col + C * P], ACT.Identity)
                last.then_inc(proj_out, 1)

            def emit(at):
                n, b, u, pos = at(0)
                if inside(n):
                    exps(n, 0)
                n2, b2, u2, pos2 = at(2)
                if inside(n2) and u2 == 0:
                    turned(b2)
                do_p = inside(n2) and (per_unit or u2 == 0)
                if inside(n):
                    exps(n, 1)
                if do_p:
                    for i in range(NU):
                        copy_out(n2, b2, u2, pos2, i)

            run(act, emit)

        @block.vector
        def _(dve):
            dve.wait_ge(loaded, 16 * n_loads)
            if U == 1:
                dve.memset(wk[64:P, :], 0.0)
                dve.memset(wv[64:P, :], 0.0).then_inc(zeroed, 1)
            before = [sum(1 if pair is None else 3 for pair in norms[:i]) for i in range(NLN)]
            SB = before[-1] + 1

            def ln_stats(b, i):
                src = x[:, bass.ds(b * TT, TT), :] if i == 0 else (
                    residual[:, bass.ds(b * TT, TT), :] if residual is not None else None)
                dve.sem_inc(K["passed"], 1)
                for t in range(TT):
                    last = dve.bn_stats(st6[:, i, t, :], src[:, t, :])
                last.then_inc(vstep, 1)
                dve.wait_ge(vstep, b * SB + before[i] + 1)
                dve.sem_inc(K["passed"], 1)
                for t in range(TT):
                    last = dve.bn_aggr(mv[:, i, t, :], st6[:, i, t, :])
                last.then_inc(stats, 1)

            def ln_apply(b, i):
                dve.wait_ge(rstd_ready, b * NLN + i + 1)
                src = (x if i == 0 else residual)[:, bass.ds(b * TT, TT), :]
                if i == 0 or norms[0] is None:
                    wait(dve, xn_turned, b)
                plain = i < NLN - 1 and norms[i] is None
                dst = residual[:, bass.ds(b * TT, TT), :] if plain else xn
                for t in range(TT):
                    last = dve.tensor_scalar(dst[:, t, :], src[:, t, :], mv[:, i, t, 0:1], rstd[:, i, t:t + 1],
                                             ALU.subtract, ALU.mult)
                if i == NLN - 1:
                    last.then_inc(xn_ready, 1)
                    return
                if plain:
                    last.then_inc(wres, 1)
                else:
                    last.then_inc(vstep, 1)
                    dve.wait_ge(vstep, b * SB + before[i] + 2)
                    g, bb = gb[i]
                    dve.tensor_tensor(xn[:], xn[:], g[:].unsqueeze(1).broadcast_to([P, TT, P]), ALU.mult)\
                       .then_inc(vstep, 1)
                    dve.wait_ge(vstep, b * SB + before[i] + 3)
                    dve.tensor_tensor(residual[:, bass.ds(b * TT, TT), :], xn[:],
                                      bb[:].unsqueeze(1).broadcast_to([P, TT, P]), ALU.add).then_inc(wres, 1)
                dve.wait_ge(wres, b * len(norms) + i + 1)

            def keys_hi(n, b, u, pos):
                dve.wait_ge(proj_out, arrived(pset(n, b), "k"))
                wait(dve, st_ready, 2 * (n - 1))
                spread_keys(dve, kb_hi, k_hi, n, b, u, pos).then_inc(kb_hi_ready, 1)

            def maxima(n, pos, i):
                qt, half = divmod(i, 2)
                dve.wait_ge(s_ready, 4 * n + i + 1)
                h = 8 // U
                if i == 0:
                    wait(dve, st_ready, 2 * (n - 1))
                dve.tensor_reduce(negm[:, pos % 2, qt, half * h:(half + 1) * h],
                                  psum_s[i % BANKS][:, 0:512 * piece_keys(qt) // T]
                                  .rearrange("p (h k) -> p h k", h=h), AX.X, ALU.max, negate=True)\
                   .then_inc(max_done, 1)

            norm_count = 2 if split_norm else 1

            def normalise(idx, n, b, u, g):
                w = 512 if split_norm else T
                dve.wait_ge(pv_done, 2 * n + 1 + g)
                dve.reciprocal(rden[:, 0, 0:w], psum_den[:, 0:w]).then_inc(rden_ready, 1)
                dve.wait_ge(rden_ready, idx + 1)
                if store_t is not None:
                    dve.tensor_tensor(store_t[:, bass.ds(b * T, T)], psum_num[:, 0:T], rden[:, 0, 0:T], ALU.mult)\
                       .then_inc(norm_done, 1)
                    return
                dst = o_t[:, 2 * g:2 * g + 2, :].rearrange("p c t -> p (c t)") if split_norm else \
                    o_t[:, u if per_unit else 0, :]
                if add_t is None:
                    dve.tensor_tensor(dst, psum_num[:, 0:w], rden[:, 0, 0:w], ALU.mult).then_inc(norm_done, 1)
                else:
                    dve.tensor_tensor(rden[:, 1, :], psum_num[:, 0:w], rden[:, 0, 0:w], ALU.mult)\
                       .then_inc(vb_sum, 1)
                    dve.wait_ge(vb_sum, idx + 1)
                    dve.tensor_tensor(dst, rden[:, 1, :], add_t[:, bass.ds(b * T, T)], ALU.add)\
                       .then_inc(norm_done, 1)

            def residuals(b):
                dve.wait_ge(w_done, b + 1)
                view = psum_w[:, 0:T].rearrange("p (t d) -> p t d", t=TT)
                base = (residual if residual is not None else x)[:, bass.ds(b * TT, TT), :]
                if bob is None:
                    dve.tensor_tensor(out[:, bass.ds(b * TT, TT), :], view, base, ALU.add).then_inc(res_done, 1)
                else:
                    dve.tensor_tensor(res[:], view, bob[:].unsqueeze(1).broadcast_to([P, TT, P]), ALU.add)\
                       .then_inc(res_done, 1)
                    dve.wait_ge(res_done, b + 1)
                    dve.tensor_tensor(out[:, bass.ds(b * TT, TT), :], res[:], base, ALU.add).then_inc(res_out, 1)

            def emit(at):
                n, b, u, pos = at(0)
                n1, b1, u1, _ = at(-1)
                nn, bn, un, posn = at(1)
                n3, b3, u3, _ = at(3)
                ln = inside(n3) and u3 == 0
                if inside(nn):
                    keys_hi(nn, bn, un, posn)
                    maxima(nn, posn, 0)
                if inside(n1):
                    if split_norm:
                        normalise(2 * n1 + 1, n1, b1, u1, 1)
                    elif per_unit or U == 1:
                        normalise(n1, n1, b1, u1, 1)
                    elif u1 == U - 1:
                        normalise(b1, n1, b1, u1, 1)
                if inside(nn):
                    maxima(nn, posn, 1)
                if ln:
                    ln_stats(b3, 0)
                if inside(nn):
                    maxima(nn, posn, 2)
                if inside(n1) and u1 == U - 1 and store_t is None:
                    residuals(b1)
                for i in range(NLN if ln else 0):
                    ln_apply(b3, i)
                    if i + 1 < NLN:
                        ln_stats(b3, i + 1)
                if inside(nn):
                    maxima(nn, posn, 3)
                if inside(n) and split_norm:
                    normalise(2 * n, n, b, u, 0)

            run(dve, emit)
            if bob is not None and store_t is None:
                dve.wait_ge(res_out, NB)

        @block.gpsimd
        def _(pool):
            pool.wait_ge(loaded, 16 * n_loads)

            def rstds(b, i):
                pool.wait_ge(stats, b * NLN + i + 1)
                pool.sem_inc(K["passed"], 1)
                pool.tensor_scalar(veps[:, i, :], mv[:, i, :, 1], EPS, None, ALU.add).then_inc(pstep, 1)
                pool.wait_ge(pstep, b * NLN + i + 1)
                pool.tensor_tensor(rstd[:, i, :], veps[:, i, :], K["half"][:, 0:TT], ALU.pow).then_inc(rstd_ready, 1)

            def context(b, pos):
                pool.sem_inc(K["passed"], 1)
                pool.tensor_copy(cdup[:, pos % 2],
                                 ctx_t[:, bass.ds(b * CK, CK)].unsqueeze(1).broadcast_to([P, 2, CK]))\
                    .then_inc(cdup_ready, 1)

            def split(m, par, src, hi, lo, what, ready):
                pool.wait_ge(proj_out, arrived(m, what))
                pool.tensor_tensor(lo[:, par], src[:], hi[:, par].bitcast(F32), ALU.subtract).then_inc(ready, 1)

            def lay_values(m, par):
                pool.wait_ge(proj_out, m * NU + NU)
                if bvb is not None:
                    o = [P, v_f.shape[1], P]
                    pool.tensor_tensor(v_f[:], v_f[:], bvb[:].unsqueeze(1).broadcast_to(o), ALU.add)\
                        .then_inc(v_step, 1)
                    pool.wait_ge(v_step, m + 1)
                wait(pool, pv_done, 2 * (m - 1) if U == 1 else 2 * U * (m - 1))
                if U == 1 and C == 1:
                    o = [P, 2, 4, 32]
                    pool.tensor_tensor(vb[:, par].rearrange("p (a q d) -> p a q d", a=2, q=4),
                                       v_f[:, 0].rearrange("p (q d) -> p q d", q=4).unsqueeze(1).broadcast_to(o),
                                       own[:].unsqueeze(2).broadcast_to(o), ALU.mult).then_inc(vb_ready, 1)
                elif U == 1:
                    o = [P, 8, 64]
                    pool.tensor_tensor(vb[:, par].rearrange("p (j d) -> p j d", j=8),
                                       v_f[:, 0].rearrange("p (j d) -> p j d", j=8),
                                       own[:].unsqueeze(1).broadcast_to(o), ALU.mult).then_inc(vb_ready, 1)
                else:
                    o = [P, 4, 4, 32]
                    for t in range(TT):
                        last = pool.tensor_tensor(
                            vb[:, par, t * 512:(t + 1) * 512].rearrange("p (u q d) -> p u q d", u=4, q=4),
                            v_f[:, t].rearrange("p (q d) -> p q d", q=4).unsqueeze(1).broadcast_to(o),
                            own[:].unsqueeze(2).broadcast_to(o), ALU.mult)
                    last.then_inc(vb_ready, 1)

            def mask(n, g):
                pool.wait_ge(exp_done, 2 * n + 1 + g)
                wait(pool, pv_done, 2 * n - 1 + g)
                pool.tensor_tensor(pm[:, g], pt[:, g, :, g * P:(g + 1) * P],
                                   K["tri_post"][:].unsqueeze(1).broadcast_to([P, 4, P]), ALU.mult)\
                    .then_inc(pm_ready, 1)

            def emit(at):
                n, b, u, pos = at(0)
                nn, bn, un, posn = at(1)
                n2, b2, u2, pos2 = at(2)
                n3, b3, u3, pos3 = at(3)
                ln = inside(n3) and u3 == 0
                first = inside(nn) and (per_unit or un == 0)
                m = pset(nn, bn)
                par_m = (posn % 2) if (per_unit or U == 1) else (posn // U) % 2
                if first:
                    wait(pool, st_ready, 2 * (m - 1) if (per_unit or U == 1) else 2 * U * (m - 1))
                    split(m, par_m, k_f, k_hi, k_lo, "k", k_split)
                    split(m, par_m, q_f, q_hi, q_lo, "q", q_split)
                if U == 1 and inside(n2):
                    wait(pool, proj_done, NU * (b2 - 1))
                    context(b2, pos2)
                if pm is not None and inside(n):
                    mask(n, 0)
                if inside(nn):
                    pool.wait_ge(k_split, m + 1)
                    wait(pool, st_ready, 2 * (nn - 1))
                    spread_keys(pool, kb_lo, k_lo, nn, bn, un, posn).then_inc(kb_lo_ready, 1)
                if first and not per_unit:
                    lay_values(m, par_m)
                for i in range(NLN if ln else 0):
                    rstds(b3, i)
                if pm is not None and inside(n):
                    mask(n, 1)

            run(pool, emit)
NT = NB * TT
NTOK = NB * T
CH = 512
NCH = NTOK // CH
CT = CH // P


@phase
def prepare(nc, name, K, x, x_hi, x_lo, *, affine=None, gate=None, tokens=None):
    with ExitStack() as ctx:
        def sb(nm, shape, dt=F32):
            return ctx.enter_context(nc.sbuf_tensor(f"{name}_{nm}", shape, dt))

        def sem(nm):
            return nc.alloc_semaphore(f"{name}_{nm}")

        st6, mv = sb("st6", [P, CT, 6]), sb("mv", [P, 2, CT, 2])
        veps, rstd = sb("veps", [P, 2, CT]), sb("rstd", [P, 2, CT])
        xn = sb("xn", [P, 2, CT, P])
        x_t = sb("x_t", [P, 2, CH])
        ga = (sb("gain", [P, 1]), sb("bias", [P, 1])) if affine else None
        psum_t = [ctx.enter_context(nc.psum_tensor(f"{name}_t{i}", [P, CH], F32)) for i in range(2)]
        loaded, stats, vstep = sem("loaded"), sem("stats"), sem("vstep")
        pstep, rstd_ready, xn_ready = sem("pstep"), sem("rstd_ready"), sem("xn_ready")
        turned, x_t_ready, hi_ready, lo_ready = sem("turned"), sem("x_t_ready"), sem("hi_ready"), sem("lo_ready")
        kept = sem("kept")
        n_loads = 2 if affine else 0
        if gate:
            topk = gate["rule"] == "topk"
            by_expert = "we_t" in gate
            gw = sb("gw", [P, NE])
            gb = sb("gb", [P, NE]) if gate["b"] is not None else None
            lt = sb("lt", [P, CT, NE])
            m8, i8 = sb("m8", [P, CT, 8]), sb("i8", [P, CT, 8], U32)
            logits = sb("logits", [P, NT, NE])
            tops = sb("tops", [P, NT, 8])
            picks = sb("picks", [P, NT, 8])
            d1, e1, s1, p0, p1 = (sb(n, [P, NT]) for n in ("d1", "e1", "s1", "p0", "p1"))
            w0, w1 = sb("w0", [P, NT, NE]), sb("w1", [P, NT, NE])
            iota = sb("iota", [P, NE])
            psum_l = ctx.enter_context(nc.psum_tensor(f"{name}_l", [P, CT, NE], F32))
            l_ready, l_read, gstep, cstep = sem("l_ready"), sem("l_read"), sem("gstep"), sem("cstep")
            exp_ready, iota_ready, we_ready = sem("exp_ready"), sem("iota_ready"), sem("we_ready")
            n_loads += 1 + (gb is not None)
            if by_expert:
                eb = sb("eb", [NE, P])
                psum_w = [ctx.enter_context(nc.psum_tensor(f"{name}_pw{i}", [P, CH], F32)) for i in range(2)]
                psum_b = [ctx.enter_context(nc.psum_tensor(f"{name}_pb{i}", [P, CH], F32)) for i in range(2)]
                w_turned, w_copied, b_done, b_copied, stored = (
                    sem(n) for n in ("w_turned", "w_copied", "b_done", "b_copied", "stored"))
                n_loads += 1

        def run(emit):
            def body(i, last):
                emit(2 * i, 0, 2 * i + 1, None if last else 2 * i + 2)
                emit(2 * i + 1, 1, *((None, None) if last else (2 * i + 2, 2 * i + 3)))
            return body

        def loop(eng, emit):
            body = run(emit)
            body(0, False)
            with eng.Fori(1, NCH // 2 - 1) as i:
                body(i, False)
            body(NCH // 2 - 1, True)

        block = ctx.enter_context(nc.Block())

        @block.sync
        def _(sp):
            if affine:
                for a, t in zip(affine, ga):
                    sp.dma_start(t[:], column(a)).then_inc(loaded, 16)
            if gate:
                sp.dma_start(gw[:], gate["w"]).then_inc(loaded, 16)
                if gb is not None:
                    sp.dma_start(gb[:], bcast_row(gate["b"])).then_inc(loaded, 16)
                if by_expert:
                    sp.dma_start(eb[:], gate["bias"]).then_inc(loaded, 16)
                    if not gate["by_token"]:
                        sp.wait_ge(w_copied, NCH)
                        sp.dma_start(gate["dram"], gate["we_t"][:]).then_inc(stored, 16)
                        sp.wait_ge(stored, 16)

        @block.vector
        def _(dve):
            def statistics(c, par):
                wait(dve, stats, c)
                wait(dve, xn_ready, c - 1)
                dve.sem_inc(K["passed"], 1)
                for t in range(CT):
                    last = dve.bn_stats(st6[:, t, :], x[:, bass.ds(c * CT, CT), :][:, t, :])
                last.then_inc(vstep, 1)
                dve.wait_ge(vstep, c + 1)
                dve.sem_inc(K["passed"], 1)
                for t in range(CT):
                    last = dve.bn_aggr(mv[:, par, t, :], st6[:, t, :])
                last.then_inc(stats, 1)

            def norm(c, par):
                src = x[:, bass.ds(c * CT, CT), :]
                dve.wait_ge(rstd_ready, c + 1)
                wait(dve, turned, c - 1)
                if tokens is not None:
                    wait(dve, kept, c - 1)
                for t in range(CT):
                    last = dve.tensor_scalar(xn[:, par, t, :], src[:, t, :], mv[:, par, t, 0:1],
                                             rstd[:, par, t:t + 1], ALU.subtract, ALU.mult)
                last.then_inc(xn_ready, 1)

            def choose(c):
                dve.wait_ge(l_ready, c + 1)
                if gb is not None:
                    dve.tensor_tensor(lt[:], psum_l[:], gb[:].unsqueeze(1).broadcast_to([P, CT, NE]), ALU.add)\
                       .then_inc(l_read, 1)
                else:
                    dve.tensor_copy(lt[:], psum_l[:]).then_inc(l_read, 1)
                dve.wait_ge(l_read, c + 1)
                dve.tensor_copy(logits[:, bass.ds(c * CT, CT), :], lt[:])
                dve.sem_inc(K["passed"], 1)
                for t in range(CT):
                    last = dve.max(m8[:, t, :], lt[:, t, :])
                last.then_inc(gstep, 1)
                dve.wait_ge(gstep, 2 * c + 1)
                dve.tensor_copy(tops[:, bass.ds(c * CT, CT), :], m8[:])
                if topk:
                    dve.sem_inc(K["passed"], 1)
                    for t in range(CT):
                        last = dve.max_index(i8[:, t, :], m8[:, t, :], lt[:, t, :])
                    last.then_inc(gstep, 1)
                    dve.wait_ge(gstep, 2 * c + 2)
                    dve.tensor_copy(picks[:, bass.ds(c * CT, CT), :], i8[:]).then_inc(cstep, 1)
                else:
                    dve.sem_inc(gstep, 1)
                    dve.tensor_copy(picks[:, bass.ds(c * CT, CT), :], m8[:]).then_inc(cstep, 1)

            statistics(0, 0)
            statistics(1, 1)
            norm(0, 0)

            def emit(c, par, nxt, after):
                if nxt is not None:
                    norm(nxt, 1 - par)
                if after is not None:
                    statistics(after, par)
                dve.wait_ge(hi_ready, c + 1)
                dve.tensor_tensor(x_lo[:, bass.ds(c * CH, CH)], x_t[:, par],
                                  x_hi[:, bass.ds(c * CH, CH)].bitcast(F32), ALU.subtract).then_inc(lo_ready, 1)
                if gate and not (isinstance(c, int) and c == 0):
                    choose(c - 1)

            loop(dve, emit)
            if gate:
                choose(NCH - 1)
                dve.wait_ge(cstep, NCH)
                n = NCH
                o = [P, NT, NE]
                weights = gate["weights"]

                def chain(ins):
                    nonlocal n
                    n += 1
                    ins.then_inc(cstep, 1)
                    dve.wait_ge(cstep, n)

                if topk:
                    dve.tensor_tensor(d1[:], tops[:, :, 1], tops[:, :, 0], ALU.subtract).then_inc(we_ready, 1)
                    dve.wait_ge(exp_ready, 1)
                    dve.wait_ge(iota_ready, NE)
                    chain(dve.tensor_scalar(s1[:], e1[:], 1.0, None, ALU.add))
                    chain(dve.reciprocal(p0[:], s1[:]))
                    chain(dve.tensor_tensor(p1[:], p0[:], e1[:], ALU.mult))
                    it = iota[:].unsqueeze(1).broadcast_to(o)
                    for k, (w, p_) in enumerate(((w0, p0), (w1, p1))):
                        chain(dve.tensor_tensor(w[:], it, picks[:, :, k:k + 1].broadcast_to(o), ALU.is_equal))
                        chain(dve.tensor_tensor(w[:], w[:], p_[:].unsqueeze(2).broadcast_to(o), ALU.mult))
                    chain(dve.tensor_tensor(weights[:], w0[:], w1[:], ALU.add))
                else:
                    dve.tensor_tensor(w0[:], logits[:], tops[:, :, 0:1].broadcast_to(o), ALU.subtract)\
                       .then_inc(we_ready, 1)
                    dve.wait_ge(exp_ready, 1)
                    chain(dve.tensor_tensor(w0[:], logits[:], tops[:, :, 1:2].broadcast_to(o), ALU.is_ge))
                    chain(dve.tensor_tensor(w0[:], w0[:], w1[:], ALU.mult))
                    chain(dve.reduce_sum(s1[:], w0[:], AX.X))
                    chain(dve.reciprocal(p0[:], s1[:]))
                    chain(dve.tensor_tensor(weights[:], w0[:], p0[:].unsqueeze(2).broadcast_to(o), ALU.mult))
                dve.sem_inc(we_ready, 1)
                for c in range(NCH if by_expert else 0):
                    dve.wait_ge(b_done, c + 1)
                    dve.tensor_copy(gate["acc"][:, c * CH:(c + 1) * CH], psum_b[c % 2][:]).then_inc(b_copied, 1)

        @block.gpsimd
        def _(pool):
            if gate and topk:
                for e in range(NE):
                    pool.memset(iota[:, e:e + 1], float(e)).then_inc(iota_ready, 1)

            def rstds(c, par):
                pool.wait_ge(stats, c + 1)
                pool.sem_inc(K["passed"], 1)
                pool.tensor_scalar(veps[:, par], mv[:, par, :, 1], EPS, None, ALU.add).then_inc(pstep, 1)
                pool.wait_ge(pstep, c + 1)
                pool.tensor_tensor(rstd[:, par], veps[:, par], K["half"][:, 0:CT], ALU.pow).then_inc(rstd_ready, 1)

            rstds(0, 0)
            rstds(1, 1)

            def emit(c, par, nxt, after):
                if after is not None:
                    rstds(after, par)
                if tokens is not None:
                    pool.wait_ge(xn_ready, c + 1)
                    pool.sem_inc(K["passed"], 1)
                    pool.tensor_copy(tokens[:, bass.ds(c * CT, CT), :], xn[:, par]).then_inc(kept, 1)

            loop(pool, emit)

        @block.scalar
        def _(act):
            if n_loads:
                act.wait_ge(loaded, 16 * n_loads)

            def emit(c, par, nxt, after):
                act.wait_ge(turned, c + 1)
                wait(act, lo_ready, c - 1)
                act.activation(x_t[:, par], psum_t[par][:], ACT.Identity, scale=ga[0][:] if ga else 1.0,
                               bias=ga[1][:] if ga else 0.0).then_inc(x_t_ready, 1)
                act.wait_ge(x_t_ready, c + 1)
                act.sem_inc(K["passed"], 1)
                act.activation(x_hi[:, bass.ds(c * CH, CH)], x_t[:, par], ACT.Identity).then_inc(hi_ready, 1)

            loop(act, emit)
            if gate:
                act.wait_ge(we_ready, 1)
                if topk:
                    act.activation(e1[:], d1[:], ACT.Exp).then_inc(exp_ready, 1)
                else:
                    act.activation(w1[:], w0[:], ACT.Exp).then_inc(exp_ready, 1)
                if by_expert:
                    for c in range(NCH):
                        act.wait_ge(w_turned, c + 1)
                        act.activation(gate["we_t"][:, c * CH:(c + 1) * CH], psum_w[c % 2][0:NE, :], ACT.Identity)\
                           .then_inc(w_copied, 1)

        @block.tensor
        def _(pe):
            if n_loads:
                pe.wait_ge(loaded, 16 * n_loads)

            def turn(c, par):
                pe.wait_ge(xn_ready, c + 1)
                wait(pe, x_t_ready, c - 1)
                for t in range(CT):
                    last = pe.transpose(psum_t[par][:, t * P:(t + 1) * P], xn[:, par, t, :], K["ident"][:])
                last.then_inc(turned, 1)

            turn(0, 0)

            def emit(c, par, nxt, after):
                if nxt is not None:
                    turn(nxt, 1 - par)
                if gate:
                    pe.wait_ge(x_t_ready, c + 1)
                    wait(pe, l_read, c)
                    for t in range(CT):
                        last = pe.matmul(psum_l[:, t, :], x_t[:, par, t * P:(t + 1) * P], gw[:],
                                         start=True, stop=True)
                    last.then_inc(l_ready, 1)

            loop(pe, emit)
            if gate and by_expert:
                pe.wait_ge(we_ready, 2)

                def turn_weights(c):
                    if c >= 2:
                        pe.wait_ge(w_copied, c - 1)
                    for t in range(CT):
                        last = pe.transpose(psum_w[c % 2][0:NE, t * P:(t + 1) * P], gate["weights"][:, c * CT + t, :],
                                            K["ident"][:])
                    last.then_inc(w_turned, 1)

                turn_weights(0)
                for c in range(NCH):
                    if c + 1 < NCH:
                        turn_weights(c + 1)
                    pe.wait_ge(w_copied, c + 1)
                    if c >= 2:
                        pe.wait_ge(b_copied, c - 1)
                    if gate["by_token"]:
                        for t in range(CT):
                            tok = c * CH + t * P
                            last = pe.matmul(psum_b[c % 2][:, t * P:(t + 1) * P], gate["we_t"][:, tok:tok + P], eb[:],
                                             start=True, stop=True)
                        last.then_inc(b_done, 1)
                    else:
                        pe.matmul(psum_b[c % 2][:], eb[:], gate["we_t"][:, c * CH:(c + 1) * CH],
                                  start=True, stop=True).then_inc(b_done, 1)


def experts(nc, name, K, x_hi, x_lo, acc, *, kind, weights, biases, last_bias=None, we_dram=None):
    glu = kind == "glu"
    E_, _, WB = weights.shape
    BLK = WB // P
    gated = we_dram is not None
    N = E_ * NCH
    PER = 2 * NCH if gated else 2
    HB = 2 if glu else 4
    with ExitStack() as ctx:
        def sb(nm, shape, dt=F32):
            return ctx.enter_context(nc.sbuf_tensor(f"{name}_{nm}", shape, dt))

        def sem(nm):
            return nc.alloc_semaphore(f"{name}_{nm}")

        WBUF = 2 if gated else 1
        raw = sb("raw", [P, WBUF, WB])
        w_hi, w_lo = sb("w_hi", [P, WBUF, WB], F32R), sb("w_lo", [P, WBUF, WB], F32R)
        bias = sb("bias", [P, biases.shape[1]])
        lb = sb("lb", [P, 1]) if last_bias is not None else None
        BC = biases.shape[1] // E_
        if glu:
            a_s, z = sb("a_s", [P, 2, CH]), sb("z", [P, 2, CH])
            z_hi, z_lo = sb("z_hi", [P, 2, 2, CH], F32R), sb("z_lo", [P, 2, 2, CH], F32R)
        h = sb("h", [P, HB, CH])
        h_hi, h_lo = sb("h_hi", [P, 2, HB, CH], F32R), sb("h_lo", [P, 2, HB, CH], F32R)
        wrow = sb("wrow", [P, 2, CH]) if gated else None
        tmp = sb("tmp", [P, 2, CH]) if gated else None
        NF = 4
        psum_f = [ctx.enter_context(nc.psum_tensor(f"{name}_f{i}", [P, CH], F32)) for i in range(NF)]
        psum_g = [ctx.enter_context(nc.psum_tensor(f"{name}_g{i}", [P, CH], F32)) for i in range(2)] if glu else None
        psum_y = [ctx.enter_context(nc.psum_tensor(f"{name}_y{i}", [P, CH], F32)) for i in range(2)]

        loaded, w_loaded = sem("loaded"), [sem(f"w_loaded{i}") for i in range(WBUF)]
        w_high, w_split = sem("w_high"), sem("w_split")
        first_done = sem("first_done")
        a_ready, z_ready, z_high, z_split = sem("a_ready"), sem("z_ready"), sem("z_high"), sem("z_split")
        g_done = sem("g_done")
        h_ready, h_high, h_split = sem("h_ready"), sem("h_high"), sem("h_split")
        y_done, y_read, added = sem("y_done"), sem("y_read"), sem("added")
        row_loaded = [sem(f"row_loaded{i}") for i in range(2)] if gated else None
        PIECES = 5 if BLK == 10 else 4
        PW = WB // PIECES

        def run(eng, emit):
            def at_of(i, j):
                def at(k):
                    jj = j + k
                    if gated:
                        return PER * i + jj, 2 * i + jj // NCH, jj % NCH, jj % PER
                    return PER * i + jj, 0, PER * i + jj, jj % PER
                return at
            reps = N // PER
            emit(at_of(0, -1))
            for j in range(PER):
                emit(at_of(0, j))
            if reps > 2:
                with eng.Fori(1, reps - 1) as i:
                    for j in range(PER):
                        emit(at_of(i, j))
            for j in range(PER + 1):
                emit(at_of(reps - 1, j))

        def inside(n):
            return not isinstance(n, int) or 0 <= n < N

        block = ctx.enter_context(nc.Block())

        @block.sync
        def _(sp):
            sp.dma_start(bias[:], biases).then_inc(loaded, 16)
            if lb is not None:
                sp.dma_start(lb[:], column(last_bias)).then_inc(loaded, 16)

            def load(e, par):
                wait(sp, w_split, (e - 1) * PIECES)
                sp.dma_start(raw[:, par, :], weights[bass.ds(e, 1), :, :].rearrange("a p n -> p (a n)"))\
                  .then_inc(w_loaded[par], 16)

            load(0, 0)
            if gated:
                load(1, 1)

            def emit(at):
                n, e, c, pos = at(1)
                if gated and inside(n):
                    wait(sp, y_read, n - 1)
                    sp.dma_start(wrow[:, pos % 2, :],
                                 we_dram[bass.ds(e, 1), c * CH:(c + 1) * CH].broadcast_to([P, CH]))\
                      .then_inc(row_loaded[pos % 2], 16)
                n, e, c, pos = at(0)
                if gated and inside(n) and c == NCH - 1 and not (isinstance(e, int) and e + 2 >= E_):
                    load(e + 2, (pos // NCH) % 2)

            run(sp, emit)

        @block.tensor
        def _(pe):
            pe.wait_ge(loaded, 16 if lb is None else 32)

            def triple(dst, wpar, blk, hi, lo, start, stop):
                cols = slice(blk * P, (blk + 1) * P)
                pe.matmul(dst, w_hi[:, wpar, cols], hi, start=start, stop=False)
                pe.matmul(dst, w_lo[:, wpar, cols], hi, start=False, stop=False)
                return pe.matmul(dst, w_hi[:, wpar, cols], lo, start=False, stop=stop)

            def first(n, e, c, pos):
                wpar = (pos // NCH) % 2 if gated else 0
                if isinstance(c, int) and c == 0:
                    pe.wait_ge(w_split, (e + 1) * PIECES)
                xs = bass.ds(c * CH, CH)
                for i in range(NF):
                    if glu:
                        wait(pe, a_ready if i % 2 == 0 else z_ready, 2 * n - 1 + i // 2)
                    else:
                        wait(pe, h_ready, 4 * (n - 1) + i + 1)
                    triple(psum_f[i][:], wpar, i, x_hi[:, xs], x_lo[:, xs], True, True).then_inc(first_done, 1)

            def middle(n, e, c, pos):
                wpar = (pos // NCH) % 2
                for g in range(2):
                    wait(pe, h_ready, 2 * n - 1 + g)
                    for j in range(2):
                        pe.wait_ge(z_split, 2 * n + 1 + j)
                        last = triple(psum_g[g][:], wpar, 4 + 2 * j + g, z_hi[:, pos % 2, j], z_lo[:, pos % 2, j], j == 0, j == 1)
                    last.then_inc(g_done, 1)

            def final(n, e, c, pos):
                wpar = (pos // NCH) % 2 if gated else 0
                wait(pe, y_read, n - 1)
                for j in range(HB):
                    pe.wait_ge(h_split, HB * n + j + 1)
                    last = triple(psum_y[pos % 2][:], wpar, BLK - HB + j, h_hi[:, pos % 2, j], h_lo[:, pos % 2, j],
                                  j == 0, j == HB - 1)
                last.then_inc(y_done, 1)

            def emit(at):
                n, e, c, pos = at(1)
                if inside(n):
                    first(n, e, c, pos)
                if glu:
                    n, e, c, pos = at(-1)
                    if inside(n):
                        final(n, e, c, pos)
                    n, e, c, pos = at(0)
                    if inside(n):
                        middle(n, e, c, pos)
                else:
                    n, e, c, pos = at(0)
                    if inside(n):
                        final(n, e, c, pos)

            run(pe, emit)

        @block.scalar
        def _(act):
            act.wait_ge(loaded, 16 if lb is None else 32)

            def col(e, k):
                if isinstance(e, int):
                    return bias[:, e * BC + k:e * BC + k + 1]
                return bias[:, bass.ds(e * BC + k, 1)]

            def emit(at):
                n, e, c, pos = at(1)
                if inside(n) and glu:
                    for j in range(2):
                        act.wait_ge(first_done, 4 * n + 2 * j + 1)
                        wait(act, z_ready, 2 * n - 1 + j)
                        act.sem_inc(K["passed"], 1)
                        act.activation(a_s[:, j], psum_f[2 * j][:], ACT.Identity, bias=col(e, j)).then_inc(a_ready, 1)
                if inside(n) and not glu:
                    for j in range(4):
                        act.wait_ge(first_done, 4 * n + j + 1)
                        wait(act, h_split, 4 * (n - 1) + j + 1)
                        act.sem_inc(K["passed"], 1)
                        act.activation(h[:, j], psum_f[j][:], ACT.Gelu, bias=col(e, j)).then_inc(h_ready, 1)
                n, e, c, pos = at(0)
                if inside(n) and glu:
                    for g in range(2):
                        act.wait_ge(g_done, 2 * n + 1 + g)
                        wait(act, h_split, 2 * n - 1 + g)
                        act.sem_inc(K["passed"], 1)
                        act.activation(h[:, g], psum_g[g][:], ACT.Silu, bias=col(e, 4 + g)).then_inc(h_ready, 1)
                        act.wait_ge(h_ready, 2 * n + 1 + g)
                        wait(act, y_done, n - 1)
                        act.activation(h_hi[:, pos % 2, g], h[:, g], ACT.Identity).then_inc(h_high, 1)

            run(act, emit)

        @block.vector
        def _(dve):
            dve.wait_ge(loaded, 16 if lb is None else 32)

            def col(e, k):
                if isinstance(e, int):
                    return bias[:, e * BC + k:e * BC + k + 1]
                return bias[:, bass.ds(e * BC + k, 1)]

            def outputs(n, e, c, pos):
                dve.wait_ge(y_done, n + 1)
                if gated:
                    dve.wait_ge(row_loaded[pos % 2], row_count(n, pos))
                    wait(dve, added, n - 1)
                    dve.tensor_tensor(tmp[:, pos % 2], psum_y[pos % 2][:], wrow[:, pos % 2, :], ALU.mult)\
                       .then_inc(y_read, 1)
                else:
                    dve.tensor_scalar(acc[:, bass.ds(c * CH, CH)], psum_y[pos % 2][:], lb[:], None, ALU.add)\
                       .then_inc(y_read, 1)

            def row_count(n, pos):
                return 8 * n + (16 if pos % 2 == 0 else 8)

            def emit(at):
                n, e, c, pos = at(-1 if glu else 0)
                if inside(n):
                    outputs(n, e, c, pos)
                n, e, c, pos = at(1)
                if inside(n) and glu:
                    for j in range(2):
                        dve.wait_ge(a_ready, 2 * n + 1 + j)
                        dve.wait_ge(first_done, 4 * n + 2 * j + 2)
                        dve.scalar_tensor_tensor(out=z[:, j], in0=psum_f[2 * j + 1][:], scalar=col(e, 2 + j),
                                                 in1=a_s[:, j], op0=ALU.add, op1=ALU.mult).then_inc(z_ready, 1)
                        dve.wait_ge(z_ready, 2 * n + 1 + j)
                        wait(dve, g_done, 2 * (n - 1))
                        dve.tensor_copy(z_hi[:, pos % 2, j], z[:, j]).then_inc(z_high, 1)
                        dve.wait_ge(z_high, 2 * n + 1 + j)
                        dve.tensor_tensor(z_lo[:, pos % 2, j], z[:, j], z_hi[:, pos % 2, j].bitcast(F32), ALU.subtract)\
                           .then_inc(z_split, 1)
                if inside(n) and not glu:
                    for j in range(4):
                        dve.wait_ge(h_ready, 4 * n + j + 1)
                        wait(dve, y_done, n - 1)
                        dve.tensor_copy(h_hi[:, pos % 2, j], h[:, j]).then_inc(h_high, 1)
                        dve.wait_ge(h_high, 4 * n + j + 1)
                        dve.tensor_tensor(h_lo[:, pos % 2, j], h[:, j], h_hi[:, pos % 2, j].bitcast(F32), ALU.subtract)\
                           .then_inc(h_split, 1)
                n, e, c, pos = at(0)
                if inside(n) and glu:
                    for g in range(2):
                        dve.wait_ge(h_high, 2 * n + 1 + g)
                        dve.tensor_tensor(h_lo[:, pos % 2, g], h[:, g], h_hi[:, pos % 2, g].bitcast(F32), ALU.subtract)\
                           .then_inc(h_split, 1)

            run(dve, emit)

        @block.gpsimd
        def _(pool):
            def split(e, par, i):
                if i == 0:
                    cnt = 8 * e + (16 if par == 0 else 8) if gated else 16
                    pool.wait_ge(w_loaded[par if gated else 0], cnt)
                    wait(pool, y_done, NCH * (e - 1))
                    pool.sem_inc(K["passed"], 1)
                cols = slice(i * PW, (i + 1) * PW)
                pool.tensor_copy(w_hi[:, par, cols], raw[:, par, cols]).then_inc(w_high, 1)
                pool.wait_ge(w_high, e * PIECES + i + 1)
                pool.tensor_tensor(w_lo[:, par, cols], raw[:, par, cols], w_hi[:, par, cols].bitcast(F32),
                                   ALU.subtract).then_inc(w_split, 1)

            for i in range(PIECES):
                split(0, 0, i)

            def emit(at):
                n, e, c, pos = at(-1 if glu else 0)
                if gated and inside(n):
                    pool.wait_ge(y_read, n + 1)
                    pool.tensor_tensor(acc[:, bass.ds(c * CH, CH)], tmp[:, pos % 2], acc[:, bass.ds(c * CH, CH)],
                                       ALU.add).then_inc(added, 1)
                n, e, c, pos = at(0)
                if gated and inside(n) and 2 <= c < 2 + PIECES and not (isinstance(e, int) and e + 1 >= E_):
                    split(e + 1, (pos // NCH + 1) % 2, c - 2)

            run(pool, emit)


@phase
def add_turned(nc, name, K, acc, base, out, more=()):
    with ExitStack() as ctx:
        def sem(nm):
            return nc.alloc_semaphore(f"{name}_{nm}")

        banks = [ctx.enter_context(nc.psum_tensor(f"{name}_p{i}", [P, CT, P], F32)) for i in range(4)]
        turned, summed, added = sem("turned"), sem("summed"), sem("added")
        block = ctx.enter_context(nc.Block())

        @block.tensor
        def _(pe):
            for c in range(NCH):
                if c >= 4:
                    pe.wait_ge(added, c - 3)
                for t in range(CT):
                    last = pe.transpose(banks[c % 4][:, t, :], acc[:, (c * CT + t) * P:(c * CT + t + 1) * P],
                                        K["ident"][:])
                last.then_inc(turned, 1)

        @block.gpsimd
        def _(pool):
            for k, other in enumerate((base, *more[1:]) if more else ()):
                for c in range(NCH):
                    tiles = slice(c * CT, (c + 1) * CT)
                    if k:
                        pool.wait_ge(summed, (k - 1) * NCH + c + 1)
                    pool.tensor_tensor(more[0][:, tiles, :], more[0][:, tiles, :], other[:, tiles, :], ALU.add)\
                        .then_inc(summed, 1)

        @block.vector
        def _(dve):
            for c in range(NCH):
                tiles = slice(c * CT, (c + 1) * CT)
                if more:
                    dve.wait_ge(summed, (len(more) - 1) * NCH + c + 1)
                dve.wait_ge(turned, c + 1)
                dve.tensor_tensor(out[:, tiles, :], banks[c % 4][:], (more[0] if more else base)[:, tiles, :],
                                  ALU.add).then_inc(added, 1)
            dve.wait_ge(added, NCH)


@phase
def experts_normed(nc, name, K, x_hi, x_lo, tokens, route, acc, x, *, weights, biases, out_biases, gains, eps):
    N = NE * NCH
    PER = 2 * NCH
    with ExitStack() as ctx:
        def sb(nm, shape, dt=F32):
            return ctx.enter_context(nc.sbuf_tensor(f"{name}_{nm}", shape, dt))

        def sem(nm):
            return nc.alloc_semaphore(f"{name}_{nm}")

        raw = sb("raw", [P, 2, 4 * P])
        w_hi, w_lo = sb("w_hi", [P, 2, 2 * P], F32R), sb("w_lo", [P, 2, 2 * P], F32R)
        bias = sb("bias", [P, 2 * NE])
        b2 = sb("b2", [P, NE, P])
        gain = sb("gain", [P, NE, P])
        h = sb("h", [P, 2, 2, CH])
        xb = sb("xb", [P, 2, CT, P])
        y = sb("y", [P, 2, CT, P])
        st6, mv = sb("st6", [P, CT, 6]), sb("mv", [P, 2, CT, 2])
        veps, rstd, rw = sb("veps", [P, CT]), sb("rstd", [P, CT]), sb("rw", [P, 2, CT])
        nm, nb = sb("nm", [P, CT]), sb("nb", [P, 2, CT])
        u, tmp = sb("u", [P, 2, CT, P]), sb("tmp", [P, CT, P])
        psum_f = [ctx.enter_context(nc.psum_tensor(f"{name}_f{i}", [P, CH], F32)) for i in range(4)]
        psum_o = [ctx.enter_context(nc.psum_tensor(f"{name}_o{i}", [P, CT, P], F32)) for i in range(2)]

        loaded, w_loaded = sem("loaded"), [sem(f"w_loaded{i}") for i in range(2)]
        w_high, w_split = sem("w_high"), sem("w_split")
        first_done, h_ready, o_done = sem("first_done"), sem("h_ready"), sem("o_done")
        xb_ready, y_ready, stepped, stats = sem("xb_ready"), sem("y_ready"), sem("stepped"), sem("stats")
        pstep, rw_ready, u_ready, tmp_ready, added = (
            sem("pstep"), sem("rw_ready"), sem("u_ready"), sem("tmp_ready"), sem("added"))
        finished = sem("finished")

        def run(eng, emit):
            def at_of(i, j):
                def at(k):
                    jj = j + k
                    return PER * i + jj, 2 * i + jj // NCH, jj % NCH, jj % PER
                return at
            for j in range(-1, PER):
                emit(at_of(0, j))
            with eng.Fori(1, N // PER - 1) as i:
                for j in range(PER):
                    emit(at_of(i, j))
            for j in range(PER + 2):
                emit(at_of(N // PER - 1, j))

        def inside(n):
            return not isinstance(n, int) or 0 <= n < N

        block = ctx.enter_context(nc.Block())

        @block.sync
        def _(sp):
            sp.dma_start(bias[:], biases).then_inc(loaded, 16)
            sp.dma_start(b2[:].rearrange("p e d -> p (e d)"), bcast_row(out_biases)).then_inc(loaded, 16)
            sp.dma_start(gain[:].rearrange("p e d -> p (e d)"), bcast_row(gains)).then_inc(loaded, 16)

            def load(e, par):
                wait(sp, o_done, NCH * (e - 1))
                wait(sp, w_split, e - 1)
                sp.dma_start(raw[:, par, :], weights[bass.ds(e, 1), :, :].rearrange("a p n -> p (a n)"))\
                  .then_inc(w_loaded[par], 16)

            load(0, 0)
            load(1, 1)

            def emit(at):
                n, e, c, pos = at(0)
                if inside(n) and c == NCH - 1 and not (isinstance(e, int) and e + 2 >= NE):
                    load(e + 2, (pos // NCH) % 2)

            run(sp, emit)

        @block.tensor
        def _(pe):
            pe.wait_ge(loaded, 48)

            def emit(at):
                n, e, c, pos = at(1)
                if inside(n):
                    par = (pos // NCH) % 2
                    if c == 0:
                        pe.wait_ge(w_split, e + 1)
                    for j in range(2):
                        dst = psum_f[2 * (pos % 2) + j][:]
                        wait(pe, h_ready, 2 * (n - 2) + j + 1)
                        cols, xs = slice(j * P, (j + 1) * P), slice(c * CH, (c + 1) * CH)
                        pe.matmul(dst, w_hi[:, par, cols], x_hi[:, xs], start=True, stop=False)
                        pe.matmul(dst, w_lo[:, par, cols], x_hi[:, xs], start=False, stop=False)
                        pe.matmul(dst, w_hi[:, par, cols], x_lo[:, xs], start=False, stop=True)\
                          .then_inc(first_done, 1)
                n, e, c, pos = at(0)
                if inside(n):
                    par = (pos // NCH) % 2
                    pe.wait_ge(h_ready, 2 * n + 2)
                    wait(pe, y_ready, n - 1)
                    for t in range(CT):
                        for j in range(2):
                            last = pe.matmul(psum_o[pos % 2][:, t, :], h[:, pos % 2, j, t * P:(t + 1) * P],
                                             raw[:, par, (2 + j) * P:(3 + j) * P], start=j == 0, stop=j == 1)
                    last.then_inc(o_done, 1)

            run(pe, emit)

        @block.scalar
        def _(act):
            act.wait_ge(loaded, 48)

            def emit(at):
                n, e, c, pos = at(1)
                if inside(n):
                    for j in range(2):
                        act.wait_ge(first_done, 2 * n + j + 1)
                        wait(act, o_done, n - 1)
                        col = bias[:, 2 * e + j:2 * e + j + 1] if isinstance(e, int) else bias[:, bass.ds(2 * e + j, 1)]
                        act.sem_inc(K["passed"], 1)
                        act.activation(h[:, pos % 2, j], psum_f[2 * (pos % 2) + j][:], ACT.Gelu, bias=col)\
                           .then_inc(h_ready, 1)
                n, e, c, pos = at(-1)
                if inside(n):
                    par = pos % 2
                    act.wait_ge(rw_ready, n + 1)
                    wait(act, tmp_ready, n - 1)
                    act.sem_inc(K["passed"], 1)
                    for t in range(CT):
                        last = act.activation(u[:, par, t, :], y[:, par, t, :], ACT.Identity,
                                              scale=rw[:, par, t:t + 1], bias=nb[:, par, t:t + 1])
                    last.then_inc(u_ready, 1)

            run(act, emit)

        @block.vector
        def _(dve):
            dve.wait_ge(loaded, 48)

            def emit(at):
                n, e, c, pos = at(0)
                if inside(n):
                    par = pos % 2
                    dve.wait_ge(o_done, n + 1)
                    dve.wait_ge(xb_ready, n + 1)
                    wait(dve, u_ready, n - 1)
                    dve.tensor_tensor(y[:, par], psum_o[par][:], xb[:, par], ALU.add).then_inc(y_ready, 1)
                    dve.wait_ge(y_ready, n + 1)
                    dve.sem_inc(K["passed"], 1)
                    for t in range(CT):
                        last = dve.bn_stats(st6[:, t, :], y[:, par, t, :])
                    last.then_inc(stepped, 1)
                    dve.wait_ge(stepped, n + 1)
                    wait(dve, rw_ready, n - 1)
                    dve.sem_inc(K["passed"], 1)
                    for t in range(CT):
                        last = dve.bn_aggr(mv[:, par, t, :], st6[:, t, :])
                    last.then_inc(stats, 1)
                n, e, c, pos = at(-2)
                if inside(n):
                    dve.wait_ge(u_ready, n + 1)
                    wait(dve, added, n)
                    dve.sem_inc(K["passed"], 1)
                    g = gain[:, e:e + 1, :] if isinstance(e, int) else gain[:, bass.ds(e, 1), :]
                    dve.tensor_tensor(tmp[:], u[:, pos % 2], g.broadcast_to([P, CT, P]), ALU.mult)\
                       .then_inc(tmp_ready, 1)
                    dve.wait_ge(tmp_ready, n + 1)
                    a = acc[:, c * CT:(c + 1) * CT, :]
                    dve.tensor_tensor(a, tmp[:], a, ALU.add).then_inc(added, 1)

            run(dve, emit)
            dve.wait_ge(added, N)
            dve.tensor_tensor(x[:], x[:], acc[:], ALU.add).then_inc(finished, 1)
            dve.wait_ge(finished, 1)

        @block.gpsimd
        def _(pool):
            pool.wait_ge(loaded, 48)

            def split(e, par):
                pool.wait_ge(w_loaded[par], 8 * e + (16 if par == 0 else 8))
                wait(pool, first_done, 2 * NCH * (e - 1))
                pool.sem_inc(K["passed"], 1)
                pool.tensor_copy(w_hi[:, par], raw[:, par, 0:2 * P]).then_inc(w_high, 1)
                pool.wait_ge(w_high, e + 1)
                pool.tensor_tensor(w_lo[:, par], raw[:, par, 0:2 * P], w_hi[:, par].bitcast(F32), ALU.subtract)\
                    .then_inc(w_split, 1)

            split(0, 0)

            def emit(at):
                n, e, c, pos = at(1)
                if inside(n):
                    wait(pool, y_ready, n - 1)
                    pool.sem_inc(K["passed"], 1)
                    b = b2[:, e:e + 1, :] if isinstance(e, int) else b2[:, bass.ds(e, 1), :]
                    pool.tensor_tensor(xb[:, pos % 2], tokens[:, c * CT:(c + 1) * CT, :],
                                       b.broadcast_to([P, CT, P]), ALU.add).then_inc(xb_ready, 1)
                n, e, c, pos = at(0)
                if inside(n):
                    par = pos % 2
                    pool.wait_ge(stats, n + 1)
                    pool.sem_inc(K["passed"], 1)
                    pool.tensor_scalar(veps[:], mv[:, par, :, 1], eps, None, ALU.add).then_inc(pstep, 1)
                    pool.wait_ge(pstep, 4 * n + 1)
                    pool.tensor_tensor(rstd[:], veps[:], K["half"][:, 0:CT], ALU.pow).then_inc(pstep, 1)
                    pool.tensor_scalar(nm[:], mv[:, par, :, 0], -1.0, None, ALU.mult).then_inc(pstep, 1)
                    pool.wait_ge(pstep, 4 * n + 3)
                    wait(pool, u_ready, n - 1)
                    pool.sem_inc(K["passed"], 1)
                    w = route[:, c * CT:(c + 1) * CT, e:e + 1] if isinstance(e, int) else \
                        route[:, c * CT:(c + 1) * CT, bass.ds(e, 1)]
                    pool.tensor_tensor(rw[:, par].unsqueeze(2), rstd[:].unsqueeze(2), w, ALU.mult)\
                        .then_inc(pstep, 1)
                    pool.wait_ge(pstep, 4 * n + 4)
                    pool.tensor_tensor(nb[:, par], rw[:, par], nm[:], ALU.mult).then_inc(rw_ready, 1)
                n, e, c, pos = at(0)
                if inside(n) and c == 2 and not (isinstance(e, int) and e + 1 >= NE):
                    split(e + 1, (pos // NCH + 1) % 2)

            run(pool, emit)


@phase
def ternary_mlp(nc, name, K, x, *, w1, w2, b1, b2):
    F = 512
    FB = F // P
    QB = 127.0
    ROUND = 1.5 * 2.0 ** 23
    G = 2
    N = NT // G
    PER = 4
    with ExitStack() as ctx:
        def sb(nm, shape, dt=F32):
            return ctx.enter_context(nc.sbuf_tensor(f"{name}_{nm}", shape, dt))

        def sem(nm):
            return nc.alloc_semaphore(f"{name}_{nm}")

        wf = [sb("w1f", [P, F]), sb("w2f", [P, F])]
        wt = [sb("w1t", [P, F], BF16), sb("w2t", [P, F], BF16)]
        wa, ws, wr, wq = (sb(n, [P, 2]) for n in ("wa", "ws", "wr", "wq"))
        ones, unround = sb("ones", [P, P]), sb("unround", [P, 1])
        b1b, b2b = sb("b1b", [P, F]), sb("b2b", [P, P])
        st6, mv = sb("st6", [P, G, 6]), sb("mv", [P, G, 2])
        veps, rstd = sb("veps", [P, G]), sb("rstd", [P, G])
        xn, xi = sb("xn", [P, G, P]), sb("xi", [P, G, P])
        xq, xq_t = sb("xq", [P, 2, G, P], BF16), sb("xq_t", [P, 2, G, P], BF16)
        xa, xc, xr, xs = (sb(n, [P, G]) for n in ("xa", "xc", "xr", "xs"))
        xd = sb("xd", [P, PER, G])
        hb, h = sb("hb", [P, G, F]), sb("h", [P, 2, G, F])
        hi = sb("hi", [P, G, F])
        hq, hq_t = sb("hq", [P, G, F], BF16), sb("hq_t", [P, 2, G, FB, P], BF16)
        ha, hc, hr, hs = (sb(n, [P, G]) for n in ("ha", "hc", "hr", "hs"))
        hd = sb("hd", [P, 2, G])
        o1 = sb("o1", [P, 2, G, P])
        psum_w = ctx.enter_context(nc.psum_tensor(f"{name}_pw", [P, 2], F32))
        psum_x = ctx.enter_context(nc.psum_tensor(f"{name}_px", [P, G, P], BF16))
        psum_h = [ctx.enter_context(nc.psum_tensor(f"{name}_ph{t}", [P, F], F32)) for t in range(G)]
        psum_t = ctx.enter_context(nc.psum_tensor(f"{name}_pt", [P, G, FB, P], BF16))
        psum_o = ctx.enter_context(nc.psum_tensor(f"{name}_po", [P, G, P], F32))

        loaded, wstep, wsummed, w_ready = sem("loaded"), sem("wstep"), sem("wsummed"), sem("w_ready")
        lstep, stats, pstep, rstd_ready = sem("lstep"), sem("stats"), sem("pstep"), sem("rstd_ready")
        xstep, xi_ready, xq_ready = sem("xstep"), sem("xi_ready"), sem("xq_ready")
        x_turned, xq_t_ready = sem("x_turned"), sem("xq_t_ready")
        h_done, hb_ready, h_ready = sem("h_done"), sem("hb_ready"), sem("h_ready")
        hstep, hi_ready, hq_ready = sem("hstep"), sem("hi_ready"), sem("hq_ready")
        h_turned, hq_t_ready = sem("h_turned"), sem("hq_t_ready")
        o_done, o1_ready, added = sem("o_done"), sem("o1_ready"), sem("added")
        XS, HS = 6, 5

        def run(eng, emit):
            def at_of(base, j):
                return lambda k: (base + j + k, (j + k) % PER)
            for j in range(-3, PER):
                emit(at_of(0, j))
            with eng.Fori(1, N // PER - 1) as i:
                for j in range(PER):
                    emit(at_of(PER * i, j))
            for j in range(PER + 1):
                emit(at_of(N - PER, j))

        def inside(n):
            return not isinstance(n, int) or 0 <= n < N

        block = ctx.enter_context(nc.Block())

        @block.sync
        def _(sp):
            for dst, src in ((wf[0], w1), (wf[1], w2), (b1b, bcast_row(b1)), (b2b, bcast_row(b2))):
                sp.dma_start(dst[:], src).then_inc(loaded, 16)

        @block.vector
        def _(dve):
            dve.memset(unround[:], -ROUND)
            dve.memset(ones[:], 1.0).then_inc(wstep, 1)
            dve.wait_ge(loaded, 64)
            nw = [1]

            def link(ins):
                nw[0] += 1
                ins.then_inc(wstep, 1)
                dve.wait_ge(wstep, nw[0])

            for i in range(2):
                link(dve.tensor_reduce(wa[:, i:i + 1], wf[i][:], AX.X, ALU.add, apply_absolute_value=True))
            dve.wait_ge(wsummed, 1)
            link(dve.tensor_scalar(ws[:], psum_w[:], 1.0 / (F * P), EPS, ALU.mult, ALU.max))
            link(dve.reciprocal(wr[:], ws[:]))
            link(dve.tensor_scalar(wq[:], ws[:], 1.0 / QB, None, ALU.mult))
            for i in range(2):
                link(dve.tensor_scalar(wf[i][:], wf[i][:], wr[:, i:i + 1], ROUND, ALU.mult, ALU.add))
                link(dve.tensor_scalar(wf[i][:], wf[i][:], ROUND, 1.0, ALU.subtract, ALU.min))
                link(dve.tensor_scalar(wt[i][:], wf[i][:], -1.0, None, ALU.max))
            dve.sem_inc(w_ready, 1)

            def rounded(src, a, c, r, s, out, chain, at0, freed):
                k = [0]

                def step(ins):
                    k[0] += 1
                    ins.then_inc(chain, 1)
                    dve.wait_ge(chain, at0 + k[0])

                step(dve.tensor_reduce(a[:], src, AX.X, ALU.max, apply_absolute_value=True))
                step(dve.tensor_scalar(c[:], a[:], EPS, None, ALU.max))
                step(dve.reciprocal(r[:], c[:]))
                step(dve.tensor_scalar(s[:], r[:], QB, None, ALU.mult))
                freed()
                for t in range(G):
                    last = dve.tensor_scalar(out[:, t], src[:, t], s[:, t:t + 1], ROUND, ALU.mult, ALU.add)
                return last

            def scale_of(dst, c, i):
                return dve.tensor_tensor(dst, c[:], wq[:, i:i + 1].broadcast_to([P, G]), ALU.mult)

            def emit(at):
                m, pm = at(1)
                if inside(m):
                    wait(dve, h_ready, m)
                    for t in range(G):
                        dve.wait_ge(h_done, G * m + t + 1)
                        dve.scalar_tensor_tensor(out=hb[:, t], in0=psum_h[t][:], scalar=xd[:, pm, t:t + 1],
                                                 in1=b1b[:], op0=ALU.mult, op1=ALU.add).then_inc(hb_ready, 1)
                k, pk = at(3)
                if inside(k):
                    wait(dve, stats, k)
                    dve.sem_inc(K["passed"], 1)
                    src = x[:, bass.ds(G * k, G), :]
                    for t in range(G):
                        last = dve.bn_stats(st6[:, t, :], src[:, t, :])
                    last.then_inc(lstep, 1)
                n, pn = at(0)
                if inside(n):
                    dve.wait_ge(h_ready, n + 1)
                    rounded(h[:, pn % 2], ha, hc, hr, hs, hi, hstep, HS * n,
                            lambda: wait(dve, hq_ready, n)).then_inc(hi_ready, 1)
                    wait(dve, o1_ready, n - 1)
                    scale_of(hd[:, pn % 2], hc, 1).then_inc(hstep, 1)
                if inside(k):
                    dve.wait_ge(lstep, k + 1)
                    wait(dve, xstep, XS * k)
                    dve.sem_inc(K["passed"], 1)
                    for t in range(G):
                        last = dve.bn_aggr(mv[:, t, :], st6[:, t, :])
                    last.then_inc(stats, 1)
                l, pl = at(-1)
                if inside(l):
                    dve.wait_ge(o_done, l + 1)
                    dve.wait_ge(hstep, HS * l + HS)
                    wait(dve, added, l - 1)
                    for t in range(G):
                        last = dve.scalar_tensor_tensor(out=o1[:, pl % 2, t], in0=psum_o[:, t, :],
                                                        scalar=hd[:, pl % 2, t:t + 1], in1=b2b[:],
                                                        op0=ALU.mult, op1=ALU.add)
                    last.then_inc(o1_ready, 1)
                if inside(k):
                    dve.wait_ge(rstd_ready, k + 1)
                    wait(dve, xi_ready, k)
                    for t in range(G):
                        last = dve.tensor_scalar(xn[:, t, :], src[:, t, :], mv[:, t, 0:1], rstd[:, t:t + 1],
                                                 ALU.subtract, ALU.mult)
                    last.then_inc(xstep, 1)
                    dve.wait_ge(xstep, XS * k + 1)
                    rounded(xn[:], xa, xc, xr, xs, xi, xstep, XS * k + 1,
                            lambda: wait(dve, xq_ready, k)).then_inc(xi_ready, 1)
                    wait(dve, hb_ready, G * (k - 3))
                    scale_of(xd[:, pk, :], xc, 0).then_inc(xstep, 1)

            run(dve, emit)
            dve.wait_ge(added, N)

        @block.gpsimd
        def _(pool):
            def emit(at):
                k, pk = at(3)
                if inside(k):
                    pool.wait_ge(stats, k + 1)
                    pool.sem_inc(K["passed"], 1)
                    pool.tensor_scalar(veps[:], mv[:, :, 1], EPS, None, ALU.add).then_inc(pstep, 1)
                    pool.wait_ge(pstep, k + 1)
                    pool.tensor_tensor(rstd[:], veps[:], K["half"][:, 0:G], ALU.pow).then_inc(rstd_ready, 1)
                l, pl = at(-1)
                if inside(l):
                    pool.wait_ge(o1_ready, l + 1)
                    pool.sem_inc(K["passed"], 1)
                    dst = x[:, bass.ds(G * l, G), :]
                    pool.tensor_tensor(dst, o1[:, pl % 2], dst, ALU.add).then_inc(added, 1)

            run(pool, emit)

        @block.tensor
        def _(pe):
            pe.wait_ge(wstep, 3)
            pe.matmul(psum_w[:], ones[:], wa[:], start=True, stop=True).then_inc(wsummed, 1)
            pe.wait_ge(w_ready, 1)

            def emit(at):
                m, pm = at(1)
                if inside(m):
                    pe.wait_ge(xq_t_ready, m + 1)
                    for t in range(G):
                        wait(pe, hb_ready, G * (m - 1) + t + 1)
                        pe.matmul(psum_h[t][:], xq_t[:, pm % 2, t], wt[0][:], start=True, stop=True)\
                          .then_inc(h_done, 1)
                l, pl = at(-1)
                if inside(l):
                    pe.wait_ge(hq_t_ready, l + 1)
                    wait(pe, o1_ready, l)
                    for t in range(G):
                        for f in range(FB):
                            last = pe.matmul(psum_o[:, t, :], hq_t[:, pl % 2, t, f, :], wt[1][:, f * P:(f + 1) * P],
                                             start=f == 0, stop=f == FB - 1)
                    last.then_inc(o_done, 1)
                n, pn = at(2)
                if inside(n):
                    pe.wait_ge(xq_ready, n + 1)
                    wait(pe, xq_t_ready, n)
                    for t in range(G):
                        last = pe.transpose(psum_x[:, t, :], xq[:, pn % 2, t, :], K["ident_bf"][:])
                    last.then_inc(x_turned, 1)
                n, pn = at(0)
                if inside(n):
                    pe.wait_ge(hq_ready, n + 1)
                    wait(pe, hq_t_ready, n)
                    for t in range(G):
                        for f in range(FB):
                            last = pe.transpose(psum_t[:, t, f, :], hq[:, t, f * P:(f + 1) * P], K["ident_bf"][:])
                    last.then_inc(h_turned, 1)

            run(pe, emit)

        @block.scalar
        def _(act):
            def emit(at):
                m, pm = at(1)
                if inside(m):
                    act.wait_ge(hb_ready, G * m + G)
                    wait(act, hi_ready, m - 1)
                    act.activation(h[:, pm % 2], hb[:], ACT.Gelu).then_inc(h_ready, 1)
                n, pn = at(2)
                if inside(n):
                    act.wait_ge(x_turned, n + 1)
                    wait(act, h_done, G * (n - 1))
                    act.activation(xq_t[:, pn % 2], psum_x[:], ACT.Identity).then_inc(xq_t_ready, 1)
                n, pn = at(0)
                if inside(n):
                    act.wait_ge(hi_ready, n + 1)
                    wait(act, h_turned, n)
                    act.activation(hq[:], hi[:], ACT.Identity, bias=unround[:]).then_inc(hq_ready, 1)
                    act.wait_ge(h_turned, n + 1)
                    wait(act, o_done, n - 1)
                    act.activation(hq_t[:, pn % 2], psum_t[:], ACT.Identity).then_inc(hq_t_ready, 1)
                k, pk = at(3)
                if inside(k):
                    act.wait_ge(xi_ready, k + 1)
                    wait(act, x_turned, k - 1)
                    act.activation(xq[:, pk % 2], xi[:], ACT.Identity, bias=unround[:]).then_inc(xq_ready, 1)

            run(act, emit)


@phase
def norm_context(nc, name, K, tokens, gain, bias, out):
    CTILES = NB * CK // P
    with ExitStack() as ctx:
        def sb(nm, shape, dt=F32):
            return ctx.enter_context(nc.sbuf_tensor(f"{name}_{nm}", shape, dt))

        def sem(nm):
            return nc.alloc_semaphore(f"{name}_{nm}")

        c = sb("c", [P, CTILES, CK])
        cn = sb("cn", [P, CTILES, CK])
        st6, mv, veps, rstd = sb("st6", [P, CTILES, 6]), sb("mv", [P, CTILES, 2]), sb("veps", [P, CTILES]), sb("rstd", [P, CTILES])
        g, b = sb("g", [CK, 1]), sb("b", [CK, 1])
        banks = [ctx.enter_context(nc.psum_tensor(f"{name}_t{i}", [CK, 4 * P], F32)) for i in range(2)]
        loaded, stepped, stats, rstd_ready = sem("loaded"), sem("stepped"), sem("stats"), sem("rstd_ready")
        pstep, cn_ready, turned, copied = sem("pstep"), sem("cn_ready"), sem("turned"), sem("copied")
        block = ctx.enter_context(nc.Block())

        @block.sync
        def _(sp):
            sp.dma_start(c[:], tokens).then_inc(loaded, 16)
            sp.dma_start(g[:], column(gain)).then_inc(loaded, 16)
            sp.dma_start(b[:], column(bias)).then_inc(loaded, 16)

        @block.vector
        def _(dve):
            dve.memset(out[CK:P, :], 0.0)
            dve.wait_ge(loaded, 48)
            for t in range(CTILES):
                last = dve.bn_stats(st6[:, t, :], c[:, t, :])
            last.then_inc(stepped, 1)
            dve.wait_ge(stepped, 1)
            for t in range(CTILES):
                last = dve.bn_aggr(mv[:, t, :], st6[:, t, :])
            last.then_inc(stats, 1)
            dve.wait_ge(rstd_ready, 1)
            for t in range(CTILES):
                last = dve.tensor_scalar(cn[:, t, :], c[:, t, :], mv[:, t, 0:1], rstd[:, t:t + 1],
                                         ALU.subtract, ALU.mult)
            last.then_inc(cn_ready, 1)

        @block.gpsimd
        def _(pool):
            pool.wait_ge(stats, 1)
            pool.tensor_scalar(veps[:], mv[:, :, 1], EPS, None, ALU.add).then_inc(pstep, 1)
            pool.wait_ge(pstep, 1)
            pool.tensor_tensor(rstd[:], veps[:], K["half"][:, 0:CTILES], ALU.pow).then_inc(rstd_ready, 1)

        @block.tensor
        def _(pe):
            pe.wait_ge(cn_ready, 1)
            for t in range(CTILES):
                pe.transpose(banks[t // 4][:, (t % 4) * P:(t % 4 + 1) * P], cn[:, t, :], K["ident"][:])\
                  .then_inc(turned, 1)

        @block.scalar
        def _(act):
            act.wait_ge(loaded, 48)
            for i in range(2):
                act.wait_ge(turned, 4 * (i + 1))
                act.activation(out[0:CK, i * 4 * P:(i + 1) * 4 * P], banks[i][:], ACT.Identity, scale=g[:], bias=b[:])\
                   .then_inc(copied, 1)


@phase
def load_tokens(nc, a, x, ctx_t):
    in_loaded, in_zeroed = nc.alloc_semaphore("in_loaded"), nc.alloc_semaphore("in_zeroed")
    with nc.Block() as block:
        @block.sync
        def _(sp):
            sp.dma_start(x[:], a["x"].rearrange("b (t p) d -> p (b t) d", p=P)).then_inc(in_loaded, 16)
            sp.dma_start(ctx_t[0:CK, :], a["ctx_t"]).then_inc(in_loaded, 16)
            sp.wait_ge(in_loaded, 32)

        @block.vector
        def _(dve):
            dve.memset(ctx_t[CK:P, :], 0.0).then_inc(in_zeroed, 1)
            dve.wait_ge(in_zeroed, 1)


@phase
def store_tokens(nc, x, out):
    out_stored = nc.alloc_semaphore("out_stored")
    with nc.Block() as block:
        @block.sync
        def _(sp):
            sp.dma_start(out.rearrange("b (t p) d -> p (b t) d", p=P), x[:]).then_inc(out_stored, 16)
            sp.wait_ge(out_stored, 16)


def heads(a, name, rows=P):
    return {"wq": a[f"{name}_wq"], "wk": a[f"{name}_wk"], "wv": a[f"{name}_wv"], "wo": a.get(f"{name}_wo"), "k_rows": rows}


def network(nc, a, out):
    with ExitStack() as stack:
        K = constants(nc, stack)
        x = stack.enter_context(nc.sbuf_tensor("tokens_x", [P, NT, D], F32))
        ctx_t = stack.enter_context(nc.sbuf_tensor("context_t", [P, NB * CK], F32))
        weights_by_expert = nc.dram_tensor("weights_by_expert", (NE, NTOK), F32, kind="Internal").ap()

        def scratch(ctx, name, shape, dt=F32):
            return ctx.enter_context(nc.sbuf_tensor(name, shape, dt))

        def parts(ctx, name):
            return (scratch(ctx, f"{name}_x_hi", [P, NTOK], F32R), scratch(ctx, f"{name}_x_lo", [P, NTOK], F32R),
                    scratch(ctx, f"{name}_acc", [P, NTOK]))

        def mixture(name, rule, kind):
            with ExitStack() as ctx:
                x_hi, x_lo, acc = parts(ctx, name)
                with ExitStack() as inner:
                    w = scratch(inner, f"{name}_route", [P, NT, NE])
                    w_t = scratch(inner, f"{name}_route_t", [NE, NTOK])
                    prepare(nc, f"{name}_prep", K, x, x_hi, x_lo,
                            gate=dict(w=a[f"{name}_gate_w"], b=a[f"{name}_gate_b"], rule=rule, weights=w, we_t=w_t,
                                      dram=weights_by_expert, bias=a[f"{name}_b_out"], acc=acc, by_token=False))
                experts(nc, f"{name}_experts", K, x_hi, x_lo, acc, kind=kind, weights=a[f"{name}_w"],
                        biases=a[f"{name}_b"], we_dram=weights_by_expert)
                add_turned(nc, f"{name}_add", K, acc, x, x)

        def mlp(name, src, base, dst, more):
            with ExitStack() as ctx:
                x_hi, x_lo, acc = parts(ctx, name)
                prepare(nc, f"{name}_prep", K, src, x_hi, x_lo, affine=(a[f"{name}_ln3_g"], a[f"{name}_ln3_b"]))
                experts(nc, f"{name}_mlp", K, x_hi, x_lo, acc, kind="gelu", weights=a[f"{name}_w"],
                        biases=a[f"{name}_b"], last_bias=a[f"{name}_b_out"])
                add_turned(nc, f"{name}_add", K, acc, base, dst, more=more)

        make_constants(nc, K)
        load_tokens(nc, a, x, ctx_t)

        attention(nc, "l0", K, heads(a, "l0", CK), dh=8, units=1, x=x, out=x, ctx_t=ctx_t,
                  biases=(a["l0_bq"], a["l0_bk"], a["l0_bv"]), out_bias=a["l0_bo"])
        mixture("l0f", "topk", "glu")

        with ExitStack() as ctx:
            y_t = scratch(ctx, "l1_y_t", [P, NTOK])
            attention(nc, "l1s", K, dict(heads(a, "l1s"), wo=a["l1c_wo"]), dh=8, units=4, x=x, out=None,
                      causal="before", store_t=y_t, biases=(a["l1s_bq"], a["l1s_bk"], a["l1s_bv"]))
            attention(nc, "l1c", K, heads(a, "l1c", CK), dh=8, units=1, x=x, out=x, ctx_t=ctx_t, add_t=y_t,
                      biases=(a["l1c_bq"], a["l1c_bk"], a["l1c_bv"]), out_bias=a["l1c_bo"])
        with ExitStack() as ctx:
            x_hi, x_lo, acc = parts(ctx, "l1f")
            kept = scratch(ctx, "l1f_tokens", [P, NT, D])
            w = scratch(ctx, "l1f_route", [P, NT, NE])
            with nc.sbuf_tensor("l1f_route_t", [NE, NTOK], F32) as w_t:
                prepare(nc, "l1f_prep", K, x, x_hi, x_lo, tokens=kept,
                        gate=dict(w=a["l1f_gate_w"], b=None, rule="topk", weights=w, we_t=w_t, dram=None,
                                  bias=a["l1f_ln_b"], acc=acc, by_token=True))
            experts_normed(nc, "l1f_experts", K, x_hi, x_lo, kept, w, acc[:].rearrange("p (t d) -> p t d", d=D), x,
                           weights=a["l1f_w"], biases=a["l1f_b"], out_biases=a["l1f_b_out"], gains=a["l1f_ln_g"],
                           eps=1e-6)

        with ExitStack() as ctx:
            base = scratch(ctx, "l2_base", [P, NT, D])
            att = scratch(ctx, "l2_att", [P, NT, D])
            attention(nc, "a1", K, heads(a, "a1"), dh=32, units=4, x=x, out=att, causal="after", residual=base,
                      norms=(None, (a["ln1_g"], a["ln1_b"])), affine_q=(a["a1_lnx_g"], a["a1_lnx_b"]),
                      affine_kv=(a["a1_lny_g"], a["a1_lny_b"]), out_bias=a["a1_bo"])
            mlp("a1", att, base, base, (att,))
            with ExitStack() as inner:
                ctx_n = scratch(inner, "context_n", [P, NB * CK])
                norm_context(nc, "ctxn", K, a["ctx"].rearrange("b (h t) d -> (b t) h d", h=1)
                             .rearrange("(n p) h d -> p n (h d)", p=P), a["a2_lny_g"], a["a2_lny_b"], ctx_n)
                attention(nc, "a2", K, heads(a, "a2", CK), dh=32, units=1, x=base, out=att, residual=base,
                          norms=((a["ln2_g"], a["ln2_b"]),), affine_q=(a["a2_lnx_g"], a["a2_lnx_b"]), ctx_t=ctx_n,
                          out_bias=a["a2_bo"])
            mlp("a2", att, base, x, (att, x))
        mixture("l2f", "threshold", "gelu")

        attention(nc, "l3", K, heads(a, "l3", CK), dh=8, units=1, x=x, out=x, ctx_t=ctx_t)
        ternary_mlp(nc, "l3f", K, x, w1=a["l3f_w1"], w2=a["l3f_w2"], b1=a["l3f_b1"], b2=a["l3f_b2"])
        store_tokens(nc, x, out)



def lay_out(v):
    import numpy as np

    def blocks(w, rows, cols):
        return [w[:, r * P:(r + 1) * P, c * P:(c + 1) * P] for r, c in zip(rows, cols)]

    def columns(*biases):
        cols = [b.reshape(b.shape[0], -1, P).transpose(2, 0, 1) for b in biases]
        return np.concatenate(cols, -1).reshape(P, -1)

    def chunks(w):
        return w.reshape(-1, P, w.shape[1]).transpose(1, 0, 2)

    def by_head(w):
        return w.transpose(1, 0, 2).reshape(w.shape[1], -1)

    a = {"x": v["x"], "ctx": v["ctx_512"], "ctx_t": v["ctx_512"].reshape(NB * CK, CK).T}
    for name, new in (("L0_xattn", "l0"), ("L1_xattn", "l1s")):
        for part in "qkv":
            a[f"{new}_w{part}"], a[f"{new}_b{part}"] = v[f"{name}_W{part}"], v[f"{name}_b{part}"]
    a["l0_wo"], a["l0_bo"] = chunks(v["L0_xattn_Wo"]), v["L0_xattn_bo"]
    for part in "qkv":
        a[f"l1c_w{part}"], a[f"l1c_b{part}"] = v[f"L1_xattn_Wc{part}"], v[f"L1_xattn_bc{part}"]
    a["l1c_wo"], a["l1c_bo"] = chunks(v["L1_xattn_Wp"]), v["L1_xattn_bp"]

    w1, w2, wg, w3 = (v[f"L0_ffn_{n}"] for n in ("w1", "w2", "wg", "w3"))
    a["l0f_w"] = np.concatenate(blocks(w1, [0], [0]) + blocks(w2, [0], [0]) + blocks(w1, [0], [1]) + blocks(w2, [0], [1])
                                + blocks(wg, [0, 0, 1, 1], [0, 1, 0, 1]) + blocks(w3, [0, 1], [0, 0]), -1)
    a["l0f_b"] = columns(v["L0_ffn_b1"], v["L0_ffn_b2"], v["L0_ffn_bg"])
    a["l0f_b_out"], a["l0f_gate_w"], a["l0f_gate_b"] = v["L0_ffn_b3"], v["L0_ffn_gate_w"], v["L0_ffn_gate_b"]

    w1, w2 = v["L1_ffn_w1"], v["L1_ffn_w2"]
    a["l1f_w"] = np.concatenate(blocks(w1, [0, 0], [0, 1]) + blocks(w2, [0, 1], [0, 0]), -1)
    a["l1f_b"] = columns(v["L1_ffn_b1"])
    a["l1f_b_out"], a["l1f_ln_g"] = v["L1_ffn_b2"].reshape(-1), v["L1_ffn_ln_g"].reshape(-1)
    a["l1f_ln_b"], a["l1f_gate_w"] = v["L1_ffn_ln_b"], v["L1_ffn_gate_w"]

    for i in (1, 2):
        n = f"L2_xattn_a{i}_"
        a[f"ln{i}_g"], a[f"ln{i}_b"] = v[f"L2_xattn_ln{i}_g"], v[f"L2_xattn_ln{i}_b"]
        for part in "qkv":
            a[f"a{i}_w{part}"] = by_head(v[f"{n}w{part}"])
        a[f"a{i}_wo"], a[f"a{i}_bo"] = chunks(v[f"{n}li1_w"]), v[f"{n}li1_b"]
        for part in ("lnx_g", "lnx_b", "lny_g", "lny_b", "ln3_g", "ln3_b"):
            a[f"a{i}_{part}"] = v[f"{n}{part}"]
        a[f"a{i}_w"] = np.concatenate(blocks(v[f"{n}li2_w"][None], [0] * 4, range(4))
                                      + blocks(v[f"{n}li3_w"][None], range(4), [0] * 4), -1)
        a[f"a{i}_b"], a[f"a{i}_b_out"] = columns(v[f"{n}li2_b"][None]), v[f"{n}li3_b"]

    a["l2f_w"] = np.concatenate(blocks(v["L2_ffn_W1"], [0] * 4, range(4))
                                + blocks(v["L2_ffn_W2"], range(4), [0] * 4), -1)
    a["l2f_b"], a["l2f_b_out"] = columns(v["L2_ffn_b1"]), v["L2_ffn_b2"]
    a["l2f_gate_w"], a["l2f_gate_b"] = v["L2_ffn_Wr"], v["L2_ffn_br"]

    a["l3_wq"], a["l3_wo"] = v["L3_xattn_Wq"].T, chunks(v["L3_xattn_Wo"].T)
    a["l3_wk"], a["l3_wv"] = v["L3_xattn_Wkv"][:D].T, v["L3_xattn_Wkv"][D:].T
    a["l3f_w1"] = v["L3_ffn_W1"].T
    a["l3f_w2"] = chunks(v["L3_ffn_W2"].T).reshape(P, -1)
    a["l3f_b1"], a["l3f_b2"] = v["L3_ffn_b1"], v["L3_ffn_b2"]
    return {f"in_{name}": np.ascontiguousarray(w) for name, w in a.items()}


def kernel(**inputs):
    import numpy as _np
    import concourse.bacc as _bacc
    from concourse import mybir as _mybir
    from concourse.bass_utils import run_bass_kernel_spmd as _run

    nc = _bacc.Bacc("TRN2", target_bir_lowering=False, num_devices=1)
    arrays = lay_out({name: _np.asarray(value) for name, value in inputs.items()})
    aps = {name[3:]: nc.dram_tensor(name, w.shape, _mybir.dt.from_np(w.dtype), kind="ExternalInput").ap()
           for name, w in arrays.items()}
    out = nc.dram_tensor("out_0_dram", (NB, T, D), _mybir.dt.float32, kind="ExternalOutput").ap()
    network(nc, aps, out)
    r = _run(nc, [arrays], core_ids=[0])
    return r.results[0]["out_0_dram"]
```
